# Optimizing a Trainium2 kernel written in Bass

```python
import numpy as np
import jax
import jax.numpy as jnp

def _softmax(x, axis=-1):
    return jax.nn.softmax(x, axis=axis)

def _gelu(x):
    return jax.nn.gelu(x, approximate=True)

def _silu(x):
    return jax.nn.silu(x)

def _sigmoid(x):
    return jax.nn.sigmoid(x)

def _layernorm(x, axis=-1, eps=1e-05):
    m = jnp.mean(x, axis=axis, keepdims=True)
    v = jnp.var(x, axis=axis, keepdims=True)
    return (x - m) / jnp.sqrt(v + eps)

def _scatter_add(tgt, idx, src, axis=0):
    return tgt.at[idx].add(src)

def _segment_sum(src, seg, n):
    return jax.ops.segment_sum(src, seg, n)
kernel_name = 'mk_decoder_preln_d1_seqx_r8_5fa8a1'

def setup_inputs(seed: int=0):
    np.random.seed(seed)
    _w = jnp.asarray

    def _rec_inputs():
        import jax
        import jax.numpy as jnp
        _rk = jax.random.key(seed)
        x = -0.0002928 + 1 * jax.random.normal(jax.random.fold_in(_rk, 1), (4, 512, 128), jnp.float32)
        _lenS = 512 - jax.random.randint(jax.random.fold_in(_rk, 7), (4,), 0, max(1, 512 // 4) + 1, jnp.int32)
        _lenS2 = 32 - jax.random.randint(jax.random.fold_in(_rk, 8), (4,), 0, max(1, 32 // 4) + 1, jnp.int32)
        _ctx_512P = jax.random.normal(jax.random.fold_in(_rk, 11), (4, 16, 64), jnp.float32)
        _ctx_512c = jax.random.dirichlet(jax.random.fold_in(_rk, 511), 0.3 * jnp.ones((16,), jnp.float32), (4, 32))
        _ctx_512t = jnp.einsum('bsk,bkd->bsd', _ctx_512c, _ctx_512P)
        _ctx_512t = _ctx_512t * jax.lax.rsqrt(jnp.mean(jnp.square(_ctx_512t)) + 1e-12) * 0.953939
        ctx_512 = -0.000514642 + 1.00011 * (_ctx_512t + 0.3 * jax.random.normal(jax.random.fold_in(_rk, 611), (4, 32, 64), jnp.float32))
        return (x, ctx_512)
    x, ctx_512 = _rec_inputs()

    def _L0_attn_setup():
        import jax, jax.numpy as jnp
        import numpy as np
        D_MODEL = 128
        NUM_HEADS = 16
        D_K = D_MODEL // NUM_HEADS
        ROPE_BASE = 10000.0

        def _rope_cos_sin(seq_len, d_k):
            inv_freq = 1.0 / ROPE_BASE ** (jnp.arange(0, d_k, 2, dtype=jnp.float32) / d_k)
            t = jnp.arange(seq_len, dtype=jnp.float32)
            freqs = t[:, None] * inv_freq[None, :]
            emb = jnp.concatenate([freqs, freqs], axis=-1)
            return (jnp.cos(emb)[None, None], jnp.sin(emb)[None, None])

        def _apply_rope(q, k, cos, sin):
            q1, q2 = (q[..., ::2], q[..., 1::2])
            k1, k2 = (k[..., ::2], k[..., 1::2])
            q_rot = jnp.concatenate([-q2, q1], axis=-1)
            k_rot = jnp.concatenate([-k2, k1], axis=-1)
            return (q * cos + q_rot * sin, k * cos + k_rot * sin)
        key = jax.random.key(seed)
        ks = jax.random.split(key, 5)
        B, S = (2, 256)
        x = jax.random.normal(ks[0], (B, S, D_MODEL), dtype=jnp.float32)
        scale = 1.0 / np.sqrt(D_MODEL)
        Wq = jax.random.normal(ks[1], (D_MODEL, D_MODEL), dtype=jnp.float32) * scale
        Wk = jax.random.normal(ks[2], (D_MODEL, D_MODEL), dtype=jnp.float32) * scale
        Wv = jax.random.normal(ks[3], (D_MODEL, D_MODEL), dtype=jnp.float32) * scale
        Wo = jax.random.normal(ks[4], (D_MODEL, D_MODEL), dtype=jnp.float32) * scale
        return {'x': x, 'Wq': Wq, 'Wk': Wk, 'Wv': Wv, 'Wo': Wo}
    _L0_attn_all = _L0_attn_setup()
    _L0_attn_in = {k: v for k, v in _L0_attn_all.items() if k in ('Wq', 'Wk', 'Wv', 'Wo')}
    del _L0_attn_all

    def _L0_xattn_setup():
        import jax, jax.numpy as jnp
        import numpy as np
        DIM = 128
        LATENT_DIM = 64
        NUM_HEADS = 16
        HEAD_DIM = DIM // NUM_HEADS
        SCALE = HEAD_DIM ** (-0.5)
        key = jax.random.key(seed)
        k1, k2, k3, k4, k5 = jax.random.split(key, 5)
        B, xN, zN = (2, 256, 256)
        x = jax.random.normal(k1, (B, xN, DIM), dtype=jnp.float32)
        z = jax.random.normal(k2, (B, zN, LATENT_DIM), dtype=jnp.float32)
        Wq = jax.random.normal(k3, (DIM, DIM), dtype=jnp.float32) * DIM ** (-0.5)
        Wkv = jax.random.normal(k4, (2 * DIM, LATENT_DIM), dtype=jnp.float32) * LATENT_DIM ** (-0.5)
        Wo = jax.random.normal(k5, (DIM, DIM), dtype=jnp.float32) * DIM ** (-0.5)
        return {'x': x, 'z': z, 'Wq': Wq, 'Wkv': Wkv, 'Wo': Wo}
    _L0_xattn_all = _L0_xattn_setup()
    _L0_xattn_in = {k: v for k, v in _L0_xattn_all.items() if k in ('Wq', 'Wkv', 'Wo')}
    del _L0_xattn_all

    def _L0_ffn_setup():
        import jax, jax.numpy as jnp
        import numpy as np
        DIM = 128
        DEPTH = 6
        HEADS = 16
        DIM_HEAD = 64
        WINDOW = 32
        INNER = HEADS * DIM_HEAD
        DIM_INNER = int(DIM * 4 * 2 / 3)
        QK_SCALE = 8.0

        def shift_tokens(t):
            a, s = jnp.split(t, 2, -1)
            s = jnp.pad(s, ((0, 0), (1, 0), (0, 0)))[:, :-1]
            return jnp.concatenate([a, s], -1)

        def l2norm(t):
            return t / jnp.maximum(jnp.linalg.norm(t, axis=-1, keepdims=True), 1e-12)

        def rotate_half(x):
            x1, x2 = jnp.split(x, 2, -1)
            return jnp.concatenate([-x2, x1], -1)

        def rotary_tables(n):
            half = jnp.arange(0, DIM_HEAD, 2, dtype=jnp.float32)
            inv_freq = 1.0 / 10000.0 ** (half / DIM_HEAD)
            t = jnp.arange(n, dtype=jnp.float32)
            freqs = t[:, None] * inv_freq[None, :]
            freqs = jnp.concatenate([freqs, freqs], -1)
            base_scale = (half + 0.4 * DIM_HEAD) / (1.4 * DIM_HEAD)
            power = (t - n // 2) / (WINDOW // 2)
            scale = base_scale[None, :] ** power[:, None]
            scale = jnp.concatenate([scale, scale], -1)
            return (freqs, scale)

        def local_attention(q, k, v):
            b, h, n, d = q.shape
            w = WINDOW
            nw = n // w
            bq = q.reshape(b, h, nw, w, d)
            bk = k.reshape(b, h, nw, w, d)
            bv = v.reshape(b, h, nw, w, d)

            def look(t):
                p = jnp.pad(t, ((0, 0), (0, 0), (1, 0), (0, 0), (0, 0)))
                return jnp.concatenate([p[:, :, :nw], p[:, :, 1:]], axis=3)
            bk2, bv2 = (look(bk), look(bv))
            seq = jnp.arange(n).reshape(nw, w)
            seq_p = jnp.pad(seq, ((1, 0), (0, 0)), constant_values=-1)
            jt = jnp.concatenate([seq_p[:nw], seq_p[1:]], axis=1)
            it = seq[:, :, None]
            jb = jt[:, None, :]
            mask = (it < jb) | (it > jb + w) | (jb == -1)
            sim = jnp.einsum('bhwie,bhwje->bhwij', bq, bk2) * QK_SCALE
            sim = jnp.where(mask, -jnp.finfo(sim.dtype).max, sim)
            attn = jax.nn.softmax(sim, -1)
            out = jnp.einsum('bhwij,bhwje->bhwie', attn, bv2)
            return out.reshape(b, h, n, d)

        def attn_layer(x, Wqkv, qs, ksc, Wo):
            b, n, _ = x.shape
            qkv = x @ Wqkv
            q, k, v = jnp.split(qkv, 3, -1)
            sh = lambda t: t.reshape(b, n, HEADS, DIM_HEAD).transpose(0, 2, 1, 3)
            q, k, v = (sh(q), sh(k), sh(v))
            q = l2norm(q) * qs
            k = l2norm(k) * ksc
            freqs, scale = rotary_tables(n)
            cos, sin = (jnp.cos(freqs), jnp.sin(freqs))
            q = q * cos * scale + rotate_half(q) * sin * scale
            inv = 1.0 / scale
            k = k * cos * inv + rotate_half(k) * sin * inv
            out = local_attention(q, k, v)
            out = out.transpose(0, 2, 1, 3).reshape(b, n, INNER)
            return out @ Wo

        def ffn_layer(x, g, bln, W1, b1, W2, b2):
            mu = x.mean(-1, keepdims=True)
            var = ((x - mu) ** 2).mean(-1, keepdims=True)
            xn = (x - mu) / jnp.sqrt(var + 1e-05) * g + bln
            hg = xn @ W1 + b1
            a, gate = jnp.split(hg, 2, -1)
            return a * jax.nn.gelu(gate, approximate=False) @ W2 + b2
        key = jax.random.key(seed)
        ks = jax.random.split(key, 8)
        B, N = (2, 256)
        init = lambda k, shape: jax.random.normal(k, shape, jnp.float32) * 0.02
        return {'x': jax.random.normal(ks[0], (B, N, DIM), jnp.float32), 'Wqkv': init(ks[1], (DEPTH, DIM, 3 * INNER)), 'q_scale': jnp.ones((DEPTH, DIM_HEAD), jnp.float32), 'k_scale': jnp.ones((DEPTH, DIM_HEAD), jnp.float32), 'Wo': init(ks[2], (DEPTH, INNER, DIM)), 'ln_g': jnp.ones((DEPTH, DIM), jnp.float32), 'ln_b': jnp.zeros((DEPTH, DIM), jnp.float32), 'W1': init(ks[3], (DEPTH, DIM, 2 * DIM_INNER)), 'b1': jnp.zeros((DEPTH, 2 * DIM_INNER), jnp.float32), 'W2': init(ks[4], (DEPTH, DIM_INNER, DIM)), 'b2': jnp.zeros((DEPTH, DIM), jnp.float32)}
    _L0_ffn_all = _L0_ffn_setup()
    _L0_ffn_in = {k: v for k, v in _L0_ffn_all.items() if k in ('Wqkv', 'q_scale', 'k_scale', 'Wo', 'ln_g', 'ln_b', 'W1', 'b1', 'W2', 'b2')}
    del _L0_ffn_all
    return {'x': x, 'ctx_512': ctx_512, 'L0_attn_Wq': _L0_attn_in['Wq'], 'L0_attn_Wk': _L0_attn_in['Wk'], 'L0_attn_Wv': _L0_attn_in['Wv'], 'L0_attn_Wo': _L0_attn_in['Wo'], 'L0_xattn_Wq': _L0_xattn_in['Wq'], 'L0_xattn_Wkv': _L0_xattn_in['Wkv'], 'L0_xattn_Wo': _L0_xattn_in['Wo'], 'L0_ffn_Wqkv': _L0_ffn_in['Wqkv'], 'L0_ffn_q_scale': _L0_ffn_in['q_scale'], 'L0_ffn_k_scale': _L0_ffn_in['k_scale'], 'L0_ffn_Wo': _L0_ffn_in['Wo'], 'L0_ffn_ln_g': _L0_ffn_in['ln_g'], 'L0_ffn_ln_b': _L0_ffn_in['ln_b'], 'L0_ffn_W1': _L0_ffn_in['W1'], 'L0_ffn_b1': _L0_ffn_in['b1'], 'L0_ffn_W2': _L0_ffn_in['W2'], 'L0_ffn_b2': _L0_ffn_in['b2']}

def reference(x, ctx_512, L0_attn_Wq, L0_attn_Wk, L0_attn_Wv, L0_attn_Wo, L0_xattn_Wq, L0_xattn_Wkv, L0_xattn_Wo, L0_ffn_Wqkv, L0_ffn_q_scale, L0_ffn_k_scale, L0_ffn_Wo, L0_ffn_ln_g, L0_ffn_ln_b, L0_ffn_W1, L0_ffn_b1, L0_ffn_W2, L0_ffn_b2):
    import jax
    import jax.numpy as jnp

    def _L0_attn_ref(x, Wq, Wk, Wv, Wo):
        import jax, jax.numpy as jnp
        import numpy as np
        D_MODEL = 128
        NUM_HEADS = 16
        D_K = D_MODEL // NUM_HEADS
        ROPE_BASE = 10000.0

        def _rope_cos_sin(seq_len, d_k):
            inv_freq = 1.0 / ROPE_BASE ** (jnp.arange(0, d_k, 2, dtype=jnp.float32) / d_k)
            t = jnp.arange(seq_len, dtype=jnp.float32)
            freqs = t[:, None] * inv_freq[None, :]
            emb = jnp.concatenate([freqs, freqs], axis=-1)
            return (jnp.cos(emb)[None, None], jnp.sin(emb)[None, None])

        def _apply_rope(q, k, cos, sin):
            q1, q2 = (q[..., ::2], q[..., 1::2])
            k1, k2 = (k[..., ::2], k[..., 1::2])
            q_rot = jnp.concatenate([-q2, q1], axis=-1)
            k_rot = jnp.concatenate([-k2, k1], axis=-1)
            return (q * cos + q_rot * sin, k * cos + k_rot * sin)
        B, S, D = x.shape
        H, dk = (NUM_HEADS, D_K)

        def proj(W):
            return (x @ W.T).reshape(B, S, H, dk).transpose(0, 2, 1, 3)
        q, k, v = (proj(Wq), proj(Wk), proj(Wv))
        cos, sin = _rope_cos_sin(S, dk)
        q, k = _apply_rope(q, k, cos, sin)
        scores = jnp.einsum('bhqd,bhkd->bhqk', q, k) / jnp.sqrt(jnp.float32(dk))
        attn = jax.nn.softmax(scores, axis=-1)
        out = jnp.einsum('bhqk,bhkd->bhqd', attn, v)
        out = out.transpose(0, 2, 1, 3).reshape(B, S, D)
        return out @ Wo.T

    def _L0_xattn_ref(x, z, Wq, Wkv, Wo):
        import jax, jax.numpy as jnp
        import numpy as np
        DIM = 128
        LATENT_DIM = 64
        NUM_HEADS = 16
        HEAD_DIM = DIM // NUM_HEADS
        SCALE = HEAD_DIM ** (-0.5)
        B, xN, _ = x.shape
        _, zN, _ = z.shape
        Q = (x @ Wq.T).reshape(B, xN, NUM_HEADS, HEAD_DIM)
        KV = (z @ Wkv.T).reshape(B, zN, 2, NUM_HEADS, HEAD_DIM)
        K = KV[:, :, 0]
        V = KV[:, :, 1]
        attn = jnp.einsum('bqhd,bkhd->bhqk', Q, K) * SCALE
        attn = jax.nn.softmax(attn, axis=-1)
        O = jnp.einsum('bhqk,bkhd->bqhd', attn, V).reshape(B, xN, DIM)
        return O @ Wo.T

    def _L0_ffn_ref(x, Wqkv, q_scale, k_scale, Wo, ln_g, ln_b, W1, b1, W2, b2):
        import jax, jax.numpy as jnp
        import numpy as np
        DIM = 128
        DEPTH = 6
        HEADS = 16
        DIM_HEAD = 64
        WINDOW = 32
        INNER = HEADS * DIM_HEAD
        DIM_INNER = int(DIM * 4 * 2 / 3)
        QK_SCALE = 8.0

        def shift_tokens(t):
            a, s = jnp.split(t, 2, -1)
            s = jnp.pad(s, ((0, 0), (1, 0), (0, 0)))[:, :-1]
            return jnp.concatenate([a, s], -1)

        def l2norm(t):
            return t / jnp.maximum(jnp.linalg.norm(t, axis=-1, keepdims=True), 1e-12)

        def rotate_half(x):
            x1, x2 = jnp.split(x, 2, -1)
            return jnp.concatenate([-x2, x1], -1)

        def rotary_tables(n):
            half = jnp.arange(0, DIM_HEAD, 2, dtype=jnp.float32)
            inv_freq = 1.0 / 10000.0 ** (half / DIM_HEAD)
            t = jnp.arange(n, dtype=jnp.float32)
            freqs = t[:, None] * inv_freq[None, :]
            freqs = jnp.concatenate([freqs, freqs], -1)
            base_scale = (half + 0.4 * DIM_HEAD) / (1.4 * DIM_HEAD)
            power = (t - n // 2) / (WINDOW // 2)
            scale = base_scale[None, :] ** power[:, None]
            scale = jnp.concatenate([scale, scale], -1)
            return (freqs, scale)

        def local_attention(q, k, v):
            b, h, n, d = q.shape
            w = WINDOW
            nw = n // w
            bq = q.reshape(b, h, nw, w, d)
            bk = k.reshape(b, h, nw, w, d)
            bv = v.reshape(b, h, nw, w, d)

            def look(t):
                p = jnp.pad(t, ((0, 0), (0, 0), (1, 0), (0, 0), (0, 0)))
                return jnp.concatenate([p[:, :, :nw], p[:, :, 1:]], axis=3)
            bk2, bv2 = (look(bk), look(bv))
            seq = jnp.arange(n).reshape(nw, w)
            seq_p = jnp.pad(seq, ((1, 0), (0, 0)), constant_values=-1)
            jt = jnp.concatenate([seq_p[:nw], seq_p[1:]], axis=1)
            it = seq[:, :, None]
            jb = jt[:, None, :]
            mask = (it < jb) | (it > jb + w) | (jb == -1)
            sim = jnp.einsum('bhwie,bhwje->bhwij', bq, bk2) * QK_SCALE
            sim = jnp.where(mask, -jnp.finfo(sim.dtype).max, sim)
            attn = jax.nn.softmax(sim, -1)
            out = jnp.einsum('bhwij,bhwje->bhwie', attn, bv2)
            return out.reshape(b, h, n, d)

        def attn_layer(x, Wqkv, qs, ksc, Wo):
            b, n, _ = x.shape
            qkv = x @ Wqkv
            q, k, v = jnp.split(qkv, 3, -1)
            sh = lambda t: t.reshape(b, n, HEADS, DIM_HEAD).transpose(0, 2, 1, 3)
            q, k, v = (sh(q), sh(k), sh(v))
            q = l2norm(q) * qs
            k = l2norm(k) * ksc
            freqs, scale = rotary_tables(n)
            cos, sin = (jnp.cos(freqs), jnp.sin(freqs))
            q = q * cos * scale + rotate_half(q) * sin * scale
            inv = 1.0 / scale
            k = k * cos * inv + rotate_half(k) * sin * inv
            out = local_attention(q, k, v)
            out = out.transpose(0, 2, 1, 3).reshape(b, n, INNER)
            return out @ Wo

        def ffn_layer(x, g, bln, W1, b1, W2, b2):
            mu = x.mean(-1, keepdims=True)
            var = ((x - mu) ** 2).mean(-1, keepdims=True)
            xn = (x - mu) / jnp.sqrt(var + 1e-05) * g + bln
            hg = xn @ W1 + b1
            a, gate = jnp.split(hg, 2, -1)
            return a * jax.nn.gelu(gate, approximate=False) @ W2 + b2
        for i in range(DEPTH):
            x = attn_layer(shift_tokens(x), Wqkv[i], q_scale[i], k_scale[i], Wo[i]) + x
            x = ffn_layer(shift_tokens(x), ln_g[i], ln_b[i], W1[i], b1[i], W2[i], b2[i]) + x
        return x
    x = x + _L0_attn_ref(_layernorm(x, axis=-1), L0_attn_Wq, L0_attn_Wk, L0_attn_Wv, L0_attn_Wo)
    x = x + _L0_xattn_ref(_layernorm(x, axis=-1), ctx_512, L0_xattn_Wq, L0_xattn_Wkv, L0_xattn_Wo)
    x = x + _L0_ffn_ref(_layernorm(x, axis=-1), L0_ffn_Wqkv, L0_ffn_q_scale, L0_ffn_k_scale, L0_ffn_Wo, L0_ffn_ln_g, L0_ffn_ln_b, L0_ffn_W1, L0_ffn_b1, L0_ffn_W2, L0_ffn_b2)
    return x

_drawn_inputs = setup_inputs


def setup_inputs(seed=0):
    import zlib

    import numpy as np

    out = dict(_drawn_inputs(seed))
    spreads = {'L0_ffn_q_scale': (1.0, 0.6),
     'L0_ffn_k_scale': (1.0, 0.6),
     'L0_ffn_ln_g': (1.0, 0.6),
     'L0_ffn_ln_b': (0.0, 0.8),
     'L0_ffn_b1': (0.0, 0.8),
     'L0_ffn_b2': (0.0, 0.1)}
    factors = {'L0_ffn_W1': 3.94, 'L0_ffn_W2': 3.887}
    for name, (base, spread) in spreads.items():
        noise = np.random.default_rng([zlib.crc32(name.encode()), seed]).standard_normal(out[name].shape)
        drawn = base * np.exp(spread * noise) if base else spread * noise
        out[name] = jnp.asarray(drawn.astype(out[name].dtype))
    for name, factor in factors.items():
        out[name] = (out[name] * factor).astype(out[name].dtype)
    return out
```

```python
from contextlib import ExitStack

import concourse.bass as bass
from concourse import mybir
from concourse.alu_op_type import AluOpType as ALU

ACT = mybir.ActivationFunctionType
AX = mybir.AxisListType
F32 = mybir.dt.float32
BF16 = mybir.dt.bfloat16

P = 128
BATCH, SEQ, DIM = 4, 512, 128
TILES = SEQ // P
HEADS = 16
DK = DIM // HEADS
PAIRS = HEADS // 2
GROUPS = HEADS // 4
CTX, LATENT = 32, 64
LAYERS = 6
DH = 64
INNER = HEADS * DH
WINDOW = 32
PAD = WINDOW
HIDDEN = int(DIM * 4 * 2 / 3)
HC = [(0, 128), (128, 128), (256, HIDDEN - 256)]
EPS = 1e-5
QK_SCALE = 8.0
LN_EXP = "natural_log_exp_and_others"
BANK = 512

Q_PARTS = [(0, 3, 0, True), (3, 2, 1, True), (5, 1, 2, True)]
K_PARTS = [(0, 3, 0, False), (3, 2, 0, False), (5, 1, 0, False)]
MAX_ROW = 6 * DK

CONST = {}
_at = 0
for _name, _n in (("ident", P), ("mean", P), ("sums", P), ("cosT", SEQ), ("sinT", SEQ),
                  ("kmask", HEADS), ("vmask", GROUPS * HEADS), ("ropeC", 2 * TILES * DH),
                  ("ropeS", 2 * TILES * DH), ("wmask", 8 * 2 * WINDOW), ("wsel", 2 * P)):
    CONST[_name] = (_at, _n)
    _at += _n
N_CONST = _at
W_ATTN = {n: i * P for i, n in enumerate(("q", "k", "qr", "kr", "v", "o0", "o1", "o2", "o3"))}
V_B1, V_G, V_B, V_B2, N_VEC = 0, 6, 7, 8, 9


def decoder(nc, x, ctxT, w_attn, w_xq, w_xkv, w_xo, wqkv, qk_scales, wo, w1, w2, vecs, consts, scratch, max_scratch, out):
    with ExitStack() as top:
        def sb_in(stack):
            return lambda name, shape, dt=F32: stack.enter_context(nc.sbuf_tensor(name, shape, dt))

        def sem(name):
            return top.enter_context(nc.semaphore(name))

        sb = sb_in(top)
        ps = top.enter_context(nc.psum_tensor("ps", [P, 8, BANK], F32))
        cst = sb("cst", [P, N_CONST])
        xT = sb("xT", [P, BATCH, PAD + SEQ])
        xsT = sb("xsT", [P, BATCH, PAD + SEQ])
        x2T = sb("x2T", [P, BATCH, SEQ])

        def const(name):
            a, n = CONST[name]
            return cst[:, a:a + n]

        ident, mean_w = const("ident"), const("mean")
        eps_tile = sb("eps", [P, 1])
        eps = eps_tile[:, 0:1]
        env = dict(eps=eps, nc=nc, sem=sem, ps=ps, const=const, ident=ident, mean_w=mean_w, xT=xT, xsT=xsT, x2T=x2T,
                   sb_in=sb_in)
        self_attention(env, x, w_attn, consts, cst, scratch, max_scratch)
        cross_attention(env, ctxT, w_xq, w_xkv, w_xo)
        layers(env, wqkv, qk_scales, wo, w1, w2, vecs)
        finish(env, out)


def self_attention(env, x, w_attn, consts, cst, scratch, max_scratch):
    nc, sem, ps, const, ident, mean_w = (env[k] for k in ("nc", "sem", "ps", "const", "ident", "mean_w"))
    xT = env["xT"]
    with ExitStack() as st:
        sb = env["sb_in"](st)
        wat = sb("wat", [P, 9 * P])
        stack = sb("stack", [P, BATCH, 2, PAIRS, SEQ], BF16)
        vaug = sb("vaug", [P, BATCH, TILES, HEADS, 32])
        project_parts(env, sb, x, wat, w_attn, consts, cst, scratch, stack, vaug)
        outs = sb("outs", [P, BATCH, GROUPS, SEQ])
        softmax_values(env, st, stack, vaug, outs, max_scratch)
        attention_out(env, st, wat, outs)


def project_parts(env, sb_outer, x, wat, w_attn, consts, cst, scratch, stack, vaug):
    nc, sem, ps, const, ident, mean_w = (env[k] for k in ("nc", "sem", "ps", "const", "ident", "mean_w"))
    xT, eps = env["xT"], env["eps"]
    with ExitStack() as st:
        sb = env["sb_in"](st)
        xtok = sb("xtok", [P, BATCH * TILES, DIM])
        cen = sb("cen", [P, SEQ])
        sq = sb("sq", [P, SEQ])
        rstd = sb("rstd", [P, SEQ])
        xn = sb("xn", [P, SEQ])
        rc = sb("rc", [P, 2, SEQ])
        rs = sb("rs", [P, 2, SEQ])
        parts = sb("parts", [P, 2, 3, 2, SEQ], BF16)
        c_ld, w_ld = sem("a_consts_loaded"), sem("a_weights_loaded")
        x_ld = [sem(f"a_x_loaded{b}") for b in range(BATCH)]
        pads, eps_set, log_ready = sem("a_pads_zeroed"), sem("a_eps_set"), sem("a_log_ready")
        vz, vo, kz = sem("a_vaug_zeroed"), sem("a_ones_set"), sem("a_stack_zeroed")
        xt_ready, xt_copied = sem("a_xT_ready"), sem("a_xT_copied")
        mean_ready, centred, squared = sem("a_mean_ready"), sem("a_centred"), sem("a_squared")
        var_ready, rstd_ready, normed = sem("a_var_ready"), sem("a_rstd_ready"), sem("a_normed")
        projected, v_copied = sem("a_projected"), sem("a_v_copied")
        cosed, sined, rotated = sem("a_cosed"), sem("a_sined"), sem("a_rotated")
        hi_ready, rest_ready, mid_ready, lo_ready = (sem("a_" + n) for n in ("hi", "rest", "mid", "lo"))
        stored = [sem(f"a_stored{b}") for b in range(BATCH)]
        laid, ones_set = sem("a_laid_out"), sem("a_minus_ones_set")
        minus1 = sb("minus1", [2, PAIRS, SEQ], BF16)
        xv = x.rearrange("(t p) d -> p t d", p=P)

        with nc.Block() as block:
            @block.sync
            def _(sp):
                sp.dma_start(cst[:, 0:CONST["kmask"][0]], consts[:, 0:CONST["kmask"][0]]).then_inc(c_ld, 16)
                for b in range(BATCH):
                    sp.dma_start(xtok[:, b * TILES:(b + 1) * TILES, :],
                                 xv[:, b * TILES:(b + 1) * TILES, :]).then_inc(x_ld[b], 16)
                    if b == 0:
                        sp.dma_start(wat[:, :], w_attn).then_inc(w_ld, 16)
                sp.dma_start(cst[:, CONST["kmask"][0]:], consts[:, CONST["kmask"][0]:]).then_inc(c_ld, 16)
                sp.wait_ge(kz, 1)
                sp.wait_ge(ones_set, 1)
                n = 0
                for parity in range(2):
                    for b in range(BATCH):
                        a = 64 * parity + MAX_ROW
                        sp.dma_start(stack[a:a + 2, b, 1, :, :], minus1[:, :, :]).then_inc(laid, 16)
                        n += 16
                for b in range(BATCH):
                    sp.wait_ge(lo_ready, b + 1)
                    sp.dma_start(scratch[b], parts[:, b % 2]).then_inc(stored[b], 16)
                    sp.wait_ge(stored[b], 16)
                    for qk, table in enumerate((Q_PARTS, K_PARTS)):
                        for parity in range(2):
                            src = scratch[b].rearrange("(c a r) s k t -> a s r k c t", a=2, r=DK)[parity]
                            for row, copies, part, same in table:
                                for j in range(copies):
                                    a = parity * 64 + (row + j) * DK
                                    sp.dma_start(stack[a:a + DK, b, qk, :, :],
                                                 src[part if same else part + j, :, qk]).then_inc(laid, 16)
                                    n += 16
                sp.wait_ge(laid, n)
                sp.wait_ge(c_ld, 32)

            @block.gpsimd
            def _(pool):
                pool.memset(eps, EPS).then_inc(eps_set, 1)
                pool.memset(minus1[:, :, :], -1.0).then_inc(ones_set, 1)
                pool.memset(xT[:, :, 0:PAD], 0.0).then_inc(pads, 1)
                pool.memset(vaug[:, :, :, :, :], 0.0).then_inc(vz, 1)
                pool.wait_ge(vz, 1)
                pool.memset(vaug[:, :, :, :, DK:DK + 1], 1.0).then_inc(vo, 1)

            @block.tensor
            def _(pe):
                pe.wait_ge(c_ld, 16)
                for b in range(BATCH):
                    pe.wait_ge(x_ld[b], 16)
                    if b >= 1:
                        pe.wait_ge(xt_copied, b)
                    for i in range(TILES):
                        t = nc.tensor.transpose(ps[:, 0, i * P:(i + 1) * P], xtok[:, b * TILES + i, :], ident)
                    t.then_inc(xt_ready, 1)
                    pe.wait_ge(xt_copied, b + 1)
                    if b >= 1:
                        pe.wait_ge(centred, b)
                    nc.tensor.matmul(ps[:, 1, :], mean_w, xT[:, b, PAD:], start=True, stop=True).then_inc(mean_ready, 1)
                    pe.wait_ge(squared, b + 1)
                    if b >= 1:
                        pe.wait_ge(rstd_ready, b)
                    nc.tensor.matmul(ps[:, 2, :], mean_w, sq[:, :], start=True, stop=True).then_inc(var_ready, 1)
                    pe.wait_ge(normed, b + 1)
                    if b == 0:
                        pe.wait_ge(w_ld, 16)
                    if b >= 1:
                        pe.wait_ge(sined, b)
                        pe.wait_ge(v_copied, b)
                    for n, name in enumerate(("q", "k", "qr", "kr")):
                        w = W_ATTN[name]
                        nc.tensor.matmul(ps[:, 3 + n, :], wat[:, w:w + P], xn[:, :], start=True, stop=True)
                    for i in range(TILES):
                        m = nc.tensor.matmul(ps[:, 7, i * P:(i + 1) * P], xn[:, i * P:(i + 1) * P],
                                             wat[:, W_ATTN["v"]:W_ATTN["v"] + P], start=True, stop=True)
                    m.then_inc(projected, 1)

            @block.scalar
            def _(act):
                nc.scalar.preload_act_table_set(LN_EXP)
                for b in range(BATCH):
                    act.wait_ge(xt_ready, b + 1)
                    nc.scalar.activation(xT[:, b, PAD:], ps[:, 0, :], ACT.Copy).then_inc(xt_copied, 1)
                    act.wait_ge(centred, b + 1)
                    nc.scalar.activation(sq[:, :], cen[:, :], ACT.Square).then_inc(squared, 1)
                    act.wait_ge(var_ready, b + 1)
                    if b == 0:
                        act.wait_ge(eps_set, 1)
                    nc.scalar.activation(rstd[:, :], ps[:, 2, :], ACT.Ln, bias=eps).then_inc(log_ready, 1)
                    act.wait_ge(log_ready, b + 1)
                    nc.scalar.activation(rstd[:, :], rstd[:, :], ACT.Exp, scale=-0.5).then_inc(rstd_ready, 1)
                    act.wait_ge(projected, b + 1)
                    if b == 0:
                        act.wait_ge(vo, 1)
                    nc.scalar.activation(vaug[:, b, :, :, 0:DK],
                                         ps[:, 7, :].rearrange("p (i h d) -> p i h d", i=TILES, h=HEADS),
                                         ACT.Copy).then_inc(v_copied, 1)
                    if b >= 2:
                        act.wait_ge(stored[b - 2], 16)
                    act.wait_ge(rotated, b + 1)
                    nc.scalar.activation(parts[:, b % 2, 0], rc[:, :, :], ACT.Copy).then_inc(hi_ready, 1)
                    act.wait_ge(rest_ready, b + 1)
                    nc.scalar.activation(parts[:, b % 2, 1], rs[:, :, :], ACT.Copy).then_inc(mid_ready, 1)

            @block.vector
            def _(dve):
                nc.vector.memset(stack[:, :, :, :, :], 0.0).then_inc(kz, 1)
                cos2 = const("cosT")[:, None, :].broadcast_to([P, 2, SEQ])
                sin2 = const("sinT")[:, None, :].broadcast_to([P, 2, SEQ])
                for b in range(BATCH):
                    dve.wait_ge(mean_ready, b + 1)
                    if b >= 1:
                        dve.wait_ge(normed, b)
                    nc.vector.tensor_tensor(cen[:, :], xT[:, b, PAD:], ps[:, 1, :], ALU.subtract).then_inc(centred, 1)
                    dve.wait_ge(rstd_ready, b + 1)
                    if b >= 1:
                        dve.wait_ge(projected, b)
                    nc.vector.tensor_tensor(xn[:, :], cen[:, :], rstd[:, :], ALU.mult).then_inc(normed, 1)
                    dve.wait_ge(projected, b + 1)
                    if b >= 1:
                        dve.wait_ge(lo_ready, b)
                    nc.vector.tensor_tensor(rc[:, :, :], ps[:, 3:5, :], cos2, ALU.mult).then_inc(cosed, 1)
                    nc.vector.tensor_tensor(rs[:, :, :], ps[:, 5:7, :], sin2, ALU.mult).then_inc(sined, 1)
                    dve.wait_ge(sined, b + 1)
                    dve.wait_ge(cosed, b + 1)
                    nc.vector.tensor_tensor(rc[:, :, :], rc[:, :, :], rs[:, :, :], ALU.add).then_inc(rotated, 1)
                    dve.wait_ge(hi_ready, b + 1)
                    nc.vector.tensor_tensor(rs[:, :, :], rc[:, :, :], parts[:, b % 2, 0], ALU.subtract)\
                        .then_inc(rest_ready, 1)
                    dve.wait_ge(mid_ready, b + 1)
                    nc.vector.tensor_tensor(parts[:, b % 2, 2], rs[:, :, :], parts[:, b % 2, 1], ALU.subtract)\
                        .then_inc(lo_ready, 1)


def softmax_values(env, outer, stack, vaug, outs, max_scratch):
    nc, sem, ps, const, ident = (env[k] for k in ("nc", "sem", "ps", "const", "ident"))
    with ExitStack() as st:
        sb = env["sb_in"](st)
        MT = TILES * HEADS
        mx = sb("mx", [P, BATCH, MT])
        mparts = sb("mparts", [P, 2, MT], BF16)
        mrows = sb("mrows", [P, P], BF16)
        identb = sb("identb", [P, P], BF16)
        RING = 8
        probs = sb("probs", [P, RING, SEQ])
        id_ready = sem("b_ident_ready")
        m_ready, m_read = sem("b_max_scores_ready"), sem("b_max_scores_read")
        mhi, mlo, mt_ready = (sem("b_" + n) for n in ("max_hi", "max_lo", "max_turned"))
        laid = [sem(f"b_max_laid{b}") for b in range(BATCH)]
        m_stored = [sem(f"b_max_stored{b}") for b in range(BATCH)]
        s_ready, e_ready = sem("b_scores_ready"), sem("b_exp_ready")
        pv_group, o_read = sem("b_probs_used"), sem("b_out_read")
        SLOTS = 3
        units = [(g, kt, j) for g in range(GROUPS) for kt in range(TILES) for j in range(4)]
        NU = len(units)
        NM = HEADS * TILES
        per_batch = NM // 2 + 1

        def rows(h):
            return slice(64 * (h % 2), 64 * (h % 2) + 64)

        with nc.Block() as block:
            @block.sync
            def _(sp):
                for b in range(BATCH):
                    sp.wait_ge(m_read, (b + 1) * per_batch)
                    sp.dma_start(max_scratch[b], mrows[:, :]).then_inc(m_stored[b], 16)
                    sp.wait_ge(m_stored[b], 16)
                    for part in range(2):
                        for parity in range(2):
                            a = part * MT + parity * (MT // 2)
                            r = 64 * parity + MAX_ROW + part
                            sp.dma_start(stack[r:r + 1, b, 0, :, :].rearrange("o c (i q) -> o (c i) q", q=P),
                                         max_scratch[b, a:a + MT // 2, :].rearrange("(o n) q -> o n q", o=1))\
                                .then_inc(laid[b], 16)

            @block.tensor
            def _(pe):
                pe.wait_ge(id_ready, 1)

                def max_scores(b, n):
                    c, parity, i = n // (2 * TILES), n // TILES % 2, n % TILES
                    slot = b * per_batch + n // 2
                    if n % 2 == 0 and slot >= 2:
                        pe.wait_ge(m_read, slot - 1)
                    h = 2 * c + parity
                    m = nc.tensor.matmul(ps[:, 2 * (slot % 2) + n % 2, :], stack[rows(h), b, 0, c, i * P:(i + 1) * P],
                                         stack[rows(h), b, 1, c, :], start=True, stop=True)
                    if n % 2:
                        m.then_inc(m_ready, 1)

                def turn_max(b):
                    slot = b * per_batch + NM // 2
                    pe.wait_ge(m_read, slot - 1)
                    pe.wait_ge(mlo, b + 1)
                    nc.tensor.transpose(ps[:, 2 * (slot % 2), 0:P // 2].bitcast(BF16),
                                        mparts[:, :, :], identb[:, :]).then_inc(mt_ready, 1)

                def scores(b, u):
                    g, kt, j = units[u]
                    n = b * NU + u
                    if n >= SLOTS:
                        pe.wait_ge(e_ready, n - SLOTS + 1)
                    h = 4 * g + j
                    c = h // 2
                    nc.tensor.matmul(ps[:, 4 + n % SLOTS, :], stack[rows(h), b, 1, c, kt * P:(kt + 1) * P],
                                     stack[rows(h), b, 0, c, :], start=True, stop=True).then_inc(s_ready, 1)

                def values(b, k):
                    g, kt, _ = units[4 * k]
                    n = b * NU + 4 * k
                    pe.wait_ge(e_ready, n + 4)
                    out_n = b * GROUPS + g
                    if kt == 0 and out_n >= 1:
                        pe.wait_ge(o_read, out_n)
                    for j in range(4):
                        m = nc.tensor.matmul(ps[32 * j:32 * j + 32, 7, :], vaug[:, b, kt, 4 * g + j, :],
                                             probs[:, (n + j) % RING, :], start=(kt == 0), stop=(kt == TILES - 1),
                                             skip_group_check=True)
                    m.then_inc(pv_group, 1)

                for n in range(NM):
                    max_scores(0, n)
                turn_max(0)
                for b in range(BATCH):
                    pe.wait_ge(laid[b], 64)
                    done = 0
                    for k in range(NU // 4):
                        for j in range(4):
                            scores(b, 4 * k + j)
                            if b + 1 < BATCH and done < NM:
                                max_scores(b + 1, done)
                                done += 1
                        if b + 1 < BATCH and done < NM:
                            max_scores(b + 1, done)
                            done += 1
                        if b + 1 < BATCH and 5 * k < NM <= 5 * (k + 1):
                            turn_max(b + 1)
                        if k >= 1:
                            values(b, k - 1)
                    values(b, NU // 4 - 1)

            @block.scalar
            def _(act):
                for n in range(BATCH * NU):
                    act.wait_ge(s_ready, n + 1)
                    if n >= RING:
                        act.wait_ge(pv_group, (n - RING) // 4 + 1)
                    nc.scalar.activation(probs[:, n % RING, :], ps[:, 4 + n % SLOTS, :], ACT.Exp,
                                         scale=float(DK) ** -0.5).then_inc(e_ready, 1)

            @block.vector
            def _(dve):
                nc.vector.tensor_copy(identb[:, :], ident).then_inc(id_ready, 1)

                def reduce(b, k):
                    slot = b * per_batch + k
                    dve.wait_ge(m_ready, b * (NM // 2) + k + 1)
                    nc.vector.tensor_reduce(mx_out(b, k), ps[:, 2 * (slot % 2):2 * (slot % 2) + 2, :],
                                            AX.X, ALU.max).then_inc(m_read, 1)

                def mx_out(b, k):
                    n = 2 * k
                    c, parity, i = n // (2 * TILES), n // TILES % 2, n % TILES
                    at = parity * (MT // 2) + c * TILES + i
                    return mx[:, b, at:at + 2]

                def split_max(b):
                    slot = b * per_batch + NM // 2
                    dve.wait_ge(m_read, slot)
                    if b >= 1:
                        dve.wait_ge(mt_ready, b)
                    nc.vector.tensor_copy(mparts[:, 0, :], mx[:, b, :]).then_inc(mhi, 1)
                    dve.wait_ge(mhi, b + 1)
                    nc.vector.tensor_tensor(mparts[:, 1, :], mx[:, b, :], mparts[:, 0, :], ALU.subtract)\
                        .then_inc(mlo, 1)
                    dve.wait_ge(mt_ready, b + 1)
                    if b >= 1:
                        dve.wait_ge(m_stored[b - 1], 16)
                    nc.vector.tensor_copy(mrows[:, :], ps[:, 2 * (slot % 2), 0:P // 2].bitcast(BF16))\
                        .then_inc(m_read, 1)

                def take_out(b, g):
                    n = b * GROUPS + g
                    dve.wait_ge(pv_group, (n + 1) * TILES)
                    nc.vector.tensor_copy(outs[:, b, g, :], ps[:, 7, :]).then_inc(o_read, 1)

                for k in range(NM // 2):
                    reduce(0, k)
                split_max(0)
                for b in range(BATCH):
                    done = 0
                    for k in range(NU // 4):
                        if b + 1 < BATCH:
                            want = min(NM, 5 * (k + 1)) // 2
                            while done < want:
                                reduce(b + 1, done)
                                done += 1
                            if 5 * k < NM <= 5 * (k + 1):
                                split_max(b + 1)
                        if k % TILES == 0 and k >= TILES:
                            take_out(b, k // TILES - 1)
                    take_out(b, GROUPS - 1)


def attention_out(env, outer, wat, outs):
    nc, sem, ps, const = (env[k] for k in ("nc", "sem", "ps", "const"))
    xT = env["xT"]
    with ExitStack() as st:
        sb = env["sb_in"](st)
        inv = sb("inv", [P, 2, SEQ])
        on = sb("on", [P, 2, SEQ])
        sums_ready, inv_ready, scaled = sem("c_sums_ready"), sem("c_inverted"), sem("c_scaled")
        y_used, y_ready, added = sem("c_scaled_used"), sem("c_y_ready"), sem("c_added")
        log_ready = sem("c_log_ready")
        N = BATCH * GROUPS

        with nc.Block() as block:
            @block.scalar
            def _(act):
                nc.scalar.preload_act_table_set(LN_EXP)
                for n in range(N):
                    act.wait_ge(sums_ready, n + 1)
                    if n >= 2:
                        act.wait_ge(scaled, n - 1)
                    nc.scalar.activation(inv[:, n % 2, :], ps[:, n % 2, :], ACT.Ln).then_inc(log_ready, 1)
                    act.wait_ge(log_ready, n + 1)
                    nc.scalar.activation(inv[:, n % 2, :], inv[:, n % 2, :], ACT.Exp, scale=-1.0)\
                        .then_inc(inv_ready, 1)

            @block.tensor
            def _(pe):
                def spread_sums(n):
                    if n >= 2:
                        pe.wait_ge(log_ready, n - 1)
                    nc.tensor.matmul(ps[:, n % 2, :], const("sums"), outs[:, n // GROUPS, n % GROUPS, :],
                                     start=True, stop=True).then_inc(sums_ready, 1)

                def project(n):
                    b, g = n // GROUPS, n % GROUPS
                    pe.wait_ge(scaled, n + 1)
                    if g == 0 and b >= 2:
                        pe.wait_ge(added, b - 1)
                    w = W_ATTN["o0"] + g * P
                    m = nc.tensor.matmul(ps[:, 2 + b % 2, :], wat[:, w:w + P], on[:, n % 2, :],
                                         start=(g == 0), stop=(g == GROUPS - 1))
                    m.then_inc(y_used, 1)

                spread_sums(0)
                for n in range(N):
                    if n + 1 < N:
                        spread_sums(n + 1)
                    project(n)

            @block.vector
            def _(dve):
                for n in range(N):
                    b, g = n // GROUPS, n % GROUPS
                    dve.wait_ge(inv_ready, n + 1)
                    if n >= 2:
                        dve.wait_ge(y_used, n - 1)
                    nc.vector.tensor_tensor(on[:, n % 2, :], outs[:, b, g, :], inv[:, n % 2, :], ALU.mult)\
                        .then_inc(scaled, 1)
                    if g == 0 and b >= 1:
                        dve.wait_ge(y_used, b * GROUPS)
                        nc.vector.tensor_tensor(xT[:, b - 1, PAD:], xT[:, b - 1, PAD:], ps[:, 2 + (b - 1) % 2, :],
                                                ALU.add).then_inc(added, 1)
                dve.wait_ge(y_used, N)
                nc.vector.tensor_tensor(xT[:, BATCH - 1, PAD:], xT[:, BATCH - 1, PAD:],
                                        ps[:, 2 + (BATCH - 1) % 2, :], ALU.add).then_inc(added, 1)


def cross_attention(env, ctxT, w_xq, w_xkv, w_xo):
    nc, sem, ps, const, ident, mean_w = (env[k] for k in ("nc", "sem", "ps", "const", "ident", "mean_w"))
    xT, x2T, eps = env["xT"], env["x2T"], env["eps"]
    with ExitStack() as st:
        sb = env["sb_in"](st)
        zT = sb("zT", [LATENT, BATCH * CTX])
        zT4 = sb("zT4", [LATENT, BATCH, 4, CTX])
        wq = sb("x_wq", [P, P])
        wkv = sb("x_wkv", [LATENT, 2 * P])
        wo = sb("x_wo", [P, P])
        kT = sb("x_kT", [P, BATCH, CTX])
        kb = sb("x_kb", [P, BATCH, HEADS, CTX])
        vb = sb("x_vb", [P, BATCH, GROUPS, P])
        cen = sb("x_cen", [P, 2, SEQ])
        sq = sb("x_sq", [P, 2, SEQ])
        rstd = sb("x_rstd", [P, 2, SEQ])
        xn = sb("x_xn", [P, 2, SEQ])
        qT = sb("x_qT", [P, 2, SEQ])
        mx = sb("x_mx", [P, 2, HEADS])
        dif = sb("x_dif", [P, 2, HEADS, CTX])
        ex = sb("x_ex", [P, 2, HEADS, CTX])
        total = sb("x_total", [P, 2, HEADS])
        inv = sb("x_inv", [P, 2, HEADS])
        prob = sb("x_prob", [P, 2, HEADS * CTX])
        pT = sb("x_pT", [P, GROUPS, SEQ])
        oT = sb("x_oT", [P, SEQ])
        ld = sem("x_loaded")
        rep, kv_ready, kt_done, kb_done, vb_done = (sem("x_" + n) for n in
                                                    ("z_repeated", "kv_ready", "k_copied", "k_spread", "v_spread"))
        mean_ready, centred, squared = sem("x_mean_ready"), sem("x_centred"), sem("x_squared")
        var_ready, rstd_ready, normed = sem("x_var_ready"), sem("x_rstd_ready"), sem("x_normed")
        q_ready, q_copied = sem("x_q_ready"), sem("x_q_copied")
        s_ready, m_done, d_done, e_done = (sem("x_" + n) for n in ("scores", "max", "shifted", "exp"))
        t_done, i_done, p_done = (sem("x_" + n) for n in ("sum", "inverse", "probs"))
        pt_ready, pt_done, o_ready, o_done, y_ready, added = (
            sem("x_" + n) for n in ("probs_turned", "probs_copied", "out_ready", "out_copied", "y_ready", "added"))
        kept = sem("x_residual_kept")
        log_ready = sem("x_log_ready")

        with nc.Block() as block:
            @block.sync
            def _(sp):
                for dst, src in ((zT, ctxT), (wq, w_xq), (wkv, w_xkv), (wo, w_xo)):
                    sp.dma_start(dst[:, :], src).then_inc(ld, 16)
                sp.wait_ge(ld, 64)

            @block.tensor
            def _(pe):
                pe.wait_ge(ld, 64)
                nc.tensor.matmul(ps[:, 3, 0:P], wkv[:, 0:P], zT[:, :], start=True, stop=True)
                pe.wait_ge(rep, 1)
                for b in range(BATCH):
                    m = nc.tensor.matmul(ps[:, 4, b * P:(b + 1) * P], zT4[:, b, :, :], wkv[:, P:2 * P],
                                         start=True, stop=True)
                m.then_inc(kv_ready, 1)

                def norm(n, b):
                    if n >= 1:
                        pe.wait_ge(centred, n)
                    nc.tensor.matmul(ps[:, 0, :], mean_w, xT[:, b, PAD:], start=True, stop=True).then_inc(mean_ready, 1)
                    pe.wait_ge(squared, n + 1)
                    if n >= 1:
                        pe.wait_ge(rstd_ready, n)
                    nc.tensor.matmul(ps[:, 1, :], mean_w, sq[:, n % 2, :], start=True, stop=True).then_inc(var_ready, 1)

                def query(b):
                    pe.wait_ge(normed, b + 1)
                    if b >= 1:
                        pe.wait_ge(q_copied, b)
                    nc.tensor.matmul(ps[:, 2, :], wq[:, :], xn[:, b % 2, :], start=True, stop=True).then_inc(q_ready, 1)

                def scores(t):
                    b, i = t // TILES, t % TILES
                    pe.wait_ge(q_copied, b + 1)
                    if t == 0:
                        pe.wait_ge(vb_done, BATCH * GROUPS)
                        pe.wait_ge(kb_done, BATCH)
                    if t >= 2:
                        pe.wait_ge(d_done, t - 1)
                    nc.tensor.matmul(ps[:, 3 + t % 2, :], qT[:, b % 2, i * P:(i + 1) * P], kb[:, b, :, :],
                                     start=True, stop=True).then_inc(s_ready, 1)

                def turn(t):
                    pe.wait_ge(p_done, t + 1)
                    if t >= 2:
                        pe.wait_ge(pt_done, t - 1)
                    for g in range(GROUPS):
                        m = nc.tensor.transpose(ps[:, 5 + t % 2, g * P:(g + 1) * P], prob[:, t % 2, g * P:(g + 1) * P],
                                                ident)
                    m.then_inc(pt_ready, 1)

                def project(b):
                    pe.wait_ge(pt_done, (b + 1) * TILES)
                    if b >= 1:
                        pe.wait_ge(added, b)
                    for g in range(GROUPS):
                        m = nc.tensor.matmul(ps[:, 7, :], vb[:, b, g, :], pT[:, g, :], start=(g == 0),
                                             stop=(g == GROUPS - 1))
                    m.then_inc(o_ready, 1)
                    pe.wait_ge(o_done, b + 1)
                    nc.tensor.matmul(ps[:, 7, :], wo[:, :], oT[:, :], start=True, stop=True).then_inc(y_ready, 1)

                norm(0, 0)
                query(0)
                for b in range(BATCH):
                    if b + 1 < BATCH:
                        norm(b + 1, b + 1)
                    for i in range(TILES):
                        scores(b * TILES + i)
                        if i >= 1:
                            turn(b * TILES + i - 1)
                    turn(b * TILES + TILES - 1)
                    if b + 1 < BATCH:
                        query(b + 1)
                    project(b)
                for b in range(BATCH):
                    pe.wait_ge(added, b + 1)
                    norm(BATCH + b, b)

            @block.scalar
            def _(act):
                nc.scalar.preload_act_table_set(LN_EXP)
                act.wait_ge(ld, 64)
                nc.scalar.activation(zT4[:, :, :, :], zT[:, :].rearrange("p (b c) -> p b c", b=BATCH)[:, :, None, :]
                                     .broadcast_to([LATENT, BATCH, 4, CTX]), ACT.Copy).then_inc(rep, 1)

                def square(n):
                    act.wait_ge(centred, n + 1)
                    nc.scalar.activation(sq[:, n % 2, :], cen[:, n % 2, :], ACT.Square).then_inc(squared, 1)
                    act.wait_ge(var_ready, n + 1)
                    if n >= 2:
                        act.wait_ge(normed, n - 1)
                    nc.scalar.activation(rstd[:, n % 2, :], ps[:, 1, :], ACT.Ln, bias=eps).then_inc(log_ready, 1)
                    act.wait_ge(log_ready, n + 1)
                    nc.scalar.activation(rstd[:, n % 2, :], rstd[:, n % 2, :], ACT.Exp, scale=-0.5)\
                        .then_inc(rstd_ready, 1)

                def query(b):
                    act.wait_ge(q_ready, b + 1)
                    nc.scalar.activation(qT[:, b % 2, :], ps[:, 2, :], ACT.Copy).then_inc(q_copied, 1)

                def exps(t):
                    act.wait_ge(d_done, t + 1)
                    nc.scalar.activation(ex[:, t % 2], dif[:, t % 2], ACT.Exp, scale=float(DK) ** -0.5)\
                        .then_inc(e_done, 1)

                def turned(t):
                    b, i = t // TILES, t % TILES
                    act.wait_ge(pt_ready, t + 1)
                    if i == 0 and b >= 1:
                        act.wait_ge(o_ready, b)
                    nc.scalar.activation(pT[:, :, i * P:(i + 1) * P],
                                         ps[:, 5 + t % 2, :].rearrange("p (g q) -> p g q", g=GROUPS), ACT.Copy)\
                        .then_inc(pt_done, 1)

                square(0)
                query(0)
                for b in range(BATCH):
                    if b + 1 < BATCH:
                        square(b + 1)
                    for i in range(TILES):
                        exps(b * TILES + i)
                        if i >= 1:
                            turned(b * TILES + i - 1)
                    turned(b * TILES + TILES - 1)
                    if b + 1 < BATCH:
                        query(b + 1)
                    act.wait_ge(o_ready, b + 1)
                    nc.scalar.activation(oT[:, :], ps[:, 7, :], ACT.Copy).then_inc(o_done, 1)
                for b in range(BATCH):
                    square(BATCH + b)

            @block.gpsimd
            def _(pool):
                for t in range(BATCH * TILES):
                    pool.wait_ge(i_done, t + 1)
                    if t >= 2:
                        pool.wait_ge(pt_ready, t - 1)
                    nc.gpsimd.tensor_tensor(prob[:, t % 2, :].rearrange("p (h c) -> p h c", h=HEADS), ex[:, t % 2],
                                            inv[:, t % 2, :, None].broadcast_to([P, HEADS, CTX]), ALU.mult)\
                        .then_inc(p_done, 1)

            @block.vector
            def _(dve):
                dve.wait_ge(kv_ready, 1)
                nc.vector.tensor_copy(kT[:, :, :], ps[:, 3, 0:P].rearrange("p (b c) -> p b c", b=BATCH))\
                    .then_inc(kt_done, 1)
                dve.wait_ge(kt_done, 1)
                for b in range(BATCH):
                    nc.vector.tensor_tensor(kb[:, b], kT[:, b, None, :].broadcast_to([P, HEADS, CTX]),
                                            const("kmask")[:, :, None].broadcast_to([P, HEADS, CTX]), ALU.mult)\
                        .then_inc(kb_done, 1)
                    for g in range(GROUPS):
                        nc.vector.tensor_tensor(
                            vb[:, b, g, :].rearrange("p (h d) -> p h d", h=HEADS),
                            ps[:, 4, b * P:(b + 1) * P].rearrange("p (h d) -> p h d", h=HEADS),
                            const("vmask")[:, g * HEADS:(g + 1) * HEADS, None].broadcast_to([P, HEADS, DK]),
                            ALU.mult).then_inc(vb_done, 1)

                def norm(n, b, dst):
                    dve.wait_ge(mean_ready, n + 1)
                    if n >= 2:
                        dve.wait_ge(normed, n - 1)
                        dve.wait_ge(var_ready, n - 1)
                    nc.vector.tensor_tensor(cen[:, n % 2, :], xT[:, b, PAD:], ps[:, 0, :], ALU.subtract)\
                        .then_inc(centred, 1)
                    dve.wait_ge(rstd_ready, n + 1)
                    if 2 <= n < BATCH:
                        dve.wait_ge(q_ready, n - 1)
                    if dst is not xn:
                        dve.wait_ge(kept, b + 1)
                    nc.vector.tensor_tensor(xn[:, n % 2, :] if dst is xn else xT[:, b, PAD:], cen[:, n % 2, :],
                                            rstd[:, n % 2, :], ALU.mult).then_inc(normed, 1)

                def softmax(t):
                    dve.wait_ge(s_ready, t + 1)
                    sv = ps[:, 3 + t % 2, :].rearrange("p (h c) -> p h c", h=HEADS)
                    if t >= 2:
                        dve.wait_ge(d_done, t - 1)
                    nc.vector.tensor_reduce(mx[:, t % 2, :], sv, AX.X, ALU.max).then_inc(m_done, 1)
                    dve.wait_ge(m_done, t + 1)
                    if t >= 2:
                        dve.wait_ge(e_done, t - 1)
                    nc.vector.tensor_tensor(dif[:, t % 2], sv, mx[:, t % 2, :, None].broadcast_to([P, HEADS, CTX]),
                                            ALU.subtract).then_inc(d_done, 1)

                def sums(t):
                    dve.wait_ge(e_done, t + 1)
                    if t >= 2:
                        dve.wait_ge(i_done, t - 1)
                    nc.vector.tensor_reduce(total[:, t % 2, :], ex[:, t % 2], AX.X, ALU.add).then_inc(t_done, 1)
                    dve.wait_ge(t_done, t + 1)
                    if t >= 2:
                        dve.wait_ge(p_done, t - 1)
                    nc.vector.reciprocal(inv[:, t % 2, :], total[:, t % 2, :]).then_inc(i_done, 1)

                norm(0, 0, xn)
                for b in range(BATCH):
                    if b + 1 < BATCH:
                        norm(b + 1, b + 1, xn)
                    for i in range(TILES):
                        softmax(b * TILES + i)
                        sums(b * TILES + i)
                    dve.wait_ge(y_ready, b + 1)
                    nc.vector.tensor_tensor(xT[:, b, PAD:], xT[:, b, PAD:], ps[:, 7, :], ALU.add).then_inc(added, 1)
                    dve.wait_ge(added, b + 1)
                    nc.vector.tensor_copy(x2T[:, b, :], xT[:, b, PAD:]).then_inc(kept, 1)
                for b in range(BATCH):
                    norm(BATCH + b, b, xT)


def finish(env, out):
    nc, sem, ps, ident = (env[k] for k in ("nc", "sem", "ps", "ident"))
    xT, x2T = env["xT"], env["x2T"]
    with ExitStack() as st:
        sb = env["sb_in"](st)
        tok = sb("tok", [P, BATCH, TILES, DIM])
        summed, turned, copied = sem("f_summed"), sem("f_turned"), sem("f_copied")
        stored = [sem(f"f_stored{b}") for b in range(BATCH)]

        with nc.Block() as block:
            @block.vector
            def _(dve):
                for b in range(BATCH):
                    nc.vector.tensor_tensor(x2T[:, b, :], x2T[:, b, :], xT[:, b, PAD:], ALU.add).then_inc(summed, 1)

            @block.tensor
            def _(pe):
                for b in range(BATCH):
                    pe.wait_ge(summed, b + 1)
                    for i in range(TILES):
                        m = nc.tensor.transpose(ps[:, b, i * P:(i + 1) * P], x2T[:, b, i * P:(i + 1) * P], ident)
                    m.then_inc(turned, 1)

            @block.scalar
            def _(act):
                for b in range(BATCH):
                    act.wait_ge(turned, b + 1)
                    nc.scalar.activation(tok[:, b], ps[:, b, :].rearrange("p (i d) -> p i d", i=TILES), ACT.Copy)\
                        .then_inc(copied, 1)

            @block.sync
            def _(sp):
                for b in range(BATCH):
                    sp.wait_ge(copied, b + 1)
                    sp.dma_start(out[b].rearrange("(i p) d -> p i d", p=P), tok[:, b]).then_inc(stored[b], 16)
                for b in range(BATCH):
                    sp.wait_ge(stored[b], 16)


def layers(env, wqkv, qk_scales, wo, w1, w2, vecs):
    nc, sem, ps, const, ident, mean_w = (env[k] for k in ("nc", "sem", "ps", "const", "ident", "mean_w"))
    xT, xsT, eps = env["xT"], env["xsT"], env["eps"]
    NT = BATCH * TILES
    QK = 2 * HEADS
    with ExitStack() as st:
        sb = env["sb_in"](st)
        wqkv_sb = sb("l_wqkv", [P, 3 * INNER])
        wo_sb = sb("l_wo", [P, PAIRS, P])
        w1_sb = sb("l_w1", [P, 2 * HIDDEN])
        w2_sb = sb("l_w2", [P, len(HC), P])
        vec = sb("l_vec", [P, N_VEC])
        scales = sb("l_scales", [P, 2, DH])
        tab_c = sb("l_tab_c", [P, 2, TILES, DH])
        tab_s = sb("l_tab_s", [P, 2, TILES, DH])
        mask = sb("l_mask", [2 * WINDOW, BANK], BF16)
        mask_sel = sb("l_mask_sel", [2 * WINDOW, 2, P], BF16)
        sq = sb("l_sq", [P, QK, DH])
        norms = sb("l_norms", [P, 2, QK])
        qn = sb("l_qn", [P, 2, HEADS, DH])
        rot = sb("l_rot", [P, 2, HEADS, DH])
        rot_s = sb("l_rot_s", [P, 2, HEADS, DH])
        qT = sb("l_qT", [P, PAIRS, P])
        kb = sb("l_kb", [P, 2, PAIRS, 2, WINDOW + P])
        vb = sb("l_vb", [P, P // WINDOW, PAIRS, 2, DH])
        mx = sb("l_mx", [P, 2, HEADS])
        dif = sb("l_dif", [P, HEADS, 2 * WINDOW])
        prob = sb("l_prob", [P, 2, HEADS, 2 * WINDOW])
        total = sb("l_total", [P, 2, HEADS])
        inv = sb("l_inv", [P, 2, HEADS])
        pT = sb("l_pT", [P, PAIRS, P])
        o_tok = sb("l_o_tok", [P, HEADS, DH])
        oT = sb("l_oT", [P, PAIRS, SEQ])
        xf = sb("l_xf", [P, SEQ])
        cen = sb("l_cen", [P, SEQ])
        fsq = sb("l_fsq", [P, SEQ])
        rstd = sb("l_rstd", [P, SEQ])
        xg = sb("l_xg", [P, SEQ])
        gel = sb("l_gel", [P, len(HC), SEQ])
        hid = sb("l_hid", [P, len(HC), SEQ])
        ln256 = sb("l_ln256", [P, 1])

        first_ld, consts_set = sem("l_first_loaded"), sem("l_consts_set")
        wo_ld, w1_ld, w2_ld, vec_ld = (sem("l_" + n) for n in ("wo_loaded", "w1_loaded", "w2_loaded", "vec_loaded"))
        next_ld, next_scales = sem("l_next_wqkv_loaded"), sem("l_next_scales_loaded")
        xs_lo, xs_hi, tabs = sem("l_xs_low_half"), sem("l_xs_high_half"), sem("l_tables_ready")
        qk_full, qk_free = sem("l_qk_ready"), sem("l_qk_read")
        squared, summed, bounded = sem("l_squared"), sem("l_squares_summed"), sem("l_squares_bounded")
        logged, norm_ready = sem("l_norm_logged"), sem("l_norm_ready")
        sined, cosed, rotated = sem("l_sined"), sem("l_cosed"), sem("l_rotated")
        slot_full = [sem(f"l_slot{i}_full") for i in range(2)]
        slot_free = [sem(f"l_slot{i}_free") for i in range(2)]
        maxed, exped, sum_ready, inv_ready = (sem("l_" + n) for n in ("maxed", "exped", "sum_ready", "inv_ready"))
        xf_ready, fsquared, rstd_ready, xn_ready, xg_ready, gelu_ready = (
            sem("l_" + n) for n in ("ffn_x_ready", "ffn_squared", "rstd_ready", "xn_ready", "xg_ready", "gelu_ready"))
        body_sems = range(wo_ld.num, gelu_ready.num + 1)

        turns = {}

        def plan(*key):
            turns[key] = len(turns)

        STEPS = NT + 4
        for t in range(STEPS):
            b = (t - 6) // TILES if t >= 6 and (t - 6) % TILES == 0 else None
            by = (t - 7) // TILES if t >= 7 and (t - 7) % TILES == 0 else None
            if by is not None:
                plan("y", by)
            if b is not None:
                plan("wo", b)
            if 1 <= t <= NT:
                plan("qT", t - 1)
                plan("kT", t - 1)
            if b is not None:
                plan("mean", b)
            if 2 <= t <= NT + 1:
                plan("pT", t - 2)
            if 1 <= t <= NT:
                plan("s", t - 1)
            if b is not None:
                plan("var", b)
            if 2 <= t <= NT + 1:
                plan("o", t - 2)
            if 1 <= t <= NT:
                plan("v", t - 1, 0)
                plan("v", t - 1, 1)
            if 2 <= t <= NT + 1:
                plan("oT", t - 2)
            if b is not None:
                for c in range(len(HC)):
                    plan("h", b, c)

        def slot(*key):
            n = turns[key] % 2
            return ps[:, 4 + 2 * n:6 + 2 * n, :]

        def full(*key):
            n = turns[key]
            return slot_full[n % 2], n // 2 + 1

        def free(*key):
            n = turns[key]
            return slot_free[n % 2], n // 2 + 1

        def take(pe, *key):
            n = turns[key]
            if n >= 2:
                pe.wait_ge(slot_free[n % 2], n // 2)

        with nc.Block() as block:
            @block.sync
            def _(sp):
                sp.dma_start(wqkv_sb[:, :], wqkv[0]).then_inc(first_ld, 16)
                sp.dma_start(scales[:, :, :], qk_scales[0:1].broadcast_to([P, 2, DH])).then_inc(first_ld, 16)
                sp.wait_ge(first_ld, 32)

            @block.gpsimd
            def _(pool):
                pool.memset(ln256[:, :], QK_SCALE * 0.6931471805599453).then_inc(consts_set, 1)
                pool.memset(xsT[:, :, 0:1], 0.0).then_inc(consts_set, 1)
                pool.memset(kb[:, :, :, :, :], 0.0).then_inc(consts_set, 1)
                pool.memset(vb[:, :, :, :, :], 0.0).then_inc(consts_set, 1)

            @block.vector
            def _(dve):
                nc.vector.tensor_copy(mask[:, :], const("wmask")[0:2 * WINDOW, :]).then_inc(consts_set, 1)
                nc.vector.tensor_copy(mask_sel[:, :, :],
                                      const("wsel")[0:2 * WINDOW, :].rearrange("p (a q) -> p a q", a=2))\
                    .then_inc(consts_set, 1)

        with nc.Fori(0, LAYERS) as layer:
            with nc.Block() as block:
                @block.sync
                def _(sp):
                    sp.dma_start(wo_sb[:, :, :], wo[layer].rearrange("(c p) n -> p c n", p=P)).then_inc(wo_ld, 16)
                    sp.dma_start(vec[:, :], vecs[layer]).then_inc(vec_ld, 16)
                    sp.dma_start(w1_sb[:, :], w1[layer]).then_inc(w1_ld, 16)
                    sp.dma_start(w2_sb[:, :, :], w2[layer].rearrange("(c p) n -> p c n", p=P)).then_inc(w2_ld, 16)
                    sp.wait_ge(tabs, 3)
                    sp.dma_start(scales[:, :, :], qk_scales[layer + 1][None].broadcast_to([P, 2, DH]))\
                        .then_inc(next_scales, 16)
                    sp.wait_ge(*full("v", NT - 1, 0))
                    sp.wait_ge(*full("v", NT - 1, 1))
                    sp.dma_start(wqkv_sb[:, :], wqkv[layer + 1]).then_inc(next_ld, 16)
                    sp.wait_ge(next_scales, 16)
                    sp.wait_ge(next_ld, 16)

                @block.gpsimd
                def _(pool):
                    for t in range(NT):
                        if t == 0:
                            pool.wait_ge(tabs, 1)
                        pool.wait_ge(qk_free, t + 1)
                        if t >= 1:
                            pool.wait_ge(*full("kT", t - 1))
                        nc.gpsimd.tensor_tensor(rot[:, :, :, :], qn[:, :, :, :],
                                                tab_c[:, :, t % TILES, None, :].broadcast_to([P, 2, HEADS, DH]),
                                                ALU.mult).then_inc(cosed, 1)
                        pool.wait_ge(cosed, t + 1)
                        pool.wait_ge(sined, t + 1)
                        nc.gpsimd.tensor_tensor(rot[:, :, :, :], rot[:, :, :, :], rot_s[:, :, :, :], ALU.add)\
                            .then_inc(rotated, 1)

                @block.tensor
                def _(pe):
                    def project_qk(t):
                        b, i = t // TILES, t % TILES
                        if i == 0:
                            pe.wait_ge(xs_lo, b + 1)
                            pe.wait_ge(xs_hi, b + 1)
                        if t >= 1:
                            pe.wait_ge(qk_free, t)
                        x_tile = xsT[:, b, PAD + i * P:PAD + (i + 1) * P]
                        for n in range(4):
                            m = nc.tensor.matmul(ps[:, n, :], x_tile, wqkv_sb[:, n * BANK:(n + 1) * BANK],
                                                 start=True, stop=True)
                        m.then_inc(qk_full, 1)

                    def turn_qk(t):
                        pe.wait_ge(rotated, t + 1)
                        for n, name in enumerate(("qT", "kT")):
                            take(pe, name, t)
                            dst = slot(name, t)
                            for c in range(PAIRS):
                                m = nc.tensor.transpose(dst[:, c // 4, (c % 4) * P:(c % 4 + 1) * P],
                                                        rot[:, n, 2 * c:2 * c + 2, :], ident)
                            m.then_inc(full(name, t)[0], 1)

                    def scores(t):
                        pe.wait_ge(*free("qT", t))
                        pe.wait_ge(*free("kT", t))
                        take(pe, "s", t)
                        dst = slot("s", t)
                        first = int(t % TILES == 0)
                        for n in range(2):
                            nc.tensor.matmul(dst[:, n, :], mask_sel[:, first, :], mask[:, :], start=True, stop=False,
                                             skip_group_check=True)
                        for c in range(PAIRS):
                            for j in range(P // WINDOW):
                                a = j * WINDOW
                                m = nc.tensor.matmul(dst[a:a + WINDOW, c // 4, (c % 4) * P:(c % 4 + 1) * P],
                                                     qT[:, c, a:a + WINDOW], kb[:, t % 2, c, :, a:a + 2 * WINDOW],
                                                     start=False, stop=True, skip_group_check=True)
                        m.then_inc(full("s", t)[0], 1)

                    def turn_probs(t):
                        pe.wait_ge(exped, t + 1)
                        take(pe, "pT", t)
                        dst = slot("pT", t)
                        for c in range(PAIRS):
                            m = nc.tensor.transpose(dst[:, c // 4, (c % 4) * P:(c % 4 + 1) * P],
                                                    prob[:, t % 2, 2 * c:2 * c + 2, :], ident)
                        m.then_inc(full("pT", t)[0], 1)

                    def values(t):
                        pe.wait_ge(*free("pT", t))
                        pe.wait_ge(*free("v", t, 0))
                        pe.wait_ge(*free("v", t, 1))
                        take(pe, "o", t)
                        dst = slot("o", t)
                        for c in range(PAIRS):
                            for j in range(P // WINDOW):
                                a = j * WINDOW
                                m = nc.tensor.matmul(dst[a:a + WINDOW, c // 4, (c % 4) * P:(c % 4 + 1) * P],
                                                     pT[:, c, a:a + WINDOW], vb[:, j, c, :, :],
                                                     start=True, stop=True, skip_group_check=True)
                        m.then_inc(full("o", t)[0], 1)

                    def turn_out(t):
                        pe.wait_ge(*free("o", t))
                        take(pe, "oT", t)
                        dst = slot("oT", t)
                        for c in range(PAIRS):
                            m = nc.tensor.transpose(dst[:, c // 4, (c % 4) * P:(c % 4 + 1) * P],
                                                    o_tok[:, 2 * c:2 * c + 2, :], ident)
                        m.then_inc(full("oT", t)[0], 1)

                    def project_v(t):
                        b, i = t // TILES, t % TILES
                        wv = wqkv_sb[:, 2 * INNER:].rearrange("p (c a d) -> p a c d", a=2, d=DH)
                        for half in range(2):
                            take(pe, "v", t, half)
                            dst = slot("v", t, half)
                            for n in range(2):
                                a = i * P + (2 * half + n) * WINDOW
                                for parity in range(2):
                                    m = nc.tensor.matmul(dst[64 * parity:64 * parity + 64, n, :],
                                                         xsT[:, b, a:a + 2 * WINDOW], wv[:, parity],
                                                         start=True, stop=True, skip_group_check=True)
                            m.then_inc(full("v", t, half)[0], 1)

                    def project_out(b):
                        if b == 0:
                            pe.wait_ge(wo_ld, 16)
                        pe.wait_ge(*free("oT", (b + 1) * TILES - 1))
                        take(pe, "wo", b)
                        for c in range(PAIRS):
                            m = nc.tensor.matmul(slot("wo", b)[:, 0, :], wo_sb[:, c, :], oT[:, c, :],
                                                 start=(c == 0), stop=(c == PAIRS - 1))
                        m.then_inc(full("wo", b)[0], 1)

                    def moment(name, src, ready, b):
                        pe.wait_ge(ready, b + 1)
                        take(pe, name, b)
                        nc.tensor.matmul(slot(name, b)[:, 0, :], mean_w, src[:, :], start=True, stop=True)\
                            .then_inc(full(name, b)[0], 1)

                    def hidden(b):
                        pe.wait_ge(xg_ready, b + 1)
                        if b == 0:
                            pe.wait_ge(w1_ld, 16)
                        for c, (a, n) in enumerate(HC):
                            take(pe, "h", b, c)
                            for s in range(2):
                                w = w1_sb[:, s * HIDDEN + a:s * HIDDEN + a + n]
                                m = nc.tensor.matmul(slot("h", b, c)[0:n, s, :], w, xg[:, :], start=True, stop=True)
                            m.then_inc(full("h", b, c)[0], 1)

                    def project_ffn(b):
                        for c in range(len(HC)):
                            pe.wait_ge(*free("h", b, c))
                        if b == 0:
                            pe.wait_ge(w2_ld, 16)
                        take(pe, "y", b)
                        for c, (a, n) in enumerate(HC):
                            m = nc.tensor.matmul(slot("y", b)[:, 0, :], w2_sb[0:n, c, :], hid[0:n, c, :],
                                                 start=(c == 0), stop=(c == len(HC) - 1))
                        m.then_inc(full("y", b)[0], 1)

                    for t in range(STEPS):
                        b = (t - 6) // TILES if t >= 6 and (t - 6) % TILES == 0 else None
                        by = (t - 7) // TILES if t >= 7 and (t - 7) % TILES == 0 else None
                        if t < NT:
                            project_qk(t)
                        if by is not None:
                            project_ffn(by)
                        if b is not None:
                            project_out(b)
                        if 1 <= t <= NT:
                            turn_qk(t - 1)
                        if b is not None:
                            moment("mean", xf, xf_ready, b)
                        if 2 <= t <= NT + 1:
                            turn_probs(t - 2)
                        if 1 <= t <= NT:
                            scores(t - 1)
                        if b is not None:
                            moment("var", fsq, fsquared, b)
                        if 2 <= t <= NT + 1:
                            values(t - 2)
                        if 1 <= t <= NT:
                            project_v(t - 1)
                        if 2 <= t <= NT + 1:
                            turn_out(t - 2)
                        if b is not None:
                            hidden(b)

                @block.scalar
                def _(act):
                    nc.scalar.preload_act_table_set(LN_EXP)

                    def copy_slot(key, dst, src=None):
                        act.wait_ge(*full(*key))
                        nc.scalar.activation(dst, slot(*key) if src is None else src, ACT.Copy)\
                            .then_inc(free(*key)[0], 1)

                    def square(t):
                        act.wait_ge(qk_full, t + 1)
                        if t >= 1:
                            act.wait_ge(summed, t)
                        nc.scalar.activation(sq[:, :, :], ps[:, 0:4, :].rearrange("p n (h d) -> p (n h) d", d=DH),
                                             ACT.Square).then_inc(squared, 1)

                    def inverse_norm(t):
                        act.wait_ge(bounded, t + 1)
                        nc.scalar.activation(norms[:, t % 2, :], norms[:, t % 2, :], ACT.Ln, scale=65536.0)\
                            .then_inc(logged, 1)
                        act.wait_ge(logged, t + 1)
                        nc.scalar.activation(norms[:, t % 2, :], norms[:, t % 2, :], ACT.Exp, scale=-0.5,
                                             bias=ln256[:, 0:1]).then_inc(norm_ready, 1)

                    def copy_q(t):
                        if t >= 1:
                            act.wait_ge(*full("s", t - 1))
                        copy_slot(("qT", t), qT[:, :, :].rearrange("p (n c) q -> p n (c q)", n=2))

                    def copy_k(t):
                        act.wait_ge(*full("kT", t))
                        src = slot("kT", t).rearrange("p n (c q) -> p (n c) q", q=P)
                        if t >= 1:
                            act.wait_ge(*full("s", t - 1))
                        for parity in range(2):
                            r = slice(64 * parity, 64 * parity + 64)
                            if t % TILES != TILES - 1:
                                nc.scalar.activation(kb[r, (t + 1) % 2, :, parity, 0:WINDOW],
                                                     src[r, :, P - WINDOW:P], ACT.Copy)
                            m = nc.scalar.activation(kb[r, t % 2, :, parity, WINDOW:], src[r, :, :], ACT.Copy)
                        m.then_inc(free("kT", t)[0], 1)

                    def exps(t):
                        act.wait_ge(*free("s", t))
                        if t >= 2:
                            act.wait_ge(*full("pT", t - 2))
                            act.wait_ge(sum_ready, t - 1)
                        nc.scalar.activation(prob[:, t % 2], dif[:, :, :], ACT.Exp, scale=QK_SCALE).then_inc(exped, 1)

                    def copy_probs(t):
                        if t >= 1:
                            act.wait_ge(*full("o", t - 1))
                        copy_slot(("pT", t), pT[:, :, :].rearrange("p (n c) q -> p n (c q)", n=2))

                    def copy_v(t, half):
                        act.wait_ge(*full("v", t, half))
                        if t >= 1:
                            act.wait_ge(*full("o", t - 1))
                        for parity in range(2):
                            r = slice(64 * parity, 64 * parity + 64)
                            m = nc.scalar.activation(vb[r, 2 * half:2 * half + 2, :, parity, :],
                                                     slot("v", t, half)[r].rearrange("p n (c d) -> p n c d", d=DH),
                                                     ACT.Copy)
                        m.then_inc(free("v", t, half)[0], 1)

                    def copy_out(t):
                        b, i = t // TILES, t % TILES
                        act.wait_ge(*full("oT", t))
                        if b >= 1 and i == 0:
                            act.wait_ge(*full("wo", b - 1))
                        nc.scalar.activation(oT[:, :, i * P:(i + 1) * P],
                                             slot("oT", t).rearrange("p n (c q) -> p (n c) q", q=P), ACT.Copy)\
                            .then_inc(free("oT", t)[0], 1)

                    for b in range(BATCH):
                        nc.scalar.activation(xsT[0:64, b, 1:], xT[0:64, b, 1:], ACT.Copy).then_inc(xs_lo, 1)
                    for t in range(STEPS):
                        b = (t - 6) // TILES if t >= 6 and (t - 6) % TILES == 0 else None
                        if t < NT:
                            square(t)
                        if b is not None:
                            act.wait_ge(*free("wo", b))
                            if b >= 1:
                                act.wait_ge(*free("mean", b - 1))
                            nc.scalar.activation(xf[0:64, :], xT[0:64, b, PAD:], ACT.Copy)
                            nc.scalar.activation(xf[64:P, :], xT[64:P, b, PAD - 1:PAD + SEQ - 1], ACT.Copy)\
                                .then_inc(xf_ready, 1)
                        if 1 <= t <= NT:
                            copy_q(t - 1)
                        if t < NT:
                            inverse_norm(t)
                        if 1 <= t <= NT:
                            copy_k(t - 1)
                        if b is not None:
                            act.wait_ge(*free("mean", b))
                            nc.scalar.activation(fsq[:, :], cen[:, :], ACT.Square).then_inc(fsquared, 1)
                        if 2 <= t <= NT + 1:
                            copy_probs(t - 2)
                        if 1 <= t <= NT:
                            exps(t - 1)
                        if b is not None:
                            act.wait_ge(*full("var", b))
                            nc.scalar.activation(rstd[:, :], slot("var", b)[:, 0, :], ACT.Ln, bias=eps)\
                                .then_inc(free("var", b)[0], 1)
                            act.wait_ge(*free("var", b))
                            nc.scalar.activation(rstd[:, :], rstd[:, :], ACT.Exp, scale=-0.5).then_inc(rstd_ready, 1)
                        if 1 <= t <= NT:
                            copy_v(t - 1, 0)
                            copy_v(t - 1, 1)
                        if 2 <= t <= NT + 1:
                            copy_out(t - 2)
                        if b is not None:
                            for c, (a, n) in enumerate(HC):
                                act.wait_ge(*full("h", b, c))
                                if b == 0 and c == 0:
                                    act.wait_ge(vec_ld, 16)
                                if b >= 1 and c == 0:
                                    for k in range(len(HC)):
                                        act.wait_ge(*free("h", b - 1, k))
                                nc.scalar.activation(gel[0:n, c, :], slot("h", b, c)[0:n, 1, :], ACT.Gelu,
                                                     bias=vec[0:n, V_B1 + 3 + c:V_B1 + 4 + c]).then_inc(gelu_ready, 1)
                            nc.scalar.preload_act_table_set(LN_EXP)

                @block.vector
                def _(dve):
                    def sum_squares(t):
                        dve.wait_ge(squared, t + 1)
                        if t >= 2:
                            dve.wait_ge(qk_free, t - 1)
                        nc.vector.tensor_reduce(norms[:, t % 2, :], sq[:, :, :], AX.X, ALU.add).then_inc(summed, 1)
                        dve.wait_ge(summed, t + 1)
                        nc.vector.tensor_scalar(norms[:, t % 2, :], norms[:, t % 2, :], 1e-24, None, ALU.max)\
                            .then_inc(bounded, 1)

                    def normalise(t):
                        dve.wait_ge(norm_ready, t + 1)
                        if t >= 1:
                            dve.wait_ge(cosed, t)
                            dve.wait_ge(sined, t)
                        nc.vector.tensor_tensor(qn[:, :, :, :].rearrange("p a h d -> p (a h) d"),
                                                ps[:, 0:4, :].rearrange("p n (h d) -> p (n h) d", d=DH),
                                                norms[:, t % 2, :, None].broadcast_to([P, QK, DH]), ALU.mult)\
                            .then_inc(qk_free, 1)

                    def sine_part(t):
                        i, H2 = t % TILES, DH // 2
                        dve.wait_ge(qk_free, t + 1)
                        if t >= 1:
                            dve.wait_ge(rotated, t)
                        if t == 0:
                            dve.wait_ge(tabs, 3)
                        for a in (0, H2):
                            m = nc.vector.tensor_tensor(rot_s[:, :, :, a:a + H2], qn[:, :, :, H2 - a:DH - a],
                                                        tab_s[:, :, i, None, a:a + H2]
                                                        .broadcast_to([P, 2, HEADS, H2]), ALU.mult)
                        m.then_inc(sined, 1)

                    def shift_scores(t):
                        s = slot("s", t).rearrange("p n (h k) -> p (n h) k", k=2 * WINDOW)
                        dve.wait_ge(*full("s", t))
                        nc.vector.tensor_reduce(mx[:, t % 2, :], s, AX.X, ALU.max).then_inc(maxed, 1)
                        dve.wait_ge(maxed, t + 1)
                        if t >= 1:
                            dve.wait_ge(exped, t)
                        nc.vector.tensor_tensor(dif[:, :, :], s,
                                                mx[:, t % 2, :, None].broadcast_to([P, HEADS, 2 * WINDOW]),
                                                ALU.subtract).then_inc(free("s", t)[0], 1)

                    def sums(t):
                        dve.wait_ge(exped, t + 1)
                        nc.vector.tensor_reduce(total[:, t % 2, :], prob[:, t % 2], AX.X, ALU.add)\
                            .then_inc(sum_ready, 1)
                        dve.wait_ge(sum_ready, t + 1)
                        if t >= 2:
                            dve.wait_ge(*free("o", t - 2))
                        nc.vector.reciprocal(inv[:, t % 2, :], total[:, t % 2, :]).then_inc(inv_ready, 1)

                    def scale_out(t):
                        dve.wait_ge(*full("o", t))
                        dve.wait_ge(inv_ready, t + 1)
                        if t >= 1:
                            dve.wait_ge(*full("oT", t - 1))
                        nc.vector.tensor_tensor(o_tok[:, :, :], slot("o", t).rearrange("p n (h d) -> p (n h) d", d=DH),
                                                inv[:, t % 2, :, None].broadcast_to([P, HEADS, DH]), ALU.mult)\
                            .then_inc(free("o", t)[0], 1)

                    for b in range(BATCH):
                        nc.vector.tensor_copy(xsT[64:P, b, 1:], xT[64:P, b, 0:PAD + SEQ - 1]).then_inc(xs_hi, 1)
                    rope_c = const("ropeC").rearrange("p (a i d) -> p a i d", a=2, i=TILES)
                    rope_s = const("ropeS").rearrange("p (a i d) -> p a i d", a=2, i=TILES)
                    nc.vector.tensor_tensor(tab_c[:, :, :, :], rope_c,
                                            scales[:, :, None, :].broadcast_to([P, 2, TILES, DH]), ALU.mult)\
                        .then_inc(tabs, 1)
                    for a in (0, DH // 2):
                        o = DH // 2 - a
                        nc.vector.tensor_tensor(tab_s[:, :, :, a:a + DH // 2], rope_s[:, :, :, a:a + DH // 2],
                                                scales[:, :, None, o:o + DH // 2]
                                                .broadcast_to([P, 2, TILES, DH // 2]), ALU.mult).then_inc(tabs, 1)
                    for t in range(STEPS):
                        b = (t - 6) // TILES if t >= 6 and (t - 6) % TILES == 0 else None
                        by = (t - 7) // TILES if t >= 7 and (t - 7) % TILES == 0 else None
                        if t < NT:
                            sum_squares(t)
                        if by is not None:
                            dve.wait_ge(*full("y", by))
                            nc.vector.scalar_tensor_tensor(out=xT[:, by, PAD:], in0=slot("y", by)[:, 0, :],
                                                           scalar=vec[:, V_B2:V_B2 + 1], in1=xT[:, by, PAD:],
                                                           op0=ALU.add, op1=ALU.add).then_inc(free("y", by)[0], 1)
                        if b is not None:
                            dve.wait_ge(*full("wo", b))
                            nc.vector.tensor_tensor(xT[:, b, PAD:], xT[:, b, PAD:], slot("wo", b)[:, 0, :], ALU.add)\
                                .then_inc(free("wo", b)[0], 1)
                        if b is not None:
                            dve.wait_ge(*full("mean", b))
                            if b >= 1:
                                dve.wait_ge(*full("var", b - 1))
                                dve.wait_ge(xn_ready, b)
                            nc.vector.tensor_tensor(cen[:, :], xf[:, :], slot("mean", b)[:, 0, :], ALU.subtract)\
                                .then_inc(free("mean", b)[0], 1)
                        if 1 <= t <= NT:
                            shift_scores(t - 1)
                        if t < NT:
                            normalise(t)
                            sine_part(t)
                        if b is not None:
                            dve.wait_ge(rstd_ready, b + 1)
                            if b >= 1:
                                dve.wait_ge(*full("h", b - 1, len(HC) - 1))
                            nc.vector.tensor_tensor(xg[:, :], cen[:, :], rstd[:, :], ALU.mult).then_inc(xn_ready, 1)
                            dve.wait_ge(xn_ready, b + 1)
                            if b == 0:
                                dve.wait_ge(vec_ld, 16)
                            nc.vector.tensor_scalar(xg[:, :], xg[:, :], vec[:, V_G:V_G + 1], vec[:, V_B:V_B + 1],
                                                    ALU.mult, ALU.add).then_inc(xg_ready, 1)
                        if 2 <= t <= NT + 1:
                            scale_out(t - 2)
                        if 1 <= t <= NT:
                            sums(t - 1)
                        if b is not None:
                            for c, (a, n) in enumerate(HC):
                                dve.wait_ge(gelu_ready, len(HC) * b + c + 1)
                                dve.wait_ge(*full("h", b, c))
                                if b >= 1 and c == 0:
                                    dve.wait_ge(*full("y", b - 1))
                                nc.vector.scalar_tensor_tensor(out=hid[0:n, c, :], in0=slot("h", b, c)[0:n, 0, :],
                                                               scalar=vec[0:n, V_B1 + c:V_B1 + c + 1],
                                                               in1=gel[0:n, c, :], op0=ALU.add, op1=ALU.mult)\
                                    .then_inc(free("h", b, c)[0], 1)
            nc.all_engine_barrier(sems_to_clear=body_sems)


def shape_constants():
    import numpy as np
    c = np.zeros((P, N_CONST), np.float32)

    def put(name, a):
        at, n = CONST[name]
        c[:, at:at + n] = np.asarray(a, np.float32).reshape(P, n)

    f = np.float32
    put("ident", np.eye(P))
    put("mean", np.full((P, P), 1.0 / DIM))
    sums = np.zeros((P, P))
    for j in range(4):
        sums[32 * j + DK, 32 * j:32 * j + 32] = 1.0
    put("sums", sums)
    inv = f(1.0) / np.power(f(10000.0), (np.arange(0, DK, 2, dtype=f) / f(DK)), dtype=f)
    fr = np.arange(SEQ, dtype=f)[:, None] * inv[None, :]
    emb = np.concatenate([fr, fr], -1)
    sign = np.where(np.arange(DK) < DK // 2, -1.0, 1.0)
    put("cosT", np.tile(np.cos(emb).T, (HEADS, 1)))
    put("sinT", np.tile(np.sin(emb).T * sign[:, None], (HEADS, 1)))
    p = np.arange(P)
    put("kmask", (p[:, None] // DK) == np.arange(HEADS)[None, :])
    put("vmask", (4 * np.arange(GROUPS)[None, :, None] + (p // CTX)[:, None, None]) == np.arange(HEADS)[None, None, :])
    half = np.arange(0, DH, 2, dtype=f)
    inv = f(1.0) / np.power(f(10000.0), half / f(DH), dtype=f)
    t = np.arange(SEQ, dtype=f)
    fr = t[:, None] * inv[None, :]
    fr = np.concatenate([fr, fr], -1)
    base = (half + f(0.4 * DH)) / f(1.4 * DH)
    power = (t - SEQ // 2) / f(WINDOW // 2)
    sc = np.power(base[None, :], power[:, None], dtype=f)
    sc = np.concatenate([sc, sc], -1)
    sgn = np.where(np.arange(DH) < DH // 2, -1.0, 1.0).astype(f)
    for name, tab in (("ropeC", np.cos(fr)), ("ropeS", np.sin(fr) * sgn)):
        a = np.stack([tab * sc, tab * (f(1.0) / sc)])
        put(name, a.reshape(2, TILES, P, DH).transpose(2, 0, 1, 3))
    m = np.zeros((P, 8, 2 * WINDOW))
    key = np.arange(2 * WINDOW)
    for r in range(WINDOW):
        bad = (key < r) | (key > r + WINDOW)
        m[r] = np.where(bad, -1e30, 0.0)
        m[WINDOW + r] = np.where(bad | (key < WINDOW), -1e30, 0.0)
    put("wmask", m)
    s = np.zeros((P, 2, P))
    for q in range(P):
        s[q % WINDOW, 0, q] = 1.0
        s[q % WINDOW + (WINDOW if q < WINDOW else 0), 1, q] = 1.0
    put("wsel", s)
    return c


def kernel(x, ctx_512, L0_attn_Wq, L0_attn_Wk, L0_attn_Wv, L0_attn_Wo, L0_xattn_Wq, L0_xattn_Wkv, L0_xattn_Wo,
           L0_ffn_Wqkv, L0_ffn_q_scale, L0_ffn_k_scale, L0_ffn_Wo, L0_ffn_ln_g, L0_ffn_ln_b, L0_ffn_W1, L0_ffn_b1,
           L0_ffn_W2, L0_ffn_b2):
    import numpy as np
    import concourse.bacc as bacc
    from concourse.bass_utils import run_bass_kernel_spmd

    T = lambda a: np.ascontiguousarray(np.asarray(a).T)
    rot = np.arange(DIM).reshape(HEADS, DK)
    rot = np.concatenate([rot[:, 1::2], rot[:, ::2]], -1).reshape(-1)
    wq, wk, wv, wo_a = (T(a) for a in (L0_attn_Wq, L0_attn_Wk, L0_attn_Wv, L0_attn_Wo))
    w_attn = np.zeros((P, 9 * P), wq.dtype)
    for name, a in (("q", wq), ("k", wk), ("qr", wq[:, rot]), ("kr", wk[:, rot]), ("v", wv)):
        w_attn[:, W_ATTN[name]:W_ATTN[name] + P] = a
    for h in range(HEADS):
        at, r = W_ATTN["o0"] + (h // 4) * P, 32 * (h % 4)
        w_attn[r:r + DK, at:at + P] = wo_a[h * DK:(h + 1) * DK]
    vecs = np.zeros((LAYERS, P, N_VEC), np.asarray(x).dtype)
    b1 = np.asarray(L0_ffn_b1)
    for s in range(2):
        for c, (at, n) in enumerate(HC):
            vecs[:, :n, V_B1 + 3 * s + c] = b1[:, s * HIDDEN + at:s * HIDDEN + at + n]
    for col, a in ((V_G, L0_ffn_ln_g), (V_B, L0_ffn_ln_b), (V_B2, L0_ffn_b2)):
        vecs[:, :, col] = np.asarray(a)
    w2 = np.zeros((LAYERS, len(HC) * P, P), vecs.dtype)
    w2[:, :HIDDEN] = np.asarray(L0_ffn_W2)
    again = lambda a: np.concatenate([np.asarray(a), np.asarray(a)[:1]], 0)
    arrays = {
        "x": np.asarray(x).reshape(BATCH * SEQ, DIM),
        "ctxT": T(np.asarray(ctx_512).reshape(BATCH * CTX, LATENT)),
        "w_attn": w_attn,
        "w_xq": T(L0_xattn_Wq), "w_xkv": T(L0_xattn_Wkv), "w_xo": T(L0_xattn_Wo),
        "wqkv": again(L0_ffn_Wqkv),
        "qk_scales": again(np.stack([np.asarray(L0_ffn_q_scale), np.asarray(L0_ffn_k_scale)], 1)),
        "wo": np.asarray(L0_ffn_Wo), "w1": np.asarray(L0_ffn_W1), "w2": w2, "vecs": vecs,
        "consts": shape_constants(),
    }
    nc = bacc.Bacc("TRN2", target_bir_lowering=False, num_devices=1)
    args = [nc.dram_tensor(n, a.shape, mybir.dt.from_np(a.dtype), kind="ExternalInput").ap() for n, a in arrays.items()]
    scratch = nc.dram_tensor("scratch", (BATCH, P, 3, 2, SEQ), BF16, kind="Internal").ap()
    max_scratch = nc.dram_tensor("max_scratch", (BATCH, P, P), BF16, kind="Internal").ap()
    out = nc.dram_tensor("out", (BATCH, SEQ, DIM), F32, kind="ExternalOutput").ap()
    decoder(nc, *args, scratch, max_scratch, out)
    r = run_bass_kernel_spmd(nc, [arrays], core_ids=[0])
    return r.results[0]["out"]
```

```python
from contextlib import ExitStack

import concourse.bass as bass
from concourse import mybir
from concourse.alu_op_type import AluOpType as ALU

ACT = mybir.ActivationFunctionType
AX = mybir.AxisListType
F32 = mybir.dt.float32
BF16 = mybir.dt.bfloat16

P = 128
BATCH, SEQ, DIM = 4, 512, 128
TILES = SEQ // P
HEADS = 16
DK = DIM // HEADS
PAIRS = HEADS // 2
GROUPS = HEADS // 4
CTX, LATENT = 32, 64
LAYERS = 6
DH = 64
INNER = HEADS * DH
WINDOW = 32
PAD = WINDOW
HIDDEN = int(DIM * 4 * 2 / 3)
HC = [(0, 128), (128, 128), (256, HIDDEN - 256)]
EPS = 1e-5
QK_SCALE = 8.0
LN_EXP = "natural_log_exp_and_others"
BANK = 512

Q_PARTS = [(0, 3, 0, True), (3, 2, 1, True), (5, 1, 2, True)]
K_PARTS = [(0, 3, 0, False), (3, 2, 0, False), (5, 1, 0, False)]
MAX_ROW = 6 * DK

CONST = {}
_at = 0
for _name, _n in (("ident", P), ("mean", P), ("sums", P), ("cosT", SEQ), ("sinT", SEQ),
                  ("kmask", HEADS), ("vmask", GROUPS * HEADS), ("ropeC", 2 * TILES * DH),
                  ("ropeS", 2 * TILES * DH), ("wmask", 8 * 2 * WINDOW), ("wsel", 2 * P)):
    CONST[_name] = (_at, _n)
    _at += _n
N_CONST = _at
W_ATTN = {n: i * P for i, n in enumerate(("q", "k", "qr", "kr", "v", "o0", "o1", "o2", "o3"))}
V_B1, V_G, V_B, V_B2, N_VEC = 0, 6, 7, 8, 9

RING = 8
WARM_UP = 5


def decoder(nc, x, ctxT, w_attn, w_xq, w_xkv, w_xo, wqkv, qk_scales, wo, w1, w2, vecs, consts, scratch, max_scratch, out):
    with ExitStack() as top:
        def sb_in(stack):
            return lambda name, shape, dt=F32: stack.enter_context(nc.sbuf_tensor(name, shape, dt))

        def sem(name):
            return top.enter_context(nc.semaphore(name))

        sb = sb_in(top)
        ps = top.enter_context(nc.psum_tensor("ps", [P, 8, BANK], F32))
        cst = sb("cst", [P, N_CONST])
        xT = sb("xT", [P, BATCH, PAD + SEQ])
        xsT = sb("xsT", [P, BATCH, PAD + SEQ])
        x2T = sb("x2T", [P, BATCH, SEQ])

        def const(name):
            a, n = CONST[name]
            return cst[:, a:a + n]

        ident, mean_w = const("ident"), const("mean")
        eps_tile = sb("eps", [P, 1])
        eps = eps_tile[:, 0:1]
        env = dict(eps=eps, nc=nc, sem=sem, ps=ps, const=const, ident=ident, mean_w=mean_w, xT=xT, xsT=xsT, x2T=x2T,
                   sb_in=sb_in)
        self_attention(env, x, w_attn, consts, cst, scratch, max_scratch)
        cross_attention(env, ctxT, w_xq, w_xkv, w_xo)
        layers(env, wqkv, qk_scales, wo, w1, w2, vecs)
        finish(env, out)


def self_attention(env, x, w_attn, consts, cst, scratch, max_scratch):
    nc, sem, ps, const, ident, mean_w = (env[k] for k in ("nc", "sem", "ps", "const", "ident", "mean_w"))
    xT = env["xT"]
    with ExitStack() as st:
        sb = env["sb_in"](st)
        wat = sb("wat", [P, 9 * P])
        stack = sb("stack", [P, BATCH, 2, PAIRS, SEQ], BF16)
        vaug = sb("vaug", [P, BATCH, TILES, HEADS, 32])
        more_outs = sb("outs", [P, BATCH - 2, GROUPS, SEQ])
        outs = [env["x2T"][:, :, :], env["xsT"][:, :, :].rearrange("p b n -> p (b n)")[:, 0:GROUPS * SEQ]
                .rearrange("p (g n) -> p g n", g=GROUPS)] + [more_outs[:, b] for b in range(BATCH - 2)]
        probs = sb("probs", [P, RING, SEQ])
        with ExitStack() as inner:
            project, laid = project_parts(env, inner, x, wat, w_attn, consts, cst, scratch, stack, vaug,
                                          probs)
            softmax = softmax_values(env, inner, stack, vaug, probs, outs, max_scratch, laid)

            with nc.Block() as block:
                @block.sync
                def _(sp):
                    project["sync"](sp)
                    softmax["sync"](sp)

                @block.gpsimd
                def _(pool):
                    project["gpsimd"](pool)
                    softmax["gpsimd"](pool)

                @block.tensor
                def _(pe):
                    project["tensor"](pe)
                    softmax["tensor"](pe)

                @block.scalar
                def _(act):
                    project["scalar"](act)
                    softmax["scalar"](act)

                @block.vector
                def _(dve):
                    project["vector"](dve)
                    softmax["vector"](dve)
        attention_out(env, st, wat, outs)


def project_parts(env, stack_of, x, wat, w_attn, consts, cst, scratch, stack, vaug, probs):
    nc, sem, ps, const, ident, mean_w = (env[k] for k in ("nc", "sem", "ps", "const", "ident", "mean_w"))
    xT, eps = env["xT"], env["eps"]
    sb = env["sb_in"](stack_of)
    xtok = probs[:, 0:BATCH, :].rearrange("p b (i d) -> p (b i) d", d=DIM)
    cen = sb("cen", [P, 2, SEQ])
    sq = sb("sq", [P, 2, SEQ])
    rstd = sb("rstd", [P, SEQ])
    xn = sb("xn", [P, 2, SEQ])
    rc = sb("rc", [P, 2, SEQ])
    rs = sb("rs", [P, 2, SEQ])
    parts = sb("parts", [P, 2, 3, 2, SEQ], BF16)
    minus1 = sb("minus1", [2, SEQ], BF16)
    c_ld, w_ld = sem("a_consts_loaded"), sem("a_weights_loaded")
    x_ld = [sem(f"a_x_loaded{b}") for b in range(BATCH)]
    pads, eps_set, log_ready = sem("a_pads_zeroed"), sem("a_eps_set"), sem("a_log_ready")
    vz, vo, stack_zeroed = sem("a_vaug_zeroed"), sem("a_ones_set"), sem("a_stack_zeroed")
    xt_ready, xt_copied = sem("a_xT_ready"), sem("a_xT_copied")
    mean_ready, centred, squared = sem("a_mean_ready"), sem("a_centred"), sem("a_squared")
    var_ready, rstd_ready, normed = sem("a_var_ready"), sem("a_rstd_ready"), sem("a_normed")
    projected, v_copied = sem("a_projected"), sem("a_v_copied")
    cosed, sined, rotated = sem("a_cosed"), sem("a_sined"), sem("a_rotated")
    hi_ready, rest_ready, mid_ready, lo_ready = (sem("a_" + n) for n in ("hi", "rest", "mid", "lo"))
    stored = [sem(f"a_stored{b}") for b in range(BATCH)]
    minus_ones_set = sem("a_minus_ones_set")
    laid_sems = [sem(f"a_laid_out{b}") for b in range(BATCH)]
    laid_count = 16 * (2 + 2 * sum(copies for table in (Q_PARTS, K_PARTS) for _, copies, _, _ in table))
    xv = x.rearrange("(t p) d -> p t d", p=P)
    STEPS = BATCH + 2

    def sync(sp):
        sp.dma_start(cst[:, 0:CONST["kmask"][0]], consts[:, 0:CONST["kmask"][0]]).then_inc(c_ld, 16)
        for b in range(BATCH):
            sp.dma_start(xtok[:, b * TILES:(b + 1) * TILES, :],
                         xv[:, b * TILES:(b + 1) * TILES, :]).then_inc(x_ld[b], 16)
            if b == 0:
                sp.dma_start(wat[:, :], w_attn).then_inc(w_ld, 16)
        sp.dma_start(cst[:, CONST["kmask"][0]:], consts[:, CONST["kmask"][0]:]).then_inc(c_ld, 16)
        sp.wait_ge(minus_ones_set, 1)
        for b in range(BATCH):
            sp.wait_ge(stack_zeroed, b + 1)
            for parity in range(2):
                a = 64 * parity + MAX_ROW
                sp.dma_start(stack[a:a + 2, b, 1, :, :],
                             minus1[:, None, :].broadcast_to([2, PAIRS, SEQ])).then_inc(laid_sems[b], 16)
            sp.wait_ge(lo_ready, b + 1)
            sp.dma_start(scratch[b], parts[:, b % 2]).then_inc(stored[b], 16)
            sp.wait_ge(stored[b], 16)
            for qk, table in enumerate((Q_PARTS, K_PARTS)):
                for parity in range(2):
                    src = scratch[b].rearrange("(c a r) s k t -> a s r k c t", a=2, r=DK)[parity]
                    for row, copies, part, same in table:
                        for j in range(copies):
                            a = parity * 64 + (row + j) * DK
                            sp.dma_start(stack[a:a + DK, b, qk, :, :],
                                         src[part if same else part + j, :, qk]).then_inc(laid_sems[b], 16)
        sp.wait_ge(c_ld, 32)

    def gpsimd(pool):
        pool.memset(eps, EPS).then_inc(eps_set, 1)
        pool.memset(minus1[:, :], -1.0).then_inc(minus_ones_set, 1)
        pool.memset(stack[:, 0], 0.0).then_inc(stack_zeroed, 1)
        pool.memset(vaug[:, :, :, :, :], 0.0).then_inc(vz, 1)
        pool.wait_ge(vz, 1)
        pool.memset(vaug[:, :, :, :, DK:DK + 1], 1.0).then_inc(vo, 1)
        for b in range(1, BATCH):
            pool.memset(stack[:, b], 0.0).then_inc(stack_zeroed, 1)
        pool.memset(xT[:, :, 0:PAD], 0.0).then_inc(pads, 1)
        pool.wait_ge(c_ld, 32)

    def tensor(pe):
        def turn(b):
            pe.wait_ge(x_ld[b], 16)
            if b >= 1:
                pe.wait_ge(xt_copied, b)
            for i in range(TILES):
                t = nc.tensor.transpose(ps[:, 0, i * P:(i + 1) * P], xtok[:, b * TILES + i, :], ident)
            t.then_inc(xt_ready, 1)

        def project(b):
            pe.wait_ge(normed, b + 1)
            if b == 0:
                pe.wait_ge(w_ld, 16)
            if b >= 1:
                pe.wait_ge(sined, b)
                pe.wait_ge(v_copied, b)
            for n, name in enumerate(("q", "k", "qr", "kr")):
                w = W_ATTN[name]
                nc.tensor.matmul(ps[:, 3 + n, :], wat[:, w:w + P], xn[:, b % 2, :], start=True, stop=True)
            for i in range(TILES):
                m = nc.tensor.matmul(ps[:, 7, i * P:(i + 1) * P], xn[:, b % 2, i * P:(i + 1) * P],
                                     wat[:, W_ATTN["v"]:W_ATTN["v"] + P], start=True, stop=True)
            m.then_inc(projected, 1)

        def mean(b):
            pe.wait_ge(xt_copied, b + 1)
            if b >= 1:
                pe.wait_ge(centred, b)
            nc.tensor.matmul(ps[:, 1, :], mean_w, xT[:, b, PAD:], start=True, stop=True).then_inc(mean_ready, 1)

        def variance(b):
            pe.wait_ge(squared, b + 1)
            if b >= 1:
                pe.wait_ge(log_ready, b)
            nc.tensor.matmul(ps[:, 2, :], mean_w, sq[:, b % 2, :], start=True, stop=True).then_inc(var_ready, 1)

        pe.wait_ge(c_ld, 16)
        for s in range(STEPS):
            if s < BATCH:
                turn(s)
                mean(s)
            if 1 <= s <= BATCH:
                variance(s - 1)
            if s >= 2:
                project(s - 2)
        pe.wait_ge(sined, BATCH)
        pe.wait_ge(v_copied, BATCH)
        pe.wait_ge(rstd_ready, BATCH)

    def scalar(act):
        nc.scalar.preload_act_table_set(LN_EXP)
        for s in range(STEPS):
            if s < BATCH:
                act.wait_ge(xt_ready, s + 1)
                nc.scalar.activation(xT[:, s, PAD:], ps[:, 0, :], ACT.Copy).then_inc(xt_copied, 1)
            if s < BATCH:
                act.wait_ge(centred, s + 1)
                if s >= 2:
                    act.wait_ge(var_ready, s - 1)
                nc.scalar.activation(sq[:, s % 2, :], cen[:, s % 2, :], ACT.Square).then_inc(squared, 1)
            if 1 <= s <= BATCH:
                b = s - 1
                act.wait_ge(var_ready, b + 1)
                if b == 0:
                    act.wait_ge(eps_set, 1)
                if b >= 1:
                    act.wait_ge(normed, b)
                nc.scalar.activation(rstd[:, :], ps[:, 2, :], ACT.Ln, bias=eps).then_inc(log_ready, 1)
                act.wait_ge(log_ready, b + 1)
                nc.scalar.activation(rstd[:, :], rstd[:, :], ACT.Exp, scale=-0.5).then_inc(rstd_ready, 1)
            if s >= 2:
                b = s - 2
                act.wait_ge(projected, b + 1)
                if b == 0:
                    act.wait_ge(vo, 1)
                nc.scalar.activation(vaug[:, b, :, :, 0:DK],
                                     ps[:, 7, :].rearrange("p (i h d) -> p i h d", i=TILES, h=HEADS),
                                     ACT.Copy).then_inc(v_copied, 1)
                if b >= 2:
                    act.wait_ge(stored[b - 2], 16)
                act.wait_ge(rotated, b + 1)
                nc.scalar.activation(parts[:, b % 2, 0], rc[:, :, :], ACT.Copy).then_inc(hi_ready, 1)
                act.wait_ge(rest_ready, s - 1)
                nc.scalar.activation(parts[:, (s - 2) % 2, 1], rs[:, :, :], ACT.Copy).then_inc(mid_ready, 1)

    def vector(dve):
        cos2 = const("cosT")[:, None, :].broadcast_to([P, 2, SEQ])
        sin2 = const("sinT")[:, None, :].broadcast_to([P, 2, SEQ])
        for s in range(STEPS):
            if s < BATCH:
                dve.wait_ge(mean_ready, s + 1)
                if s >= 2:
                    dve.wait_ge(normed, s - 1)
                    dve.wait_ge(squared, s - 1)
                nc.vector.tensor_tensor(cen[:, s % 2, :], xT[:, s, PAD:], ps[:, 1, :], ALU.subtract)\
                    .then_inc(centred, 1)
            if 1 <= s <= BATCH:
                b = s - 1
                dve.wait_ge(rstd_ready, b + 1)
                if b >= 2:
                    dve.wait_ge(projected, b - 1)
                nc.vector.tensor_tensor(xn[:, b % 2, :], cen[:, b % 2, :], rstd[:, :], ALU.mult)\
                    .then_inc(normed, 1)
            if s >= 2:
                b = s - 2
                dve.wait_ge(projected, b + 1)
                if b >= 1:
                    dve.wait_ge(lo_ready, b)
                nc.vector.tensor_tensor(rc[:, :, :], ps[:, 3:5, :], cos2, ALU.mult).then_inc(cosed, 1)
                nc.vector.tensor_tensor(rs[:, :, :], ps[:, 5:7, :], sin2, ALU.mult).then_inc(sined, 1)
                dve.wait_ge(sined, b + 1)
                dve.wait_ge(cosed, b + 1)
                nc.vector.tensor_tensor(rc[:, :, :], rc[:, :, :], rs[:, :, :], ALU.add).then_inc(rotated, 1)
                dve.wait_ge(hi_ready, s - 1)
                nc.vector.tensor_tensor(rs[:, :, :], rc[:, :, :], parts[:, s % 2, 0], ALU.subtract)\
                    .then_inc(rest_ready, 1)
                dve.wait_ge(mid_ready, s - 1)
                nc.vector.tensor_tensor(parts[:, s % 2, 2], rs[:, :, :], parts[:, s % 2, 1], ALU.subtract)\
                    .then_inc(lo_ready, 1)

    return (dict(sync=sync, gpsimd=gpsimd, tensor=tensor, scalar=scalar, vector=vector),
            [(laid, laid_count) for laid in laid_sems])


def softmax_values(env, stack_of, stack, vaug, probs, outs, max_scratch, parts_laid):
    nc, sem, ps, const, ident = (env[k] for k in ("nc", "sem", "ps", "const", "ident"))
    sb = env["sb_in"](stack_of)
    MT = TILES * HEADS
    mx = sb("mx", [P, BATCH, MT])
    mparts = sb("mparts", [P, 2, MT], BF16)
    mrows = sb("mrows", [P, P], BF16)
    identb = sb("identb", [P, P], BF16)
    id_ready, warm = sem("b_ident_ready"), sem("b_warm")
    m_ready, m_read = sem("b_max_scores_ready"), sem("b_max_scores_read")
    mhi, mlo, mt_ready = (sem("b_" + n) for n in ("max_hi", "max_lo", "max_turned"))
    laid = [sem(f"b_max_laid{b}") for b in range(BATCH)]
    m_stored = [sem(f"b_max_stored{b}") for b in range(BATCH)]
    s_ready, e_ready = sem("b_scores_ready"), sem("b_exp_ready")
    pv_group, o_read = sem("b_probs_used"), sem("b_out_read")
    SLOTS = 3
    units = [(g, kt, j) for g in range(GROUPS) for kt in range(TILES) for j in range(4)]
    NU = len(units)
    NM = HEADS * TILES
    order = [(b, k) for b in range(BATCH) for k in range(NM // 2)]
    for b in reversed(range(BATCH)):
        order.insert((b + 1) * (NM // 2) + 6, (b, "turn"))
    slot_of = {event: n for n, event in enumerate(order)}
    AHEAD = NM + 32

    def rows(h):
        return slice(64 * (h % 2), 64 * (h % 2) + 64)

    def sync(sp):
        for b in range(BATCH):
            sp.wait_ge(m_read, slot_of[b, "turn"] + 1)
            sp.dma_start(max_scratch[b], mrows[:, :]).then_inc(m_stored[b], 16)
            sp.wait_ge(m_stored[b], 16)
            for part in range(2):
                for parity in range(2):
                    a = part * MT + parity * (MT // 2)
                    r = 64 * parity + MAX_ROW + part
                    sp.dma_start(stack[r:r + 1, b, 0, :, :].rearrange("o c (i q) -> o (c i) q", q=P),
                                 max_scratch[b, a:a + MT // 2, :].rearrange("(o n) q -> o n q", o=1))\
                        .then_inc(laid[b], 16)

    def tensor(pe):
        pe.wait_ge(id_ready, 1)

        def max_scores(b, n):
            c, parity, i = n // (2 * TILES), n // TILES % 2, n % TILES
            slot = slot_of[b, n // 2]
            if n % 2 == 0 and slot >= 2:
                pe.wait_ge(m_read, slot - 1)
            h = 2 * c + parity
            if n == 0:
                pe.wait_ge(*parts_laid[b])
            m = nc.tensor.matmul(ps[:, 2 * (slot % 2) + n % 2, :], stack[rows(h), b, 0, c, i * P:(i + 1) * P],
                                 stack[rows(h), b, 1, c, :], start=True, stop=True)
            if n % 2:
                m.then_inc(m_ready, 1)

        def turn_max(b):
            slot = slot_of[b, "turn"]
            pe.wait_ge(m_read, slot - 1)
            pe.wait_ge(mlo, b + 1)
            nc.tensor.transpose(ps[:, 2 * (slot % 2), 0:P // 2].bitcast(BF16),
                                mparts[:, :, :], identb[:, :]).then_inc(mt_ready, 1)

        def scores(b, u):
            g, kt, j = units[u]
            n = b * NU + u
            if n >= SLOTS:
                pe.wait_ge(e_ready, n - SLOTS + 1)
            h = 4 * g + j
            c = h // 2
            nc.tensor.matmul(ps[:, 4 + n % SLOTS, :], stack[rows(h), b, 1, c, kt * P:(kt + 1) * P],
                             stack[rows(h), b, 0, c, :], start=True, stop=True).then_inc(s_ready, 1)

        def values(b, k):
            g, kt, _ = units[4 * k]
            n = b * NU + 4 * k
            pe.wait_ge(e_ready, n + 4)
            out_n = b * GROUPS + g
            if kt == 0 and out_n >= 1:
                pe.wait_ge(o_read, out_n)
            for j in range(4):
                m = nc.tensor.matmul(ps[32 * j:32 * j + 32, 7, :], vaug[:, b, kt, 4 * g + j, :],
                                     probs[:, (n + j) % RING, :], start=(kt == 0), stop=(kt == TILES - 1),
                                     skip_group_check=True)
            m.then_inc(pv_group, 1)

        def stream(first, last):
            for m in range(first, min(last, BATCH * NM)):
                max_scores(m // NM, m % NM)
                after = slot_of[m // NM, m % NM // 2] + 1
                if m % 2 and after < len(order) and order[after][1] == "turn":
                    turn_max(order[after][0])

        stream(0, AHEAD)
        for _ in range(WARM_UP):
            w = nc.tensor.matmul(ps[:, 7, :], ident, env["xT"][:, 0, PAD:], start=True, stop=True)
        w.then_inc(warm, 1)
        pe.wait_ge(warm, 1)
        for b in range(BATCH):
            pe.wait_ge(laid[b], 64)
            for k in range(NU // 4):
                for j in range(4):
                    scores(b, 4 * k + j)
                    m = AHEAD + b * NU + 4 * k + j
                    stream(m, m + 1)
                if k >= 1:
                    values(b, k - 1)
            values(b, NU // 4 - 1)

    def scalar(act):
        for n in range(BATCH * NU):
            act.wait_ge(s_ready, n + 1)
            if n >= RING:
                act.wait_ge(pv_group, (n - RING) // 4 + 1)
            nc.scalar.activation(probs[:, n % RING, :], ps[:, 4 + n % SLOTS, :], ACT.Exp,
                                 scale=float(DK) ** -0.5).then_inc(e_ready, 1)

    def gpsimd(pool):
        nc.gpsimd.tensor_copy(identb[:, :], ident).then_inc(id_ready, 1)

    def vector(dve):
        def reduce(b, k):
            slot = slot_of[b, k]
            dve.wait_ge(m_ready, b * (NM // 2) + k + 1)
            nc.vector.tensor_reduce(mx_out(b, k), ps[:, 2 * (slot % 2):2 * (slot % 2) + 2, :],
                                    AX.X, ALU.max).then_inc(m_read, 1)

        def mx_out(b, k):
            n = 2 * k
            c, parity, i = n // (2 * TILES), n // TILES % 2, n % TILES
            at = parity * (MT // 2) + c * TILES + i
            return mx[:, b, at:at + 2]

        def split_max(b):
            dve.wait_ge(m_read, slot_of[b, NM // 2 - 1] + 1)
            if b >= 1:
                dve.wait_ge(mt_ready, b)
            nc.vector.tensor_copy(mparts[:, 0, :], mx[:, b, :]).then_inc(mhi, 1)
            dve.wait_ge(mhi, b + 1)
            nc.vector.tensor_tensor(mparts[:, 1, :], mx[:, b, :], mparts[:, 0, :], ALU.subtract).then_inc(mlo, 1)

        def take_turned(b):
            slot = slot_of[b, "turn"]
            dve.wait_ge(mt_ready, b + 1)
            if b >= 1:
                dve.wait_ge(m_stored[b - 1], 16)
            nc.vector.tensor_copy(mrows[:, :], ps[:, 2 * (slot % 2), 0:P // 2].bitcast(BF16)).then_inc(m_read, 1)

        def take_out(b, g):
            n = b * GROUPS + g
            dve.wait_ge(pv_group, (n + 1) * TILES)
            nc.vector.tensor_copy(outs[b][:, g, :], ps[:, 7, :]).then_inc(o_read, 1)

        def stream(first, last):
            for m in range(first, min(last, BATCH * NM), 2):
                b, k = m // NM, m % NM // 2
                reduce(b, k)
                if k == NM // 2 - 1:
                    split_max(b)
                after = slot_of[b, k] + 1
                if after < len(order) and order[after][1] == "turn":
                    take_turned(order[after][0])

        stream(0, AHEAD)
        for b in range(BATCH):
            for k in range(NU // 4):
                m = AHEAD + b * NU + 4 * k
                stream(m, m + 4)
                if k % TILES == 0 and k >= TILES:
                    take_out(b, k // TILES - 1)
            take_out(b, GROUPS - 1)

    return dict(sync=sync, gpsimd=gpsimd, tensor=tensor, scalar=scalar, vector=vector)


def attention_out(env, outer, wat, outs):
    nc, sem, ps, const = (env[k] for k in ("nc", "sem", "ps", "const"))
    xT = env["xT"]
    with ExitStack() as st:
        sb = env["sb_in"](st)
        inv = sb("inv", [P, 2, SEQ])
        on = sb("on", [P, 2, SEQ])
        sums_ready, inv_ready, scaled = sem("c_sums_ready"), sem("c_inverted"), sem("c_scaled")
        y_used, y_ready, added = sem("c_scaled_used"), sem("c_y_ready"), sem("c_added")
        log_ready = sem("c_log_ready")
        N = BATCH * GROUPS

        with nc.Block() as block:
            @block.scalar
            def _(act):
                nc.scalar.preload_act_table_set(LN_EXP)
                for n in range(N):
                    act.wait_ge(sums_ready, n + 1)
                    if n >= 2:
                        act.wait_ge(scaled, n - 1)
                    nc.scalar.activation(inv[:, n % 2, :], ps[:, n % 2, :], ACT.Ln).then_inc(log_ready, 1)
                    act.wait_ge(log_ready, n + 1)
                    nc.scalar.activation(inv[:, n % 2, :], inv[:, n % 2, :], ACT.Exp, scale=-1.0)\
                        .then_inc(inv_ready, 1)

            @block.tensor
            def _(pe):
                def spread_sums(n):
                    if n >= 2:
                        pe.wait_ge(log_ready, n - 1)
                    nc.tensor.matmul(ps[:, n % 2, :], const("sums"), outs[n // GROUPS][:, n % GROUPS, :],
                                     start=True, stop=True).then_inc(sums_ready, 1)

                def project(n):
                    b, g = n // GROUPS, n % GROUPS
                    pe.wait_ge(scaled, n + 1)
                    if g == 0 and b >= 2:
                        pe.wait_ge(added, b - 1)
                    w = W_ATTN["o0"] + g * P
                    m = nc.tensor.matmul(ps[:, 2 + b % 2, :], wat[:, w:w + P], on[:, n % 2, :],
                                         start=(g == 0), stop=(g == GROUPS - 1))
                    m.then_inc(y_used, 1)

                spread_sums(0)
                for n in range(N):
                    if n + 1 < N:
                        spread_sums(n + 1)
                    project(n)

            @block.vector
            def _(dve):
                for n in range(N):
                    b, g = n // GROUPS, n % GROUPS
                    dve.wait_ge(inv_ready, n + 1)
                    if n >= 2:
                        dve.wait_ge(y_used, n - 1)
                    nc.vector.tensor_tensor(on[:, n % 2, :], outs[b][:, g, :], inv[:, n % 2, :], ALU.mult)\
                        .then_inc(scaled, 1)
                    if g == 0 and b >= 1:
                        dve.wait_ge(y_used, b * GROUPS)
                        nc.vector.tensor_tensor(xT[:, b - 1, PAD:], xT[:, b - 1, PAD:], ps[:, 2 + (b - 1) % 2, :],
                                                ALU.add).then_inc(added, 1)
                dve.wait_ge(y_used, N)
                nc.vector.tensor_tensor(xT[:, BATCH - 1, PAD:], xT[:, BATCH - 1, PAD:],
                                        ps[:, 2 + (BATCH - 1) % 2, :], ALU.add).then_inc(added, 1)


def cross_attention(env, ctxT, w_xq, w_xkv, w_xo):
    nc, sem, ps, const, ident, mean_w = (env[k] for k in ("nc", "sem", "ps", "const", "ident", "mean_w"))
    xT, x2T, eps = env["xT"], env["x2T"], env["eps"]
    with ExitStack() as st:
        sb = env["sb_in"](st)
        zT = sb("zT", [LATENT, BATCH * CTX])
        zT4 = sb("zT4", [LATENT, BATCH, 4, CTX])
        wq = sb("x_wq", [P, P])
        wkv = sb("x_wkv", [LATENT, 2 * P])
        wo = sb("x_wo", [P, P])
        kT = sb("x_kT", [P, BATCH, CTX])
        kb = sb("x_kb", [P, BATCH, HEADS, CTX])
        vb = sb("x_vb", [P, BATCH, GROUPS, P])
        cen = sb("x_cen", [P, 2, SEQ])
        sq = sb("x_sq", [P, 2, SEQ])
        rstd = sb("x_rstd", [P, 2, SEQ])
        xn = sb("x_xn", [P, 2, SEQ])
        qT = sb("x_qT", [P, 2, SEQ])
        mx = sb("x_mx", [P, 2, HEADS])
        dif = sb("x_dif", [P, 2, HEADS, CTX])
        ex = sb("x_ex", [P, 2, HEADS, CTX])
        total = sb("x_total", [P, 2, HEADS])
        inv = sb("x_inv", [P, 2, HEADS])
        prob = sb("x_prob", [P, 2, HEADS * CTX])
        pT = sb("x_pT", [P, GROUPS, SEQ])
        oT = sb("x_oT", [P, SEQ])
        ld = sem("x_loaded")
        rep, kv_ready, kt_done, kb_done, vb_done = (sem("x_" + n) for n in
                                                    ("z_repeated", "kv_ready", "k_copied", "k_spread", "v_spread"))
        mean_ready, centred, squared = sem("x_mean_ready"), sem("x_centred"), sem("x_squared")
        var_ready, rstd_ready, normed = sem("x_var_ready"), sem("x_rstd_ready"), sem("x_normed")
        q_ready, q_copied = sem("x_q_ready"), sem("x_q_copied")
        s_ready, m_done, d_done, e_done = (sem("x_" + n) for n in ("scores", "max", "shifted", "exp"))
        t_done, i_done, p_done = (sem("x_" + n) for n in ("sum", "inverse", "probs"))
        pt_ready, pt_done, o_ready, o_done, y_ready, added = (
            sem("x_" + n) for n in ("probs_turned", "probs_copied", "out_ready", "out_copied", "y_ready", "added"))
        kept = sem("x_residual_kept")
        log_ready = sem("x_log_ready")

        with nc.Block() as block:
            @block.sync
            def _(sp):
                for dst, src in ((zT, ctxT), (wq, w_xq), (wkv, w_xkv), (wo, w_xo)):
                    sp.dma_start(dst[:, :], src).then_inc(ld, 16)
                sp.wait_ge(ld, 64)

            @block.tensor
            def _(pe):
                pe.wait_ge(ld, 64)
                nc.tensor.matmul(ps[:, 3, 0:P], wkv[:, 0:P], zT[:, :], start=True, stop=True)
                pe.wait_ge(rep, 1)
                for b in range(BATCH):
                    m = nc.tensor.matmul(ps[:, 4, b * P:(b + 1) * P], zT4[:, b, :, :], wkv[:, P:2 * P],
                                         start=True, stop=True)
                m.then_inc(kv_ready, 1)

                def norm(n, b):
                    if n >= 1:
                        pe.wait_ge(centred, n)
                    nc.tensor.matmul(ps[:, 0, :], mean_w, xT[:, b, PAD:], start=True, stop=True).then_inc(mean_ready, 1)
                    pe.wait_ge(squared, n + 1)
                    if n >= 1:
                        pe.wait_ge(rstd_ready, n)
                    nc.tensor.matmul(ps[:, 1, :], mean_w, sq[:, n % 2, :], start=True, stop=True).then_inc(var_ready, 1)

                def query(b):
                    pe.wait_ge(normed, b + 1)
                    if b >= 1:
                        pe.wait_ge(q_copied, b)
                    nc.tensor.matmul(ps[:, 2, :], wq[:, :], xn[:, b % 2, :], start=True, stop=True).then_inc(q_ready, 1)

                def scores(t):
                    b, i = t // TILES, t % TILES
                    pe.wait_ge(q_copied, b + 1)
                    if t == 0:
                        pe.wait_ge(vb_done, BATCH * GROUPS)
                        pe.wait_ge(kb_done, BATCH)
                    if t >= 2:
                        pe.wait_ge(d_done, t - 1)
                    nc.tensor.matmul(ps[:, 3 + t % 2, :], qT[:, b % 2, i * P:(i + 1) * P], kb[:, b, :, :],
                                     start=True, stop=True).then_inc(s_ready, 1)

                def turn(t):
                    pe.wait_ge(p_done, t + 1)
                    if t >= 2:
                        pe.wait_ge(pt_done, t - 1)
                    for g in range(GROUPS):
                        m = nc.tensor.transpose(ps[:, 5 + t % 2, g * P:(g + 1) * P], prob[:, t % 2, g * P:(g + 1) * P],
                                                ident)
                    m.then_inc(pt_ready, 1)

                def project(b):
                    pe.wait_ge(pt_done, (b + 1) * TILES)
                    if b >= 1:
                        pe.wait_ge(added, b)
                    for g in range(GROUPS):
                        m = nc.tensor.matmul(ps[:, 7, :], vb[:, b, g, :], pT[:, g, :], start=(g == 0),
                                             stop=(g == GROUPS - 1))
                    m.then_inc(o_ready, 1)
                    pe.wait_ge(o_done, b + 1)
                    nc.tensor.matmul(ps[:, 7, :], wo[:, :], oT[:, :], start=True, stop=True).then_inc(y_ready, 1)

                norm(0, 0)
                query(0)
                for b in range(BATCH):
                    if b + 1 < BATCH:
                        norm(b + 1, b + 1)
                    for i in range(TILES):
                        scores(b * TILES + i)
                        if i >= 1:
                            turn(b * TILES + i - 1)
                    turn(b * TILES + TILES - 1)
                    if b + 1 < BATCH:
                        query(b + 1)
                    project(b)
                for b in range(BATCH):
                    pe.wait_ge(added, b + 1)
                    norm(BATCH + b, b)

            @block.scalar
            def _(act):
                nc.scalar.preload_act_table_set(LN_EXP)
                act.wait_ge(ld, 64)
                nc.scalar.activation(zT4[:, :, :, :], zT[:, :].rearrange("p (b c) -> p b c", b=BATCH)[:, :, None, :]
                                     .broadcast_to([LATENT, BATCH, 4, CTX]), ACT.Copy).then_inc(rep, 1)

                def square(n):
                    act.wait_ge(centred, n + 1)
                    nc.scalar.activation(sq[:, n % 2, :], cen[:, n % 2, :], ACT.Square).then_inc(squared, 1)
                    act.wait_ge(var_ready, n + 1)
                    if n >= 2:
                        act.wait_ge(normed, n - 1)
                    nc.scalar.activation(rstd[:, n % 2, :], ps[:, 1, :], ACT.Ln, bias=eps).then_inc(log_ready, 1)
                    act.wait_ge(log_ready, n + 1)
                    nc.scalar.activation(rstd[:, n % 2, :], rstd[:, n % 2, :], ACT.Exp, scale=-0.5)\
                        .then_inc(rstd_ready, 1)

                def query(b):
                    act.wait_ge(q_ready, b + 1)
                    nc.scalar.activation(qT[:, b % 2, :], ps[:, 2, :], ACT.Copy).then_inc(q_copied, 1)

                def exps(t):
                    act.wait_ge(d_done, t + 1)
                    nc.scalar.activation(ex[:, t % 2], dif[:, t % 2], ACT.Exp, scale=float(DK) ** -0.5)\
                        .then_inc(e_done, 1)

                def turned(t):
                    b, i = t // TILES, t % TILES
                    act.wait_ge(pt_ready, t + 1)
                    if i == 0 and b >= 1:
                        act.wait_ge(o_ready, b)
                    nc.scalar.activation(pT[:, :, i * P:(i + 1) * P],
                                         ps[:, 5 + t % 2, :].rearrange("p (g q) -> p g q", g=GROUPS), ACT.Copy)\
                        .then_inc(pt_done, 1)

                square(0)
                query(0)
                for b in range(BATCH):
                    if b + 1 < BATCH:
                        square(b + 1)
                    for i in range(TILES):
                        exps(b * TILES + i)
                        if i >= 1:
                            turned(b * TILES + i - 1)
                    turned(b * TILES + TILES - 1)
                    if b + 1 < BATCH:
                        query(b + 1)
                    act.wait_ge(o_ready, b + 1)
                    nc.scalar.activation(oT[:, :], ps[:, 7, :], ACT.Copy).then_inc(o_done, 1)
                for b in range(BATCH):
                    square(BATCH + b)

            @block.gpsimd
            def _(pool):
                for t in range(BATCH * TILES):
                    pool.wait_ge(i_done, t + 1)
                    if t >= 2:
                        pool.wait_ge(pt_ready, t - 1)
                    nc.gpsimd.tensor_tensor(prob[:, t % 2, :].rearrange("p (h c) -> p h c", h=HEADS), ex[:, t % 2],
                                            inv[:, t % 2, :, None].broadcast_to([P, HEADS, CTX]), ALU.mult)\
                        .then_inc(p_done, 1)

            @block.vector
            def _(dve):
                dve.wait_ge(kv_ready, 1)
                nc.vector.tensor_copy(kT[:, :, :], ps[:, 3, 0:P].rearrange("p (b c) -> p b c", b=BATCH))\
                    .then_inc(kt_done, 1)
                dve.wait_ge(kt_done, 1)
                for b in range(BATCH):
                    nc.vector.tensor_tensor(kb[:, b], kT[:, b, None, :].broadcast_to([P, HEADS, CTX]),
                                            const("kmask")[:, :, None].broadcast_to([P, HEADS, CTX]), ALU.mult)\
                        .then_inc(kb_done, 1)
                    for g in range(GROUPS):
                        nc.vector.tensor_tensor(
                            vb[:, b, g, :].rearrange("p (h d) -> p h d", h=HEADS),
                            ps[:, 4, b * P:(b + 1) * P].rearrange("p (h d) -> p h d", h=HEADS),
                            const("vmask")[:, g * HEADS:(g + 1) * HEADS, None].broadcast_to([P, HEADS, DK]),
                            ALU.mult).then_inc(vb_done, 1)

                def norm(n, b, dst):
                    dve.wait_ge(mean_ready, n + 1)
                    if n >= 2:
                        dve.wait_ge(normed, n - 1)
                        dve.wait_ge(var_ready, n - 1)
                    nc.vector.tensor_tensor(cen[:, n % 2, :], xT[:, b, PAD:], ps[:, 0, :], ALU.subtract)\
                        .then_inc(centred, 1)
                    dve.wait_ge(rstd_ready, n + 1)
                    if 2 <= n < BATCH:
                        dve.wait_ge(q_ready, n - 1)
                    if dst is not xn:
                        dve.wait_ge(kept, b + 1)
                    nc.vector.tensor_tensor(xn[:, n % 2, :] if dst is xn else xT[:, b, PAD:], cen[:, n % 2, :],
                                            rstd[:, n % 2, :], ALU.mult).then_inc(normed, 1)

                def softmax(t):
                    dve.wait_ge(s_ready, t + 1)
                    sv = ps[:, 3 + t % 2, :].rearrange("p (h c) -> p h c", h=HEADS)
                    if t >= 2:
                        dve.wait_ge(d_done, t - 1)
                    nc.vector.tensor_reduce(mx[:, t % 2, :], sv, AX.X, ALU.max).then_inc(m_done, 1)
                    dve.wait_ge(m_done, t + 1)
                    if t >= 2:
                        dve.wait_ge(e_done, t - 1)
                    nc.vector.tensor_tensor(dif[:, t % 2], sv, mx[:, t % 2, :, None].broadcast_to([P, HEADS, CTX]),
                                            ALU.subtract).then_inc(d_done, 1)

                def sums(t):
                    dve.wait_ge(e_done, t + 1)
                    if t >= 2:
                        dve.wait_ge(i_done, t - 1)
                    nc.vector.tensor_reduce(total[:, t % 2, :], ex[:, t % 2], AX.X, ALU.add).then_inc(t_done, 1)
                    dve.wait_ge(t_done, t + 1)
                    if t >= 2:
                        dve.wait_ge(p_done, t - 1)
                    nc.vector.reciprocal(inv[:, t % 2, :], total[:, t % 2, :]).then_inc(i_done, 1)

                norm(0, 0, xn)
                for b in range(BATCH):
                    if b + 1 < BATCH:
                        norm(b + 1, b + 1, xn)
                    for i in range(TILES):
                        softmax(b * TILES + i)
                        sums(b * TILES + i)
                    dve.wait_ge(y_ready, b + 1)
                    nc.vector.tensor_tensor(xT[:, b, PAD:], xT[:, b, PAD:], ps[:, 7, :], ALU.add).then_inc(added, 1)
                    dve.wait_ge(added, b + 1)
                    nc.vector.tensor_copy(x2T[:, b, :], xT[:, b, PAD:]).then_inc(kept, 1)
                for b in range(BATCH):
                    norm(BATCH + b, b, xT)


def finish(env, out):
    nc, sem, ps, ident = (env[k] for k in ("nc", "sem", "ps", "ident"))
    xT, x2T = env["xT"], env["x2T"]
    with ExitStack() as st:
        sb = env["sb_in"](st)
        tok = sb("tok", [P, BATCH, TILES, DIM])
        summed, turned, copied = sem("f_summed"), sem("f_turned"), sem("f_copied")
        stored = [sem(f"f_stored{b}") for b in range(BATCH)]

        with nc.Block() as block:
            @block.vector
            def _(dve):
                for b in range(BATCH):
                    nc.vector.tensor_tensor(x2T[:, b, :], x2T[:, b, :], xT[:, b, PAD:], ALU.add).then_inc(summed, 1)

            @block.tensor
            def _(pe):
                for b in range(BATCH):
                    pe.wait_ge(summed, b + 1)
                    for i in range(TILES):
                        m = nc.tensor.transpose(ps[:, b, i * P:(i + 1) * P], x2T[:, b, i * P:(i + 1) * P], ident)
                    m.then_inc(turned, 1)

            @block.scalar
            def _(act):
                for b in range(BATCH):
                    act.wait_ge(turned, b + 1)
                    nc.scalar.activation(tok[:, b], ps[:, b, :].rearrange("p (i d) -> p i d", i=TILES), ACT.Copy)\
                        .then_inc(copied, 1)

            @block.sync
            def _(sp):
                for b in range(BATCH):
                    sp.wait_ge(copied, b + 1)
                    sp.dma_start(out[b].rearrange("(i p) d -> p i d", p=P), tok[:, b]).then_inc(stored[b], 16)
                for b in range(BATCH):
                    sp.wait_ge(stored[b], 16)


def layers(env, wqkv, qk_scales, wo, w1, w2, vecs):
    nc, sem, ps, const, ident, mean_w = (env[k] for k in ("nc", "sem", "ps", "const", "ident", "mean_w"))
    xT, xsT, eps = env["xT"], env["xsT"], env["eps"]
    NT = BATCH * TILES
    with ExitStack() as st:
        sb = env["sb_in"](st)
        wqkv_sb = sb("l_wqkv", [P, 3 * INNER])
        wqkv_next = sb("l_wqkv_next", [P, 3 * INNER])
        wo_sb = sb("l_wo", [P, PAIRS, P])
        w1_sb = sb("l_w1", [P, 2 * HIDDEN])
        w2_sb = sb("l_w2", [P, len(HC), P])
        vec = sb("l_vec", [P, N_VEC])
        scales = sb("l_scales", [P, 2, DH])
        tab_c = sb("l_tab_c", [P, 2, TILES, DH])
        tab_s = sb("l_tab_s", [P, 2, TILES, DH])
        mask = sb("l_mask", [P, BANK], BF16)
        mask_sel = sb("l_mask_sel", [P, 2, P], BF16)
        sq = sb("l_sq", [P, 2, HEADS, DH])
        norms = sb("l_norms", [P, 2, 2, HEADS])
        qn = sb("l_qn", [P, 2, HEADS, DH])
        rot = sb("l_rot", [P, 2, HEADS, DH])
        rot_s = sb("l_rot_s", [P, 2, HEADS, DH])
        qT = sb("l_qT", [P, PAIRS, P])
        kb = sb("l_kb", [P, 2, PAIRS, 2, WINDOW + P])
        vb = sb("l_vb", [P, P // WINDOW, PAIRS, 2, DH])
        mx = sb("l_mx", [P, 2, HEADS])
        dif = sb("l_dif", [P, HEADS, 2 * WINDOW])
        prob = sb("l_prob", [P, 2, HEADS, 2 * WINDOW])
        total = sb("l_total", [P, 2, HEADS])
        inv = sb("l_inv", [P, 2, HEADS])
        pT = sb("l_pT", [P, PAIRS, P])
        o_tok = sb("l_o_tok", [P, HEADS, DH])
        oT = sb("l_oT", [P, PAIRS, SEQ])
        xf = sb("l_xf", [P, SEQ])
        cen = sb("l_cen", [P, SEQ])
        fsq = sb("l_fsq", [P, SEQ])
        rstd = sb("l_rstd", [P, SEQ])
        xg = sb("l_xg", [P, SEQ])
        gel = sb("l_gel", [P, len(HC), SEQ])
        hid = sb("l_hid", [P, len(HC), SEQ])
        ln256 = sb("l_ln256", [P, 1])

        first_ld, consts_set = sem("l_first_loaded"), sem("l_consts_set")
        wo_ld, w1_ld, w2_ld, vec_ld = (sem("l_" + n) for n in ("wo_loaded", "w1_loaded", "w2_loaded", "vec_loaded"))
        next_ld, next_scales = sem("l_next_wqkv_loaded"), sem("l_next_scales_loaded")
        wqkv_moved = sem("l_wqkv_moved")
        xs_lo, xs_hi = sem("l_xs_low_half"), sem("l_xs_high_half")
        cos_ready, sin_ready = sem("l_cosines_ready"), sem("l_sines_ready")
        squared, summed, bounded = sem("l_squared"), sem("l_squares_summed"), sem("l_squares_bounded")
        logged, norm_ready = sem("l_norm_logged"), sem("l_norm_ready")
        sined, cosed, rotated, carried = (sem("l_" + n) for n in ("sined", "cosed", "rotated", "carried"))
        slot_full = [sem(f"l_slot{i}_full") for i in range(4)]
        slot_free = [sem(f"l_slot{i}_free") for i in range(4)]
        maxed, exped, sum_ready, inv_ready = (sem("l_" + n) for n in ("maxed", "exped", "sum_ready", "inv_ready"))
        xf_ready, fsquared, rstd_ready, xn_ready, xg_ready, gelu_ready = (
            sem("l_" + n) for n in ("ffn_x_ready", "ffn_squared", "rstd_ready", "xn_ready", "xg_ready", "gelu_ready"))
        body_sems = range(wo_ld.num, gelu_ready.num + 1)

        HEAD = 6
        STEPS = NT + HEAD

        def batch_at(t, first):
            return (t - first) // TILES if t >= first and (t - first) % TILES == 0 and t - first < NT else None

        def pieces(t):
            return [batch_at(t, first) for first in (6, 7, 8, 9)]

        def plan_turns(steps, tiles):
            turns, taken = {}, [0] * 4

            def plan(key, n):
                turns[key] = n, taken[n]
                taken[n] += 1

            for t in steps:
                b_wo, b_norm, b_hid, b_y = pieces(t)
                if t < tiles:
                    plan(("k", t), 1)
                if 0 <= t - 1 < tiles:
                    plan(("kT", t - 1), 3)
                    plan(("qT", t - 1), 2)
                if t < tiles:
                    plan(("q", t), 0)
                if 0 <= t - 2 < tiles:
                    plan(("pT", t - 2), 2)
                if 0 <= t - 1 < tiles:
                    plan(("s", t - 1), 3)
                if 0 <= t - 2 < tiles:
                    plan(("o", t - 2), 2)
                for key, b in ((("wo", b_wo), b_wo), (("mean", b_norm), b_norm), (("h", b_hid, 0), b_hid)):
                    if b is not None:
                        plan(key, 1)
                if 0 <= t - 1 < tiles:
                    plan(("v", t - 1, 0), 0)
                    plan(("v", t - 1, 1), 3)
                if b_y is not None:
                    plan(("y", b_y), 1)
                if b_hid is not None:
                    plan(("h", b_hid, 1), 1)
                    plan(("h", b_hid, 2), 0)
                if b_norm is not None:
                    plan(("var", b_norm), 0)
                if 0 <= t - 2 < tiles:
                    plan(("oT", t - 2), 2)
            return turns

        with nc.Block() as block:
            @block.sync
            def _(sp):
                sp.dma_start(wqkv_sb[:, :], wqkv[0]).then_inc(first_ld, 16)
                sp.dma_start(scales[:, :, :], qk_scales[0:1].broadcast_to([P, 2, DH])).then_inc(first_ld, 16)
                sp.wait_ge(first_ld, 32)

            @block.gpsimd
            def _(pool):
                pool.memset(ln256[:, :], QK_SCALE * 0.6931471805599453).then_inc(consts_set, 1)
                pool.memset(xsT[:, :, 0:1], 0.0).then_inc(consts_set, 1)
                pool.memset(kb[:, :, :, :, :], 0.0).then_inc(consts_set, 1)
                pool.memset(vb[:, :, :, :, :], 0.0).then_inc(consts_set, 1)

            @block.vector
            def _(dve):
                nc.vector.memset(mask[2 * WINDOW:, :], 0.0).then_inc(consts_set, 1)
                nc.vector.memset(mask_sel[2 * WINDOW:, :, :], 0.0).then_inc(consts_set, 1)
                nc.vector.tensor_copy(mask[0:2 * WINDOW, :], const("wmask")[0:2 * WINDOW, :]).then_inc(consts_set, 1)
                nc.vector.tensor_copy(mask_sel[0:2 * WINDOW, :, :],
                                      const("wsel")[0:2 * WINDOW, :].rearrange("p (a q) -> p a q", a=2))\
                    .then_inc(consts_set, 1)

        def segment(layer, steps, tiles):
            first = steps[0]
            turns = plan_turns(steps, tiles)
            before = {s.num: n for n, group in (
                (2 * first, (squared, summed, bounded, logged, norm_ready, cosed, sined, rotated)),
                (max(first - 1, 0), (carried, maxed, exped)),
                (max(first - 2, 0), (sum_ready, inv_ready)),
                (2 if first else 0, (xs_lo, xs_hi))) for s in group}
            more = tiles > NT and first > 0

            def slot(*key):
                n = turns[key][0]
                return ps[:, 2 * n:2 * n + 2, :]

            def filled(key):
                return slot_full[turns[key][0]]

            def read(key):
                return slot_free[turns[key][0]]

            def wait(engine, semaphore, count):
                if count > before[semaphore.num]:
                    engine.wait_ge(semaphore, count - before[semaphore.num])

            def wait_full(engine, *key):
                if key in turns:
                    n, turn = turns[key]
                    engine.wait_ge(slot_full[n], turn + 1)

            def wait_free(engine, *key):
                if key in turns:
                    n, turn = turns[key]
                    engine.wait_ge(slot_free[n], turn + 1)

            def take(pe, *key):
                n, turn = turns[key]
                if turn >= 1:
                    pe.wait_ge(slot_free[n], turn)

            with nc.Block() as block:
                @block.sync
                def _(sp):
                    if first > 0:
                        sp.dma_start(wo_sb[:, :, :], wo[layer].rearrange("(c p) n -> p c n", p=P)).then_inc(wo_ld, 16)
                        sp.dma_start(vec[:, :], vecs[layer]).then_inc(vec_ld, 16)
                        sp.dma_start(w1_sb[:, :], w1[layer]).then_inc(w1_ld, 16)
                        sp.dma_start(w2_sb[:, :, :], w2[layer].rearrange("(c p) n -> p c n", p=P))\
                            .then_inc(w2_ld, 16)
                    if more:
                        sp.dma_start(wqkv_next[:, :], wqkv[layer + 1]).then_inc(next_ld, 16)
                        sp.dma_start(scales[:, :, :], qk_scales[layer + 1][None].broadcast_to([P, 2, DH]))\
                            .then_inc(next_scales, 16)

                @block.gpsimd
                def _(pool):
                    def cosine_table():
                        if more:
                            pool.wait_ge(next_scales, 16)
                            wait(pool, cosed, 2 * NT)
                        nc.gpsimd.tensor_tensor(tab_c[:, :, :, :],
                                                const("ropeC").rearrange("p (a i d) -> p a i d", a=2, i=TILES),
                                                scales[:, :, None, :].broadcast_to([P, 2, TILES, DH]), ALU.mult)\
                            .then_inc(cos_ready, 1)
                        pool.wait_ge(cos_ready, 1)

                    def carry(t):
                        wait_free(pool, "kT", t - 1)
                        wait_full(pool, "s", t - 2)
                        nc.gpsimd.tensor_copy(kb[:, t % 2, :, :, 0:WINDOW],
                                              kb[:, (t - 1) % 2, :, :, P:P + WINDOW]).then_inc(carried, 1)

                    def rotate(t, r):
                        n, name, part = 1 - r, ("k", "q")[r], 2 * t + r
                        wait_free(pool, name, t)
                        wait_full(pool, name + "T", t - 1)
                        nc.gpsimd.tensor_tensor(rot[:, n], qn[:, n],
                                                tab_c[:, n, t % TILES, None, :].broadcast_to([P, HEADS, DH]),
                                                ALU.mult).then_inc(cosed, 1)
                        wait(pool, cosed, part + 1)
                        wait(pool, sined, part + 1)
                        nc.gpsimd.tensor_tensor(rot[:, n], rot[:, n], rot_s[:, n], ALU.add).then_inc(rotated, 1)

                    for t in steps:
                        if t < tiles:
                            if t >= 1:
                                carry(t)
                            if t % NT == 0:
                                cosine_table()
                            rotate(t, 0)
                            rotate(t, 1)

                @block.tensor
                def _(pe):
                    def project(name, t):
                        b, i = t // TILES % BATCH, t % TILES
                        if i == 0:
                            wait(pe, xs_lo, t // TILES + 1)
                            wait(pe, xs_hi, t // TILES + 1)
                        if t == NT:
                            pe.wait_ge(wqkv_moved, 1)
                        take(pe, name, t)
                        for c in range(2):
                            a = "qk".index(name) * INNER + c * BANK
                            m = nc.tensor.matmul(slot(name, t)[:, c, :], xsT[:, b, PAD + i * P:PAD + (i + 1) * P],
                                                 wqkv_sb[:, a:a + BANK], start=True, stop=True)
                        m.then_inc(filled((name, t)), 1)

                    def turn(name, t):
                        wait(pe, rotated, 2 * t + (1 if name == "k" else 2))
                        take(pe, name + "T", t)
                        dst = slot(name + "T", t)
                        for c in range(PAIRS):
                            m = nc.tensor.transpose(dst[:, c // 4, (c % 4) * P:(c % 4 + 1) * P],
                                                    rot[:, "qk".index(name), 2 * c:2 * c + 2, :], ident)
                        m.then_inc(filled((name + "T", t)), 1)

                    def scores(t):
                        wait_free(pe, "qT", t)
                        wait_free(pe, "kT", t)
                        wait(pe, carried, t)
                        take(pe, "s", t)
                        dst = slot("s", t)
                        opening = int(t % TILES == 0)
                        for n in range(2):
                            nc.tensor.matmul(dst[:, n, :], mask_sel[:, opening, :], mask[:, :], start=True, stop=False,
                                             skip_group_check=True)
                        for c in range(PAIRS):
                            for j in range(P // WINDOW):
                                a = j * WINDOW
                                m = nc.tensor.matmul(dst[a:a + WINDOW, c // 4, (c % 4) * P:(c % 4 + 1) * P],
                                                     qT[:, c, a:a + WINDOW], kb[:, t % 2, c, :, a:a + 2 * WINDOW],
                                                     start=False, stop=True, skip_group_check=True)
                        m.then_inc(filled(("s", t)), 1)

                    def turn_probs(t):
                        wait(pe, exped, t + 1)
                        take(pe, "pT", t)
                        dst = slot("pT", t)
                        for c in range(PAIRS):
                            m = nc.tensor.transpose(dst[:, c // 4, (c % 4) * P:(c % 4 + 1) * P],
                                                    prob[:, t % 2, 2 * c:2 * c + 2, :], ident)
                        m.then_inc(filled(("pT", t)), 1)

                    def values(t):
                        wait_free(pe, "pT", t)
                        wait_free(pe, "v", t, 0)
                        wait_free(pe, "v", t, 1)
                        take(pe, "o", t)
                        dst = slot("o", t)
                        for c in range(PAIRS):
                            for j in range(P // WINDOW):
                                a = j * WINDOW
                                m = nc.tensor.matmul(dst[a:a + WINDOW, c // 4, (c % 4) * P:(c % 4 + 1) * P],
                                                     pT[:, c, a:a + WINDOW], vb[:, j, c, :, :],
                                                     start=True, stop=True, skip_group_check=True)
                        m.then_inc(filled(("o", t)), 1)

                    def turn_out(t):
                        wait_free(pe, "o", t)
                        take(pe, "oT", t)
                        dst = slot("oT", t)
                        for c in range(PAIRS):
                            m = nc.tensor.transpose(dst[:, c // 4, (c % 4) * P:(c % 4 + 1) * P],
                                                    o_tok[:, 2 * c:2 * c + 2, :], ident)
                        m.then_inc(filled(("oT", t)), 1)

                    def project_v(t, half):
                        b, i = t // TILES % BATCH, t % TILES
                        wv = wqkv_sb[:, 2 * INNER:].rearrange("p (c a d) -> p a c d", a=2, d=DH)
                        if t == NT and half == 0:
                            pe.wait_ge(wqkv_moved, 2)
                        take(pe, "v", t, half)
                        dst = slot("v", t, half)
                        for n in range(2):
                            a = i * P + (2 * half + n) * WINDOW
                            for parity in range(2):
                                m = nc.tensor.matmul(dst[64 * parity:64 * parity + 64, n, :],
                                                     xsT[:, b, a:a + 2 * WINDOW], wv[:, parity],
                                                     start=True, stop=True, skip_group_check=True)
                        m.then_inc(filled(("v", t, half)), 1)

                    def project_out(b):
                        if b == 0:
                            pe.wait_ge(wo_ld, 16)
                        wait_free(pe, "oT", (b + 1) * TILES - 1)
                        take(pe, "wo", b)
                        for c in range(PAIRS):
                            m = nc.tensor.matmul(slot("wo", b)[:, 0, :], wo_sb[:, c, :], oT[:, c, :],
                                                 start=(c == 0), stop=(c == PAIRS - 1))
                        m.then_inc(filled(("wo", b)), 1)

                    def moment(name, src, ready, b):
                        pe.wait_ge(ready, b + 1)
                        take(pe, name, b)
                        nc.tensor.matmul(slot(name, b)[:, 0, :], mean_w, src[:, :], start=True, stop=True)\
                            .then_inc(filled((name, b)), 1)

                    def hidden(b, c):
                        a, n = HC[c]
                        pe.wait_ge(xg_ready, b + 1)
                        if b == 0 and c == 0:
                            pe.wait_ge(w1_ld, 16)
                        take(pe, "h", b, c)
                        for s in range(2):
                            w = w1_sb[:, s * HIDDEN + a:s * HIDDEN + a + n]
                            m = nc.tensor.matmul(slot("h", b, c)[0:n, s, :], w, xg[:, :], start=True, stop=True)
                        m.then_inc(filled(("h", b, c)), 1)

                    def project_ffn(b):
                        for c in range(len(HC)):
                            wait_free(pe, "h", b, c)
                        if b == 0:
                            pe.wait_ge(w2_ld, 16)
                        take(pe, "y", b)
                        for c, (a, n) in enumerate(HC):
                            m = nc.tensor.matmul(slot("y", b)[:, 0, :], w2_sb[0:n, c, :], hid[0:n, c, :],
                                                 start=(c == 0), stop=(c == len(HC) - 1))
                        m.then_inc(filled(("y", b)), 1)

                    for t in steps:
                        b_wo, b_norm, b_hid, b_y = pieces(t)
                        if t < tiles:
                            project("k", t)
                        if 0 <= t - 1 < tiles:
                            turn("k", t - 1)
                            turn("q", t - 1)
                        if t < tiles:
                            project("q", t)
                        if 0 <= t - 2 < tiles:
                            turn_probs(t - 2)
                        if 0 <= t - 1 < tiles:
                            scores(t - 1)
                        if 0 <= t - 2 < tiles:
                            values(t - 2)
                        if b_wo is not None:
                            project_out(b_wo)
                        if b_norm is not None:
                            moment("mean", xf, xf_ready, b_norm)
                        if b_hid is not None:
                            hidden(b_hid, 0)
                        if 0 <= t - 1 < tiles:
                            project_v(t - 1, 0)
                            project_v(t - 1, 1)
                        if b_y is not None:
                            project_ffn(b_y)
                        if b_hid is not None:
                            hidden(b_hid, 1)
                            hidden(b_hid, 2)
                        if b_norm is not None:
                            moment("var", fsq, fsquared, b_norm)
                        if 0 <= t - 2 < tiles:
                            turn_out(t - 2)

                @block.scalar
                def _(act):
                    if first == 0:
                        nc.scalar.preload_act_table_set(LN_EXP)

                    def copy_slot(key, dst, src=None):
                        wait_full(act, *key)
                        nc.scalar.activation(dst, slot(*key) if src is None else src, ACT.Copy)\
                            .then_inc(read(key), 1)

                    def square(t, r):
                        name, part = ("k", "q")[r], 2 * t + r
                        wait_full(act, name, t)
                        wait(act, summed, part - 1)
                        nc.scalar.activation(sq[:, 1 - r], slot(name, t).rearrange("p n (h d) -> p (n h) d", d=DH),
                                             ACT.Square).then_inc(squared, 1)

                    def inverse_norm(t, r):
                        part = 2 * t + r
                        wait(act, bounded, part + 1)
                        nc.scalar.activation(norms[:, t % 2, 1 - r], norms[:, t % 2, 1 - r], ACT.Ln, scale=65536.0)\
                            .then_inc(logged, 1)
                        wait(act, logged, part + 1)
                        nc.scalar.activation(norms[:, t % 2, 1 - r], norms[:, t % 2, 1 - r], ACT.Exp, scale=-0.5,
                                             bias=ln256[:, 0:1]).then_inc(norm_ready, 1)

                    def copy_q(t):
                        wait_full(act, "s", t - 1)
                        copy_slot(("qT", t), qT[:, :, :].rearrange("p (n c) q -> p n (c q)", n=2))

                    def copy_k(t, parity):
                        wait_full(act, "kT", t)
                        wait_full(act, "s", t - 2)
                        wait(act, carried, t - 1)
                        src = slot("kT", t).rearrange("p n (c q) -> p (n c) q", q=P)
                        rows = slice(64 * parity, 64 * parity + 64)
                        m = nc.scalar.activation(kb[rows, t % 2, :, parity, WINDOW:], src[rows, :, :], ACT.Copy)
                        if parity == 1:
                            m.then_inc(read(("kT", t)), 1)

                    def exps(t):
                        wait_free(act, "s", t)
                        wait_full(act, "pT", t - 2)
                        wait(act, sum_ready, t - 1)
                        nc.scalar.activation(prob[:, t % 2], dif[:, :, :], ACT.Exp, scale=QK_SCALE).then_inc(exped, 1)

                    def copy_probs(t):
                        wait_full(act, "o", t - 1)
                        copy_slot(("pT", t), pT[:, :, :].rearrange("p (n c) q -> p n (c q)", n=2))

                    def copy_v(t, half):
                        wait_full(act, "v", t, half)
                        wait_full(act, "o", t - 1)
                        for parity in range(2):
                            r = slice(64 * parity, 64 * parity + 64)
                            m = nc.scalar.activation(vb[r, 2 * half:2 * half + 2, :, parity, :],
                                                     slot("v", t, half)[r].rearrange("p n (c d) -> p n c d", d=DH),
                                                     ACT.Copy)
                        m.then_inc(read(("v", t, half)), 1)

                    def copy_out(t):
                        i = t % TILES
                        wait_full(act, "oT", t)
                        if i == 0:
                            wait_full(act, "wo", t // TILES - 1)
                        nc.scalar.activation(oT[:, :, i * P:(i + 1) * P],
                                             slot("oT", t).rearrange("p n (c q) -> p (n c) q", q=P), ACT.Copy)\
                            .then_inc(read(("oT", t)), 1)

                    def gelu(b, c):
                        n = HC[c][1]
                        wait_full(act, "h", b, c)
                        if b == 0 and c == 0:
                            act.wait_ge(vec_ld, 16)
                        if b >= 1 and c == 0:
                            for k in range(len(HC)):
                                wait_free(act, "h", b - 1, k)
                        nc.scalar.activation(gel[0:n, c, :], slot("h", b, c)[0:n, 1, :], ACT.Gelu,
                                             bias=vec[0:n, V_B1 + 3 + c:V_B1 + 4 + c]).then_inc(gelu_ready, 1)

                    def shift_low(batch):
                        b = batch % BATCH
                        wait_free(act, "y", batch - BATCH)
                        wait_full(act, "q", (batch - BATCH) * TILES + TILES - 1)
                        for half in range(2):
                            wait_full(act, "v", (batch - BATCH) * TILES + TILES - 1, half)
                        nc.scalar.activation(xsT[0:64, b, 1:], xT[0:64, b, 1:], ACT.Copy).then_inc(xs_lo, 1)

                    if first == 0:
                        shift_low(0)
                    for t in steps:
                        b_wo, b_norm, b_hid, _ = pieces(t)
                        if t < tiles:
                            square(t, 0)
                        if 0 <= t - 1 < tiles:
                            copy_k(t - 1, 0)
                            copy_q(t - 1)
                        if t < tiles:
                            inverse_norm(t, 0)
                        if 0 <= t - 1 < tiles:
                            copy_k(t - 1, 1)
                        if t < tiles:
                            square(t, 1)
                        if 0 <= t - 2 < tiles:
                            copy_probs(t - 2)
                        if t < tiles:
                            inverse_norm(t, 1)
                        if 0 <= t - 1 < tiles:
                            exps(t - 1)
                        if b_hid is not None:
                            gelu(b_hid, 0)
                        if 0 <= t - 1 < tiles:
                            copy_v(t - 1, 0)
                        if b_norm is not None:
                            wait_free(act, "mean", b_norm)
                            nc.scalar.activation(fsq[:, :], cen[:, :], ACT.Square).then_inc(fsquared, 1)
                        if b_hid is not None:
                            gelu(b_hid, 1)
                        if 0 <= t - 1 < tiles:
                            copy_v(t - 1, 1)
                        if b_hid is not None:
                            gelu(b_hid, 2)
                            nc.scalar.preload_act_table_set(LN_EXP)
                        if b_norm is not None:
                            wait_full(act, "var", b_norm)
                            nc.scalar.activation(rstd[:, :], slot("var", b_norm)[:, 0, :], ACT.Ln, bias=eps)\
                                .then_inc(read(("var", b_norm)), 1)
                            wait_free(act, "var", b_norm)
                            nc.scalar.activation(rstd[:, :], rstd[:, :], ACT.Exp, scale=-0.5).then_inc(rstd_ready, 1)
                        if 0 <= t - 2 < tiles:
                            copy_out(t - 2)
                        if b_wo is not None:
                            wait_free(act, "wo", b_wo)
                            if b_wo >= 1:
                                wait_free(act, "mean", b_wo - 1)
                            nc.scalar.activation(xf[0:64, :], xT[0:64, b_wo, PAD:], ACT.Copy)
                            nc.scalar.activation(xf[64:P, :], xT[64:P, b_wo, PAD - 1:PAD + SEQ - 1], ACT.Copy)\
                                .then_inc(xf_ready, 1)
                        if t % TILES == TILES - 2 and t + 2 < tiles:
                            shift_low(t // TILES + 1)

                @block.vector
                def _(dve):
                    def sum_squares(t, r):
                        part, half = 2 * t + r, norms[:, t % 2, 1 - r]
                        wait(dve, squared, part + 1)
                        wait_free(dve, ("k", "q")[r], t - 2)
                        nc.vector.tensor_reduce(half, sq[:, 1 - r], AX.X, ALU.add).then_inc(summed, 1)
                        wait(dve, summed, part + 1)
                        nc.vector.tensor_scalar(half, half, 1e-24, None, ALU.max).then_inc(bounded, 1)

                    def normalise(t, r):
                        name, part = ("k", "q")[r], 2 * t + r
                        wait(dve, norm_ready, part + 1)
                        wait(dve, cosed, part - 1)
                        wait(dve, sined, part - 1)
                        nc.vector.tensor_tensor(qn[:, 1 - r],
                                                slot(name, t).rearrange("p n (h d) -> p (n h) d", d=DH),
                                                norms[:, t % 2, 1 - r, :, None].broadcast_to([P, HEADS, DH]),
                                                ALU.mult).then_inc(read((name, t)), 1)

                    def sine_part(t, r):
                        i, H2, part = t % TILES, DH // 2, 2 * t + r
                        wait_free(dve, ("k", "q")[r], t)
                        wait(dve, rotated, part - 1)
                        if t % NT == 0 and r == 0:
                            dve.wait_ge(sin_ready, 2)
                        for a in (0, H2):
                            m = nc.vector.tensor_tensor(rot_s[:, 1 - r, :, a:a + H2], qn[:, 1 - r, :, H2 - a:DH - a],
                                                        tab_s[:, 1 - r, i, None, a:a + H2]
                                                        .broadcast_to([P, HEADS, H2]), ALU.mult)
                        m.then_inc(sined, 1)

                    def shift_scores(t):
                        s = slot("s", t).rearrange("p n (h k) -> p (n h) k", k=2 * WINDOW)
                        wait_full(dve, "s", t)
                        nc.vector.tensor_reduce(mx[:, t % 2, :], s, AX.X, ALU.max).then_inc(maxed, 1)
                        wait(dve, maxed, t + 1)
                        wait(dve, exped, t)
                        nc.vector.tensor_tensor(dif[:, :, :], s,
                                                mx[:, t % 2, :, None].broadcast_to([P, HEADS, 2 * WINDOW]),
                                                ALU.subtract).then_inc(read(("s", t)), 1)

                    def sums(t):
                        wait(dve, exped, t + 1)
                        nc.vector.tensor_reduce(total[:, t % 2, :], prob[:, t % 2], AX.X, ALU.add)\
                            .then_inc(sum_ready, 1)
                        wait(dve, sum_ready, t + 1)
                        wait_free(dve, "o", t - 2)
                        nc.vector.reciprocal(inv[:, t % 2, :], total[:, t % 2, :]).then_inc(inv_ready, 1)

                    def scale_out(t):
                        wait_full(dve, "o", t)
                        wait(dve, inv_ready, t + 1)
                        wait_full(dve, "oT", t - 1)
                        nc.vector.tensor_tensor(o_tok[:, :, :], slot("o", t).rearrange("p n (h d) -> p (n h) d", d=DH),
                                                inv[:, t % 2, :, None].broadcast_to([P, HEADS, DH]), ALU.mult)\
                            .then_inc(read(("o", t)), 1)

                    def gate(b, c):
                        n = HC[c][1]
                        dve.wait_ge(gelu_ready, len(HC) * b + c + 1)
                        wait_full(dve, "h", b, c)
                        if b >= 1 and c == 0:
                            wait_full(dve, "y", b - 1)
                        nc.vector.scalar_tensor_tensor(out=hid[0:n, c, :], in0=slot("h", b, c)[0:n, 0, :],
                                                       scalar=vec[0:n, V_B1 + c:V_B1 + c + 1],
                                                       in1=gel[0:n, c, :], op0=ALU.add, op1=ALU.mult)\
                            .then_inc(read(("h", b, c)), 1)

                    def shift_high(batch):
                        b = batch % BATCH
                        wait_free(dve, "y", batch - BATCH)
                        wait_full(dve, "q", (batch - BATCH) * TILES + TILES - 1)
                        for half in range(2):
                            wait_full(dve, "v", (batch - BATCH) * TILES + TILES - 1, half)
                        nc.vector.tensor_copy(xsT[64:P, b, 1:], xT[64:P, b, 0:PAD + SEQ - 1]).then_inc(xs_hi, 1)

                    def sine_table():
                        if more:
                            dve.wait_ge(next_scales, 16)
                            wait(dve, sined, 2 * NT)
                        rope_s = const("ropeS").rearrange("p (a i d) -> p a i d", a=2, i=TILES)
                        for a in (0, DH // 2):
                            o = DH // 2 - a
                            nc.vector.tensor_tensor(tab_s[:, :, :, a:a + DH // 2], rope_s[:, :, :, a:a + DH // 2],
                                                    scales[:, :, None, o:o + DH // 2]
                                                    .broadcast_to([P, 2, TILES, DH // 2]), ALU.mult)\
                                .then_inc(sin_ready, 1)

                    if first == 0:
                        shift_high(0)
                    for t in steps:
                        b_wo, b_norm, b_hid, b_y = pieces(t)
                        if 0 <= t - 2 < tiles:
                            sums(t - 2)
                        if t < tiles:
                            sum_squares(t, 0)
                        if b_hid is not None:
                            dve.wait_ge(rstd_ready, b_hid + 1)
                            if b_hid >= 1:
                                wait_full(dve, "h", b_hid - 1, len(HC) - 1)
                            nc.vector.tensor_tensor(xg[:, :], cen[:, :], rstd[:, :], ALU.mult).then_inc(xn_ready, 1)
                            dve.wait_ge(xn_ready, b_hid + 1)
                            if b_hid == 0:
                                dve.wait_ge(vec_ld, 16)
                            nc.vector.tensor_scalar(xg[:, :], xg[:, :], vec[:, V_G:V_G + 1], vec[:, V_B:V_B + 1],
                                                    ALU.mult, ALU.add).then_inc(xg_ready, 1)
                        if t % NT == 0 and t < tiles:
                            sine_table()
                        if t < tiles:
                            normalise(t, 0)
                            sine_part(t, 0)
                            sum_squares(t, 1)
                            normalise(t, 1)
                        if 0 <= t - 1 < tiles:
                            shift_scores(t - 1)
                        if t < tiles:
                            sine_part(t, 1)
                        if 0 <= t - 2 < tiles:
                            scale_out(t - 2)
                        if b_wo is not None:
                            wait_full(dve, "wo", b_wo)
                            nc.vector.tensor_tensor(xT[:, b_wo, PAD:], xT[:, b_wo, PAD:], slot("wo", b_wo)[:, 0, :],
                                                    ALU.add).then_inc(read(("wo", b_wo)), 1)
                        if b_norm is not None:
                            wait_full(dve, "mean", b_norm)
                            if b_norm >= 1:
                                wait_full(dve, "var", b_norm - 1)
                                dve.wait_ge(xn_ready, b_norm)
                            nc.vector.tensor_tensor(cen[:, :], xf[:, :], slot("mean", b_norm)[:, 0, :], ALU.subtract)\
                                .then_inc(read(("mean", b_norm)), 1)
                        if b_hid is not None:
                            for c in range(len(HC)):
                                gate(b_hid, c)
                        if b_y is not None:
                            wait_full(dve, "y", b_y)
                            nc.vector.scalar_tensor_tensor(out=xT[:, b_y, PAD:], in0=slot("y", b_y)[:, 0, :],
                                                           scalar=vec[:, V_B2:V_B2 + 1], in1=xT[:, b_y, PAD:],
                                                           op0=ALU.add, op1=ALU.add).then_inc(read(("y", b_y)), 1)
                        if t % TILES == TILES - 2 and t + 2 < tiles:
                            shift_high(t // TILES + 1)
                        if more and t == NT - 1:
                            dve.wait_ge(next_ld, 16)
                            wait_full(dve, "k", t)
                            wait_full(dve, "q", t)
                            nc.vector.tensor_copy(wqkv_sb[:, 0:2 * INNER], wqkv_next[:, 0:2 * INNER])\
                                .then_inc(wqkv_moved, 1)
                        if more and t == NT:
                            for half in range(2):
                                wait_full(dve, "v", t - 1, half)
                            nc.vector.tensor_copy(wqkv_sb[:, 2 * INNER:], wqkv_next[:, 2 * INNER:])\
                                .then_inc(wqkv_moved, 1)
            nc.all_engine_barrier(sems_to_clear=body_sems)

        segment(0, range(HEAD), STEPS)
        with nc.Fori(0, LAYERS - 1) as layer:
            segment(layer, range(HEAD, STEPS), STEPS)
        segment(LAYERS - 1, range(HEAD, STEPS), NT)


def shape_constants():
    import numpy as np
    c = np.zeros((P, N_CONST), np.float32)

    def put(name, a):
        at, n = CONST[name]
        c[:, at:at + n] = np.asarray(a, np.float32).reshape(P, n)

    f = np.float32
    put("ident", np.eye(P))
    put("mean", np.full((P, P), 1.0 / DIM))
    sums = np.zeros((P, P))
    for j in range(4):
        sums[32 * j + DK, 32 * j:32 * j + 32] = 1.0
    put("sums", sums)
    inv = f(1.0) / np.power(f(10000.0), (np.arange(0, DK, 2, dtype=f) / f(DK)), dtype=f)
    fr = np.arange(SEQ, dtype=f)[:, None] * inv[None, :]
    emb = np.concatenate([fr, fr], -1)
    sign = np.where(np.arange(DK) < DK // 2, -1.0, 1.0)
    put("cosT", np.tile(np.cos(emb).T, (HEADS, 1)))
    put("sinT", np.tile(np.sin(emb).T * sign[:, None], (HEADS, 1)))
    p = np.arange(P)
    put("kmask", (p[:, None] // DK) == np.arange(HEADS)[None, :])
    put("vmask", (4 * np.arange(GROUPS)[None, :, None] + (p // CTX)[:, None, None]) == np.arange(HEADS)[None, None, :])
    half = np.arange(0, DH, 2, dtype=f)
    inv = f(1.0) / np.power(f(10000.0), half / f(DH), dtype=f)
    t = np.arange(SEQ, dtype=f)
    fr = t[:, None] * inv[None, :]
    fr = np.concatenate([fr, fr], -1)
    base = (half + f(0.4 * DH)) / f(1.4 * DH)
    power = (t - SEQ // 2) / f(WINDOW // 2)
    sc = np.power(base[None, :], power[:, None], dtype=f)
    sc = np.concatenate([sc, sc], -1)
    sgn = np.where(np.arange(DH) < DH // 2, -1.0, 1.0).astype(f)
    for name, tab in (("ropeC", np.cos(fr)), ("ropeS", np.sin(fr) * sgn)):
        a = np.stack([tab * sc, tab * (f(1.0) / sc)])
        put(name, a.reshape(2, TILES, P, DH).transpose(2, 0, 1, 3))
    m = np.zeros((P, 8, 2 * WINDOW))
    key = np.arange(2 * WINDOW)
    for r in range(WINDOW):
        bad = (key < r) | (key > r + WINDOW)
        m[r] = np.where(bad, -1e30, 0.0)
        m[WINDOW + r] = np.where(bad | (key < WINDOW), -1e30, 0.0)
    put("wmask", m)
    s = np.zeros((P, 2, P))
    for q in range(P):
        s[q % WINDOW, 0, q] = 1.0
        s[q % WINDOW + (WINDOW if q < WINDOW else 0), 1, q] = 1.0
    put("wsel", s)
    return c


def kernel(x, ctx_512, L0_attn_Wq, L0_attn_Wk, L0_attn_Wv, L0_attn_Wo, L0_xattn_Wq, L0_xattn_Wkv, L0_xattn_Wo,
           L0_ffn_Wqkv, L0_ffn_q_scale, L0_ffn_k_scale, L0_ffn_Wo, L0_ffn_ln_g, L0_ffn_ln_b, L0_ffn_W1, L0_ffn_b1,
           L0_ffn_W2, L0_ffn_b2):
    import numpy as np
    import concourse.bacc as bacc
    from concourse.bass_utils import run_bass_kernel_spmd

    T = lambda a: np.ascontiguousarray(np.asarray(a).T)
    rot = np.arange(DIM).reshape(HEADS, DK)
    rot = np.concatenate([rot[:, 1::2], rot[:, ::2]], -1).reshape(-1)
    wq, wk, wv, wo_a = (T(a) for a in (L0_attn_Wq, L0_attn_Wk, L0_attn_Wv, L0_attn_Wo))
    w_attn = np.zeros((P, 9 * P), wq.dtype)
    for name, a in (("q", wq), ("k", wk), ("qr", wq[:, rot]), ("kr", wk[:, rot]), ("v", wv)):
        w_attn[:, W_ATTN[name]:W_ATTN[name] + P] = a
    for h in range(HEADS):
        at, r = W_ATTN["o0"] + (h // 4) * P, 32 * (h % 4)
        w_attn[r:r + DK, at:at + P] = wo_a[h * DK:(h + 1) * DK]
    vecs = np.zeros((LAYERS, P, N_VEC), np.asarray(x).dtype)
    b1 = np.asarray(L0_ffn_b1)
    for s in range(2):
        for c, (at, n) in enumerate(HC):
            vecs[:, :n, V_B1 + 3 * s + c] = b1[:, s * HIDDEN + at:s * HIDDEN + at + n]
    for col, a in ((V_G, L0_ffn_ln_g), (V_B, L0_ffn_ln_b), (V_B2, L0_ffn_b2)):
        vecs[:, :, col] = np.asarray(a)
    w2 = np.zeros((LAYERS, len(HC) * P, P), vecs.dtype)
    w2[:, :HIDDEN] = np.asarray(L0_ffn_W2)
    arrays = {
        "x": np.asarray(x).reshape(BATCH * SEQ, DIM),
        "ctxT": T(np.asarray(ctx_512).reshape(BATCH * CTX, LATENT)),
        "w_attn": w_attn,
        "w_xq": T(L0_xattn_Wq), "w_xkv": T(L0_xattn_Wkv), "w_xo": T(L0_xattn_Wo),
        "wqkv": np.asarray(L0_ffn_Wqkv),
        "qk_scales": np.stack([np.asarray(L0_ffn_q_scale), np.asarray(L0_ffn_k_scale)], 1),
        "wo": np.asarray(L0_ffn_Wo), "w1": np.asarray(L0_ffn_W1), "w2": w2, "vecs": vecs,
        "consts": shape_constants(),
    }
    nc = bacc.Bacc("TRN2", target_bir_lowering=False, num_devices=1)
    args = [nc.dram_tensor(n, a.shape, mybir.dt.from_np(a.dtype), kind="ExternalInput").ap() for n, a in arrays.items()]
    scratch = nc.dram_tensor("scratch", (BATCH, P, 3, 2, SEQ), BF16, kind="Internal").ap()
    max_scratch = nc.dram_tensor("max_scratch", (BATCH, P, P), BF16, kind="Internal").ap()
    out = nc.dram_tensor("out", (BATCH, SEQ, DIM), F32, kind="ExternalOutput").ap()
    decoder(nc, *args, scratch, max_scratch, out)
    r = run_bass_kernel_spmd(nc, [arrays], core_ids=[0])
    return r.results[0]["out"]
```

```python
from contextlib import ExitStack

import concourse.bass as bass
from concourse import mybir
from concourse.alu_op_type import AluOpType as ALU

ACT = mybir.ActivationFunctionType
AX = mybir.AxisListType
F32 = mybir.dt.float32
BF16 = mybir.dt.bfloat16

P = 128
BATCH, SEQ, DIM = 4, 512, 128
TILES = SEQ // P
HEADS = 16
DK = DIM // HEADS
PAIRS = HEADS // 2
GROUPS = HEADS // 4
CTX, LATENT = 32, 64
LAYERS = 6
DH = 64
INNER = HEADS * DH
WINDOW = 32
PAD = WINDOW
HIDDEN = int(DIM * 4 * 2 / 3)
HC = [(0, 128), (128, 128), (256, HIDDEN - 256)]
EPS = 1e-5
QK_SCALE = 8.0
LN_2 = 0.6931471805599453
LN_EXP = "natural_log_exp_and_others"
BANK = 512

Q_PARTS = [(0, 3, 0, True), (3, 2, 1, True), (5, 1, 2, True)]
K_PARTS = [(0, 3, 0, False), (3, 2, 0, False), (5, 1, 0, False)]
MAX_ROW = 6 * DK

CONST = {}
_at = 0
for _name, _n in (("ident", P), ("mean", P), ("sums", P), ("cosT", SEQ), ("sinT", SEQ),
                  ("kmask", HEADS), ("vmask", GROUPS * HEADS), ("ropeC", 2 * TILES * DH),
                  ("ropeS", 2 * TILES * DH), ("wmask", 8 * 2 * WINDOW), ("wsel", 2 * P)):
    CONST[_name] = (_at, _n)
    _at += _n
N_CONST = _at
W_ATTN = {n: i * P for i, n in enumerate(("q", "k", "qr", "kr", "v", "o0", "o1", "o2", "o3"))}
V_B1, V_G, V_B, V_B2, N_VEC = 0, 6, 7, 8, 9
RING = 8
WARM_UP = 5


def decoder(nc, x, ctxT, w_attn, w_xq, w_xkv, w_xo, wqkv, qk_scales, wo, w1, w2, vecs, consts, scratch, max_scratch,
            out):
    with ExitStack() as top:
        def sb_in(stack):
            return lambda name, shape, dt=F32: stack.enter_context(nc.sbuf_tensor(name, shape, dt))

        def sem(name):
            return top.enter_context(nc.semaphore(name))

        sb = sb_in(top)
        ps = top.enter_context(nc.psum_tensor("ps", [P, 8, BANK], F32))
        cst = sb("cst", [P, N_CONST])
        xT = sb("xT", [P, BATCH, PAD + SEQ])
        xsT = sb("xsT", [P, BATCH, PAD + SEQ])
        x2T = sb("x2T", [P, BATCH, SEQ])

        def const(name):
            a, n = CONST[name]
            return cst[:, a:a + n]

        ident, mean_w = const("ident"), const("mean")
        eps_tile = sb("eps", [P, 1])
        eps = eps_tile[:, 0:1]
        env = dict(eps=eps, nc=nc, sem=sem, ps=ps, const=const, ident=ident, mean_w=mean_w, xT=xT, xsT=xsT, x2T=x2T,
                   sb_in=sb_in)
        self_attention(env, x, w_attn, consts, cst, scratch, max_scratch)
        kept = dict(wqkv=sb("l_wqkv", [P, 3 * INNER]), scales=sb("l_scales", [P, 2, DH]),
                    kb=sb("l_kb", [P, 2, PAIRS, 2, WINDOW + P]), vb=sb("l_vb", [P, P // WINDOW, PAIRS, 2, DH]))
        cross_attention(env, ctxT, w_xq, w_xkv, w_xo, wqkv, qk_scales, kept)
        layers(env, kept, wqkv, qk_scales, wo, w1, w2, vecs)
        finish(env, out)


def self_attention(env, x, w_attn, consts, cst, scratch, max_scratch):
    nc = env["nc"]
    with ExitStack() as st:
        sb = env["sb_in"](st)
        wat = sb("wat", [P, 9 * P])
        stack = sb("stack", [P, BATCH, 2, PAIRS, SEQ], BF16)
        vaug = sb("vaug", [P, BATCH, TILES, HEADS, 32])
        more_outs = sb("outs", [P, BATCH - 2, GROUPS, SEQ])
        outs = [env["x2T"][:, :, :], env["xsT"][:, :, :].rearrange("p b n -> p (b n)")[:, 0:GROUPS * SEQ]
                .rearrange("p (g n) -> p g n", g=GROUPS)] + [more_outs[:, b] for b in range(BATCH - 2)]
        probs = sb("probs", [P, RING, SEQ])
        with ExitStack() as inner:
            project, laid = project_parts(env, inner, x, wat, w_attn, consts, cst, scratch, stack, vaug,
                                          probs)
            softmax = softmax_values(env, inner, stack, vaug, probs, outs, max_scratch, laid)

            with nc.Block() as block:
                @block.sync
                def _(sp):
                    project["sync"](sp)
                    softmax["sync"](sp)

                @block.gpsimd
                def _(pool):
                    project["gpsimd"](pool)
                    softmax["gpsimd"](pool)

                @block.tensor
                def _(pe):
                    project["tensor"](pe)
                    softmax["tensor"](pe)

                @block.scalar
                def _(act):
                    project["scalar"](act)
                    softmax["scalar"](act)

                @block.vector
                def _(dve):
                    project["vector"](dve)
                    softmax["vector"](dve)
        attention_out(env, wat, outs)


def project_parts(env, stack_of, x, wat, w_attn, consts, cst, scratch, stack, vaug, probs):
    nc, sem, ps, const, ident, mean_w = (env[k] for k in ("nc", "sem", "ps", "const", "ident", "mean_w"))
    xT, eps = env["xT"], env["eps"]
    sb = env["sb_in"](stack_of)
    xtok = probs[:, 0:BATCH, :].rearrange("p b (i d) -> p (b i) d", d=DIM)
    cen = sb("cen", [P, 2, SEQ])
    sq = sb("sq", [P, 2, SEQ])
    rstd = sb("rstd", [P, SEQ])
    xn = sb("xn", [P, 2, SEQ])
    rc = sb("rc", [P, 2, SEQ])
    rs = sb("rs", [P, 2, SEQ])
    parts = sb("parts", [P, 2, 3, 2, SEQ], BF16)
    minus1 = sb("minus1", [2, SEQ], BF16)
    c_ld, w_ld = sem("a_consts_loaded"), sem("a_weights_loaded")
    x_ld = [sem(f"a_x_loaded{b}") for b in range(BATCH)]
    pads, eps_set, log_ready = sem("a_pads_zeroed"), sem("a_eps_set"), sem("a_log_ready")
    vz, vo, stack_zeroed = sem("a_vaug_zeroed"), sem("a_ones_set"), sem("a_stack_zeroed")
    xt_ready, xt_copied = sem("a_xT_ready"), sem("a_xT_copied")
    mean_ready, centred, squared = sem("a_mean_ready"), sem("a_centred"), sem("a_squared")
    var_ready, rstd_ready, normed = sem("a_var_ready"), sem("a_rstd_ready"), sem("a_normed")
    projected, v_copied = sem("a_projected"), sem("a_v_copied")
    cosed, sined, rotated = sem("a_cosed"), sem("a_sined"), sem("a_rotated")
    hi_ready, rest_ready, mid_ready, lo_ready = (sem("a_" + n) for n in ("hi", "rest", "mid", "lo"))
    stored = [sem(f"a_stored{b}") for b in range(BATCH)]
    minus_ones_set = sem("a_minus_ones_set")
    laid_sems = [sem(f"a_laid_out{b}") for b in range(BATCH)]
    laid_count = 16 * (2 + 2 * sum(copies for table in (Q_PARTS, K_PARTS) for _, copies, _, _ in table))
    xv = x.rearrange("(t p) d -> p t d", p=P)
    STEPS = BATCH + 2

    def sync(sp):
        sp.dma_start(cst[:, 0:CONST["kmask"][0]], consts[:, 0:CONST["kmask"][0]]).then_inc(c_ld, 16)
        for b in range(BATCH):
            sp.dma_start(xtok[:, b * TILES:(b + 1) * TILES, :],
                         xv[:, b * TILES:(b + 1) * TILES, :]).then_inc(x_ld[b], 16)
            if b == 0:
                sp.dma_start(wat[:, :], w_attn).then_inc(w_ld, 16)
        sp.dma_start(cst[:, CONST["kmask"][0]:], consts[:, CONST["kmask"][0]:]).then_inc(c_ld, 16)
        sp.wait_ge(minus_ones_set, 1)
        for b in range(BATCH):
            sp.wait_ge(stack_zeroed, b + 1)
            for parity in range(2):
                a = 64 * parity + MAX_ROW
                sp.dma_start(stack[a:a + 2, b, 1, :, :],
                             minus1[:, None, :].broadcast_to([2, PAIRS, SEQ])).then_inc(laid_sems[b], 16)
            sp.wait_ge(lo_ready, b + 1)
            sp.dma_start(scratch[b], parts[:, b % 2]).then_inc(stored[b], 16)
            sp.wait_ge(stored[b], 16)
            for qk, table in enumerate((Q_PARTS, K_PARTS)):
                for parity in range(2):
                    src = scratch[b].rearrange("(c a r) s k t -> a s r k c t", a=2, r=DK)[parity]
                    for row, copies, part, same in table:
                        for j in range(copies):
                            a = parity * 64 + (row + j) * DK
                            sp.dma_start(stack[a:a + DK, b, qk, :, :],
                                         src[part if same else part + j, :, qk]).then_inc(laid_sems[b], 16)
        sp.wait_ge(c_ld, 32)

    def gpsimd(pool):
        pool.memset(eps, EPS).then_inc(eps_set, 1)
        pool.memset(minus1[:, :], -1.0).then_inc(minus_ones_set, 1)
        pool.memset(stack[:, 0], 0.0).then_inc(stack_zeroed, 1)
        pool.memset(vaug[:, :, :, :, :], 0.0).then_inc(vz, 1)
        pool.wait_ge(vz, 1)
        pool.memset(vaug[:, :, :, :, DK:DK + 1], 1.0).then_inc(vo, 1)
        for b in range(1, BATCH):
            pool.memset(stack[:, b], 0.0).then_inc(stack_zeroed, 1)
        pool.memset(xT[:, :, 0:PAD], 0.0).then_inc(pads, 1)
        pool.wait_ge(c_ld, 32)

    def tensor(pe):
        def turn(b):
            pe.wait_ge(x_ld[b], 16)
            if b >= 1:
                pe.wait_ge(xt_copied, b)
            for i in range(TILES):
                t = nc.tensor.transpose(ps[:, 0, i * P:(i + 1) * P], xtok[:, b * TILES + i, :], ident)
            t.then_inc(xt_ready, 1)

        def project(b):
            pe.wait_ge(normed, b + 1)
            if b == 0:
                pe.wait_ge(w_ld, 16)
            if b >= 1:
                pe.wait_ge(sined, b)
                pe.wait_ge(v_copied, b)
            for n, name in enumerate(("q", "k", "qr", "kr")):
                w = W_ATTN[name]
                nc.tensor.matmul(ps[:, 3 + n, :], wat[:, w:w + P], xn[:, b % 2, :], start=True, stop=True)
            for i in range(TILES):
                m = nc.tensor.matmul(ps[:, 7, i * P:(i + 1) * P], xn[:, b % 2, i * P:(i + 1) * P],
                                     wat[:, W_ATTN["v"]:W_ATTN["v"] + P], start=True, stop=True)
            m.then_inc(projected, 1)

        def mean(b):
            pe.wait_ge(xt_copied, b + 1)
            if b >= 1:
                pe.wait_ge(centred, b)
            nc.tensor.matmul(ps[:, 1, :], mean_w, xT[:, b, PAD:], start=True, stop=True).then_inc(mean_ready, 1)

        def variance(b):
            pe.wait_ge(squared, b + 1)
            if b >= 1:
                pe.wait_ge(log_ready, b)
            nc.tensor.matmul(ps[:, 2, :], mean_w, sq[:, b % 2, :], start=True, stop=True).then_inc(var_ready, 1)

        pe.wait_ge(c_ld, 16)
        for s in range(STEPS):
            if s < BATCH:
                turn(s)
                mean(s)
            if 1 <= s <= BATCH:
                variance(s - 1)
            if s >= 2:
                project(s - 2)
        pe.wait_ge(sined, BATCH)
        pe.wait_ge(v_copied, BATCH)
        pe.wait_ge(rstd_ready, BATCH)

    def scalar(act):
        nc.scalar.preload_act_table_set(LN_EXP)
        for s in range(STEPS):
            if s < BATCH:
                act.wait_ge(xt_ready, s + 1)
                nc.scalar.activation(xT[:, s, PAD:], ps[:, 0, :], ACT.Copy).then_inc(xt_copied, 1)
            if s < BATCH:
                act.wait_ge(centred, s + 1)
                if s >= 2:
                    act.wait_ge(var_ready, s - 1)
                nc.scalar.activation(sq[:, s % 2, :], cen[:, s % 2, :], ACT.Square).then_inc(squared, 1)
            if 1 <= s <= BATCH:
                b = s - 1
                act.wait_ge(var_ready, b + 1)
                if b == 0:
                    act.wait_ge(eps_set, 1)
                if b >= 1:
                    act.wait_ge(normed, b)
                nc.scalar.activation(rstd[:, :], ps[:, 2, :], ACT.Ln, bias=eps).then_inc(log_ready, 1)
                act.wait_ge(log_ready, b + 1)
                nc.scalar.activation(rstd[:, :], rstd[:, :], ACT.Exp, scale=-0.5).then_inc(rstd_ready, 1)
            if s >= 2:
                b = s - 2
                act.wait_ge(projected, b + 1)
                if b == 0:
                    act.wait_ge(vo, 1)
                nc.scalar.activation(vaug[:, b, :, :, 0:DK],
                                     ps[:, 7, :].rearrange("p (i h d) -> p i h d", i=TILES, h=HEADS),
                                     ACT.Copy).then_inc(v_copied, 1)
                if b >= 2:
                    act.wait_ge(stored[b - 2], 16)
                act.wait_ge(rotated, b + 1)
                nc.scalar.activation(parts[:, b % 2, 0], rc[:, :, :], ACT.Copy).then_inc(hi_ready, 1)
                act.wait_ge(rest_ready, s - 1)
                nc.scalar.activation(parts[:, (s - 2) % 2, 1], rs[:, :, :], ACT.Copy).then_inc(mid_ready, 1)

    def vector(dve):
        cos2 = const("cosT")[:, None, :].broadcast_to([P, 2, SEQ])
        sin2 = const("sinT")[:, None, :].broadcast_to([P, 2, SEQ])
        for s in range(STEPS):
            if s < BATCH:
                dve.wait_ge(mean_ready, s + 1)
                if s >= 2:
                    dve.wait_ge(normed, s - 1)
                    dve.wait_ge(squared, s - 1)
                nc.vector.tensor_tensor(cen[:, s % 2, :], xT[:, s, PAD:], ps[:, 1, :], ALU.subtract)\
                    .then_inc(centred, 1)
            if 1 <= s <= BATCH:
                b = s - 1
                dve.wait_ge(rstd_ready, b + 1)
                if b >= 2:
                    dve.wait_ge(projected, b - 1)
                nc.vector.tensor_tensor(xn[:, b % 2, :], cen[:, b % 2, :], rstd[:, :], ALU.mult)\
                    .then_inc(normed, 1)
            if s >= 2:
                b = s - 2
                dve.wait_ge(projected, b + 1)
                if b >= 1:
                    dve.wait_ge(lo_ready, b)
                nc.vector.tensor_tensor(rc[:, :, :], ps[:, 3:5, :], cos2, ALU.mult).then_inc(cosed, 1)
                nc.vector.tensor_tensor(rs[:, :, :], ps[:, 5:7, :], sin2, ALU.mult).then_inc(sined, 1)
                dve.wait_ge(sined, b + 1)
                dve.wait_ge(cosed, b + 1)
                nc.vector.tensor_tensor(rc[:, :, :], rc[:, :, :], rs[:, :, :], ALU.add).then_inc(rotated, 1)
                dve.wait_ge(hi_ready, s - 1)
                nc.vector.tensor_tensor(rs[:, :, :], rc[:, :, :], parts[:, s % 2, 0], ALU.subtract)\
                    .then_inc(rest_ready, 1)
                dve.wait_ge(mid_ready, s - 1)
                nc.vector.tensor_tensor(parts[:, s % 2, 2], rs[:, :, :], parts[:, s % 2, 1], ALU.subtract)\
                    .then_inc(lo_ready, 1)

    return (dict(sync=sync, gpsimd=gpsimd, tensor=tensor, scalar=scalar, vector=vector),
            [(laid, laid_count) for laid in laid_sems])


def softmax_values(env, stack_of, stack, vaug, probs, outs, max_scratch, parts_laid):
    nc, sem, ps, ident = (env[k] for k in ("nc", "sem", "ps", "ident"))
    sb = env["sb_in"](stack_of)
    MT = TILES * HEADS
    mx = sb("mx", [P, BATCH, MT])
    mparts = sb("mparts", [P, 2, MT], BF16)
    mrows = sb("mrows", [P, P], BF16)
    identb = sb("identb", [P, P], BF16)
    id_ready, warm = sem("b_ident_ready"), sem("b_warm")
    m_ready, m_read = sem("b_max_scores_ready"), sem("b_max_scores_read")
    mhi, mlo, mt_ready = (sem("b_" + n) for n in ("max_hi", "max_lo", "max_turned"))
    laid = [sem(f"b_max_laid{b}") for b in range(BATCH)]
    m_stored = [sem(f"b_max_stored{b}") for b in range(BATCH)]
    s_ready, e_ready = sem("b_scores_ready"), sem("b_exp_ready")
    pv_group, o_read = sem("b_probs_used"), sem("b_out_read")
    SLOTS = 3
    units = [(g, kt, j) for g in range(GROUPS) for kt in range(TILES) for j in range(4)]
    NU = len(units)
    NM = HEADS * TILES
    order = [(b, k) for b in range(BATCH) for k in range(NM // 2)]
    for b in reversed(range(BATCH)):
        order.insert((b + 1) * (NM // 2) + 6, (b, "turn"))
    slot_of = {event: n for n, event in enumerate(order)}
    AHEAD = NM + 32

    def rows(h):
        return slice(64 * (h % 2), 64 * (h % 2) + 64)

    def sync(sp):
        for b in range(BATCH):
            sp.wait_ge(m_read, slot_of[b, "turn"] + 1)
            sp.dma_start(max_scratch[b], mrows[:, :]).then_inc(m_stored[b], 16)
            sp.wait_ge(m_stored[b], 16)
            for part in range(2):
                for parity in range(2):
                    a = part * MT + parity * (MT // 2)
                    r = 64 * parity + MAX_ROW + part
                    sp.dma_start(stack[r:r + 1, b, 0, :, :].rearrange("o c (i q) -> o (c i) q", q=P),
                                 max_scratch[b, a:a + MT // 2, :].rearrange("(o n) q -> o n q", o=1))\
                        .then_inc(laid[b], 16)

    def tensor(pe):
        pe.wait_ge(id_ready, 1)

        def max_scores(b, n):
            c, parity, i = n // (2 * TILES), n // TILES % 2, n % TILES
            slot = slot_of[b, n // 2]
            if n % 2 == 0 and slot >= 2:
                pe.wait_ge(m_read, slot - 1)
            h = 2 * c + parity
            if n == 0:
                pe.wait_ge(*parts_laid[b])
            m = nc.tensor.matmul(ps[:, 2 * (slot % 2) + n % 2, :], stack[rows(h), b, 0, c, i * P:(i + 1) * P],
                                 stack[rows(h), b, 1, c, :], start=True, stop=True)
            if n % 2:
                m.then_inc(m_ready, 1)

        def turn_max(b):
            slot = slot_of[b, "turn"]
            pe.wait_ge(m_read, slot - 1)
            pe.wait_ge(mlo, b + 1)
            nc.tensor.transpose(ps[:, 2 * (slot % 2), 0:P // 2].bitcast(BF16),
                                mparts[:, :, :], identb[:, :]).then_inc(mt_ready, 1)

        def scores(b, u):
            g, kt, j = units[u]
            n = b * NU + u
            if n >= SLOTS:
                pe.wait_ge(e_ready, n - SLOTS + 1)
            h = 4 * g + j
            c = h // 2
            nc.tensor.matmul(ps[:, 4 + n % SLOTS, :], stack[rows(h), b, 1, c, kt * P:(kt + 1) * P],
                             stack[rows(h), b, 0, c, :], start=True, stop=True).then_inc(s_ready, 1)

        def values(b, k):
            g, kt, _ = units[4 * k]
            n = b * NU + 4 * k
            pe.wait_ge(e_ready, n + 4)
            out_n = b * GROUPS + g
            if kt == 0 and out_n >= 1:
                pe.wait_ge(o_read, out_n)
            for j in range(4):
                m = nc.tensor.matmul(ps[32 * j:32 * j + 32, 7, :], vaug[:, b, kt, 4 * g + j, :],
                                     probs[:, (n + j) % RING, :], start=(kt == 0), stop=(kt == TILES - 1),
                                     skip_group_check=True)
            m.then_inc(pv_group, 1)

        def stream(first, last):
            for m in range(first, min(last, BATCH * NM)):
                max_scores(m // NM, m % NM)
                after = slot_of[m // NM, m % NM // 2] + 1
                if m % 2 and after < len(order) and order[after][1] == "turn":
                    turn_max(order[after][0])

        stream(0, AHEAD)
        for _ in range(WARM_UP):
            w = nc.tensor.matmul(ps[:, 7, :], ident, env["xT"][:, 0, PAD:], start=True, stop=True)
        w.then_inc(warm, 1)
        pe.wait_ge(warm, 1)
        for b in range(BATCH):
            pe.wait_ge(laid[b], 64)
            for k in range(NU // 4):
                for j in range(4):
                    scores(b, 4 * k + j)
                    m = AHEAD + b * NU + 4 * k + j
                    stream(m, m + 1)
                if k >= 1:
                    values(b, k - 1)
            values(b, NU // 4 - 1)

    def scalar(act):
        for n in range(BATCH * NU):
            act.wait_ge(s_ready, n + 1)
            if n >= RING:
                act.wait_ge(pv_group, (n - RING) // 4 + 1)
            nc.scalar.activation(probs[:, n % RING, :], ps[:, 4 + n % SLOTS, :], ACT.Exp,
                                 scale=float(DK) ** -0.5).then_inc(e_ready, 1)

    def gpsimd(pool):
        nc.gpsimd.tensor_copy(identb[:, :], ident).then_inc(id_ready, 1)

    def vector(dve):
        def reduce(b, k):
            slot = slot_of[b, k]
            dve.wait_ge(m_ready, b * (NM // 2) + k + 1)
            nc.vector.tensor_reduce(mx_out(b, k), ps[:, 2 * (slot % 2):2 * (slot % 2) + 2, :],
                                    AX.X, ALU.max).then_inc(m_read, 1)

        def mx_out(b, k):
            n = 2 * k
            c, parity, i = n // (2 * TILES), n // TILES % 2, n % TILES
            at = parity * (MT // 2) + c * TILES + i
            return mx[:, b, at:at + 2]

        def split_max(b):
            dve.wait_ge(m_read, slot_of[b, NM // 2 - 1] + 1)
            if b >= 1:
                dve.wait_ge(mt_ready, b)
            nc.vector.tensor_copy(mparts[:, 0, :], mx[:, b, :]).then_inc(mhi, 1)
            dve.wait_ge(mhi, b + 1)
            nc.vector.tensor_tensor(mparts[:, 1, :], mx[:, b, :], mparts[:, 0, :], ALU.subtract).then_inc(mlo, 1)

        def take_turned(b):
            slot = slot_of[b, "turn"]
            dve.wait_ge(mt_ready, b + 1)
            if b >= 1:
                dve.wait_ge(m_stored[b - 1], 16)
            nc.vector.tensor_copy(mrows[:, :], ps[:, 2 * (slot % 2), 0:P // 2].bitcast(BF16)).then_inc(m_read, 1)

        def take_out(b, g):
            n = b * GROUPS + g
            dve.wait_ge(pv_group, (n + 1) * TILES)
            nc.vector.tensor_copy(outs[b][:, g, :], ps[:, 7, :]).then_inc(o_read, 1)

        def stream(first, last):
            for m in range(first, min(last, BATCH * NM), 2):
                b, k = m // NM, m % NM // 2
                reduce(b, k)
                if k == NM // 2 - 1:
                    split_max(b)
                after = slot_of[b, k] + 1
                if after < len(order) and order[after][1] == "turn":
                    take_turned(order[after][0])

        stream(0, AHEAD)
        for b in range(BATCH):
            for k in range(NU // 4):
                m = AHEAD + b * NU + 4 * k
                stream(m, m + 4)
                if k % TILES == 0 and k >= TILES:
                    take_out(b, k // TILES - 1)
            take_out(b, GROUPS - 1)

    return dict(sync=sync, gpsimd=gpsimd, tensor=tensor, scalar=scalar, vector=vector)


def attention_out(env, wat, outs):
    nc, sem, ps, const = (env[k] for k in ("nc", "sem", "ps", "const"))
    RING = 3
    xT = env["xT"]
    with ExitStack() as st:
        sb = env["sb_in"](st)
        inv = sb("inv", [P, RING, SEQ])
        on = sb("on", [P, RING, SEQ])
        sums_ready, inv_ready, scaled = sem("c_sums_ready"), sem("c_inverted"), sem("c_scaled")
        y_used, added = sem("c_scaled_used"), sem("c_added")
        log_ready = sem("c_log_ready")
        N = BATCH * GROUPS

        with nc.Block() as block:
            @block.scalar
            def _(act):
                nc.scalar.preload_act_table_set(LN_EXP)
                for n in range(N):
                    act.wait_ge(sums_ready, n + 1)
                    if n >= RING:
                        act.wait_ge(scaled, n - RING + 1)
                    nc.scalar.activation(inv[:, n % RING, :], ps[:, n % RING, :], ACT.Ln).then_inc(log_ready, 1)
                    act.wait_ge(log_ready, n + 1)
                    nc.scalar.activation(inv[:, n % RING, :], inv[:, n % RING, :], ACT.Exp, scale=-1.0)\
                        .then_inc(inv_ready, 1)

            @block.tensor
            def _(pe):
                def spread_sums(n):
                    if n >= RING:
                        pe.wait_ge(log_ready, n - RING + 1)
                    nc.tensor.matmul(ps[:, n % RING, :], const("sums"), outs[n // GROUPS][:, n % GROUPS, :],
                                     start=True, stop=True).then_inc(sums_ready, 1)

                def project(n):
                    b, g = n // GROUPS, n % GROUPS
                    pe.wait_ge(scaled, n + 1)
                    if g == 0 and b >= 2:
                        pe.wait_ge(added, b - 1)
                    w = W_ATTN["o0"] + g * P
                    m = nc.tensor.matmul(ps[:, RING + b % 2, :], wat[:, w:w + P], on[:, n % RING, :],
                                         start=(g == 0), stop=(g == GROUPS - 1))
                    m.then_inc(y_used, 1)

                for n in range(RING - 1):
                    spread_sums(n)
                for n in range(N):
                    if n + RING - 1 < N:
                        spread_sums(n + RING - 1)
                    project(n)

            @block.vector
            def _(dve):
                for n in range(N):
                    b, g = n // GROUPS, n % GROUPS
                    dve.wait_ge(inv_ready, n + 1)
                    if n >= RING:
                        dve.wait_ge(y_used, n - RING + 1)
                    nc.vector.tensor_tensor(on[:, n % RING, :], outs[b][:, g, :], inv[:, n % RING, :], ALU.mult)\
                        .then_inc(scaled, 1)
                    if g == 0 and b >= 1:
                        dve.wait_ge(y_used, b * GROUPS)
                        nc.vector.tensor_tensor(xT[:, b - 1, PAD:], xT[:, b - 1, PAD:], ps[:, RING + (b - 1) % 2, :],
                                                ALU.add).then_inc(added, 1)
                dve.wait_ge(y_used, N)
                nc.vector.tensor_tensor(xT[:, BATCH - 1, PAD:], xT[:, BATCH - 1, PAD:],
                                        ps[:, RING + (BATCH - 1) % 2, :], ALU.add).then_inc(added, 1)


def cross_attention(env, ctxT, w_xq, w_xkv, w_xo, wqkv, qk_scales, kept):
    nc, sem, ps, const, ident, mean_w = (env[k] for k in ("nc", "sem", "ps", "const", "ident", "mean_w"))
    xT, x2T, eps = env["xT"], env["x2T"], env["eps"]
    NT = BATCH * TILES
    with ExitStack() as st:
        sb = env["sb_in"](st)
        zT = sb("zT", [LATENT, BATCH * CTX])
        zT4 = sb("zT4", [LATENT, BATCH, 4, CTX])
        wq = sb("x_wq", [P, P])
        wkv = sb("x_wkv", [LATENT, 2 * P])
        wo = sb("x_wo", [P, P])
        kT = sb("x_kT", [P, BATCH, CTX])
        kb = sb("x_kb", [P, BATCH, HEADS, CTX])
        vb = sb("x_vb", [P, BATCH, GROUPS, P])
        cen = sb("x_cen", [P, 2, SEQ])
        sq = sb("x_sq", [P, 2, SEQ])
        rstd = sb("x_rstd", [P, 2, SEQ])
        xn = sb("x_xn", [P, 2, SEQ])
        qT = sb("x_qT", [P, BATCH, SEQ])
        mx = sb("x_mx", [P, 2, HEADS])
        dif = sb("x_dif", [P, 2, HEADS, CTX])
        ex = sb("x_ex", [P, 2, HEADS, CTX])
        total = sb("x_total", [P, 2, HEADS])
        inv = sb("x_inv", [P, 2, HEADS])
        prob = sb("x_prob", [P, 2, HEADS * CTX])
        pT = sb("x_pT", [P, GROUPS, SEQ])
        oT = sb("x_oT", [P, SEQ])
        ld, first_ld, zeroed = sem("x_loaded"), sem("l_first_loaded"), sem("l_zeroed")
        rep, kv_ready, kt_done, kb_done, vb_done = (sem("x_" + n) for n in
                                                    ("z_repeated", "kv_ready", "k_copied", "k_spread", "v_spread"))
        mean_ready, centred, squared = sem("x_mean_ready"), sem("x_centred"), sem("x_squared")
        var_ready, rstd_ready, normed = sem("x_var_ready"), sem("x_rstd_ready"), sem("x_normed")
        q_ready, q_copied = sem("x_q_ready"), sem("x_q_copied")
        s_ready, m_done, d_done, e_done = (sem("x_" + n) for n in ("scores", "max", "shifted", "exp"))
        t_done, i_done, p_done = (sem("x_" + n) for n in ("sum", "inverse", "probs"))
        pt_ready, pt_done, o_ready, o_done, y_ready, added = (
            sem("x_" + n) for n in ("probs_turned", "probs_copied", "out_ready", "out_copied", "y_ready", "added"))
        copied = sem("x_residual_kept")
        log_ready = sem("x_log_ready")

        NORM_STEPS = BATCH + 2
        STEPS = NT + 7

        def batch_at(t, first):
            return (t - first) // TILES if t >= first and (t - first) % TILES == 0 and t - first < NT else None

        def pieces(t):
            return [batch_at(t, TILES + n) for n in (2, 3, 4, 5, 6)]

        with nc.Block() as block:
            @block.sync
            def _(sp):
                for dst, src in ((zT, ctxT), (wkv, w_xkv), (wq, w_xq), (wo, w_xo)):
                    sp.dma_start(dst[:, :], src).then_inc(ld, 16)
                sp.dma_start(kept["wqkv"][:, :], wqkv[0]).then_inc(first_ld, 16)
                sp.dma_start(kept["scales"][:, :, :], qk_scales[0:1].broadcast_to([P, 2, DH])).then_inc(first_ld, 16)
                sp.wait_ge(ld, 64)
                sp.wait_ge(first_ld, 32)

            @block.tensor
            def _(pe):
                pe.wait_ge(ld, 64)
                nc.tensor.matmul(ps[:, 3, 0:P], wkv[:, 0:P], zT[:, :], start=True, stop=True)
                pe.wait_ge(rep, 1)
                for b in range(BATCH):
                    m = nc.tensor.matmul(ps[:, 4, b * P:(b + 1) * P], zT4[:, b, :, :], wkv[:, P:2 * P],
                                         start=True, stop=True)
                m.then_inc(kv_ready, 1)

                def mean(n):
                    if n >= 1:
                        pe.wait_ge(centred, n)
                    if n >= BATCH:
                        pe.wait_ge(added, n - BATCH + 1)
                    nc.tensor.matmul(ps[:, 0, :], mean_w, xT[:, n % BATCH, PAD:], start=True, stop=True)\
                        .then_inc(mean_ready, 1)

                def variance(n):
                    pe.wait_ge(squared, n + 1)
                    if n >= 1:
                        pe.wait_ge(log_ready, n)
                    nc.tensor.matmul(ps[:, 1, :], mean_w, sq[:, n % 2, :], start=True, stop=True).then_inc(var_ready, 1)

                def query(b):
                    pe.wait_ge(normed, b + 1)
                    if b >= 1:
                        pe.wait_ge(q_copied, b)
                    nc.tensor.matmul(ps[:, 2, :], wq[:, :], xn[:, b % 2, :], start=True, stop=True).then_inc(q_ready, 1)

                def scores(t):
                    b, i = t // TILES, t % TILES
                    pe.wait_ge(q_copied, b + 1)
                    if t == 0:
                        pe.wait_ge(vb_done, BATCH * GROUPS)
                        pe.wait_ge(kb_done, BATCH)
                    if t >= 2:
                        pe.wait_ge(d_done, t - 1)
                    nc.tensor.matmul(ps[:, 3 + t % 2, :], qT[:, b, i * P:(i + 1) * P], kb[:, b, :, :],
                                     start=True, stop=True).then_inc(s_ready, 1)

                def turn(t):
                    pe.wait_ge(p_done, t + 1)
                    if t >= 2:
                        pe.wait_ge(pt_done, t - 1)
                    for g in range(GROUPS):
                        m = nc.tensor.transpose(ps[:, 5 + t % 2, g * P:(g + 1) * P], prob[:, t % 2, g * P:(g + 1) * P],
                                                ident)
                    m.then_inc(pt_ready, 1)

                def values(b):
                    pe.wait_ge(pt_done, (b + 1) * TILES)
                    if b >= 1:
                        pe.wait_ge(o_done, b)
                    for g in range(GROUPS):
                        m = nc.tensor.matmul(ps[:, 7, :], vb[:, b, g, :], pT[:, g, :], start=(g == 0),
                                             stop=(g == GROUPS - 1))
                    m.then_inc(o_ready, 1)

                def output(b):
                    pe.wait_ge(o_done, b + 1)
                    if b >= 1:
                        pe.wait_ge(added, b)
                    nc.tensor.matmul(ps[:, 2, :], wo[:, :], oT[:, :], start=True, stop=True).then_inc(y_ready, 1)

                for s in range(NORM_STEPS):
                    if s < BATCH:
                        mean(s)
                    if 1 <= s <= BATCH:
                        variance(s - 1)
                    if s >= 2:
                        query(s - 2)
                for t in range(STEPS):
                    b_o, b_y, _, b_mean, b_var = pieces(t)
                    if t < NT:
                        scores(t)
                    if b_o is not None:
                        values(b_o)
                    if b_y is not None:
                        output(b_y)
                    if b_mean is not None:
                        mean(BATCH + b_mean)
                    if b_var is not None:
                        variance(BATCH + b_var)
                    if 0 <= t - 2 < NT:
                        turn(t - 2)

            @block.scalar
            def _(act):
                nc.scalar.preload_act_table_set(LN_EXP)
                act.wait_ge(ld, 64)
                nc.scalar.activation(zT4[:, :, :, :], zT[:, :].rearrange("p (b c) -> p b c", b=BATCH)[:, :, None, :]
                                     .broadcast_to([LATENT, BATCH, 4, CTX]), ACT.Copy).then_inc(rep, 1)

                def square(n):
                    act.wait_ge(centred, n + 1)
                    if n >= 2:
                        act.wait_ge(var_ready, n - 1)
                    nc.scalar.activation(sq[:, n % 2, :], cen[:, n % 2, :], ACT.Square).then_inc(squared, 1)

                def inverse_deviation(n):
                    act.wait_ge(var_ready, n + 1)
                    if n >= 2:
                        act.wait_ge(normed, n - 1)
                    nc.scalar.activation(rstd[:, n % 2, :], ps[:, 1, :], ACT.Ln, bias=eps).then_inc(log_ready, 1)
                    act.wait_ge(log_ready, n + 1)
                    nc.scalar.activation(rstd[:, n % 2, :], rstd[:, n % 2, :], ACT.Exp, scale=-0.5)\
                        .then_inc(rstd_ready, 1)

                def query(b):
                    act.wait_ge(q_ready, b + 1)
                    nc.scalar.activation(qT[:, b, :], ps[:, 2, :], ACT.Copy).then_inc(q_copied, 1)

                def exps(t):
                    act.wait_ge(d_done, t + 1)
                    if t >= 2:
                        act.wait_ge(t_done, t - 1)
                        act.wait_ge(p_done, t - 1)
                    nc.scalar.activation(ex[:, t % 2], dif[:, t % 2], ACT.Exp, scale=float(DK) ** -0.5)\
                        .then_inc(e_done, 1)

                def turned(t):
                    b, i = t // TILES, t % TILES
                    act.wait_ge(pt_ready, t + 1)
                    if i == 0 and b >= 1:
                        act.wait_ge(o_ready, b)
                    nc.scalar.activation(pT[:, :, i * P:(i + 1) * P],
                                         ps[:, 5 + t % 2, :].rearrange("p (g q) -> p g q", g=GROUPS), ACT.Copy)\
                        .then_inc(pt_done, 1)

                for s in range(NORM_STEPS):
                    if s < BATCH:
                        square(s)
                    if 1 <= s <= BATCH:
                        inverse_deviation(s - 1)
                    if s >= 2:
                        query(s - 2)
                for t in range(STEPS):
                    b_o, _, b_add, b_mean, b_var = pieces(t)
                    if b_add is not None:
                        act.wait_ge(added, b_add + 1)
                        nc.scalar.activation(x2T[:, b_add, :], xT[:, b_add, PAD:], ACT.Copy).then_inc(copied, 1)
                    if t < NT:
                        exps(t)
                    if b_o is not None:
                        act.wait_ge(o_ready, b_o + 1)
                        if b_o >= 1:
                            act.wait_ge(y_ready, b_o)
                        nc.scalar.activation(oT[:, :], ps[:, 7, :], ACT.Copy).then_inc(o_done, 1)
                    if b_mean is not None:
                        square(BATCH + b_mean)
                    if b_var is not None:
                        inverse_deviation(BATCH + b_var)
                    if 0 <= t - 2 < NT:
                        turned(t - 2)

            @block.gpsimd
            def _(pool):
                pool.wait_ge(kt_done, 1)
                for b in range(BATCH):
                    nc.gpsimd.tensor_tensor(kb[:, b], kT[:, b, None, :].broadcast_to([P, HEADS, CTX]),
                                            const("kmask")[:, :, None].broadcast_to([P, HEADS, CTX]), ALU.mult)\
                        .then_inc(kb_done, 1)
                pool.memset(env["xsT"][:, :, 0:1], 0.0).then_inc(zeroed, 1)
                pool.memset(kept["kb"][:, :, :, :, :], 0.0).then_inc(zeroed, 1)
                pool.memset(kept["vb"][:, :, :, :, :], 0.0).then_inc(zeroed, 1)
                for t in range(NT):
                    pool.wait_ge(i_done, t + 1)
                    if t >= 2:
                        pool.wait_ge(pt_ready, t - 1)
                    nc.gpsimd.tensor_tensor(prob[:, t % 2, :].rearrange("p (h c) -> p h c", h=HEADS), ex[:, t % 2],
                                            inv[:, t % 2, :, None].broadcast_to([P, HEADS, CTX]), ALU.mult)\
                        .then_inc(p_done, 1)

            @block.vector
            def _(dve):
                def spread_v(b):
                    for g in range(GROUPS):
                        nc.vector.tensor_tensor(
                            vb[:, b, g, :].rearrange("p (h d) -> p h d", h=HEADS),
                            ps[:, 4, b * P:(b + 1) * P].rearrange("p (h d) -> p h d", h=HEADS),
                            const("vmask")[:, g * HEADS:(g + 1) * HEADS, None].broadcast_to([P, HEADS, DK]),
                            ALU.mult).then_inc(vb_done, 1)

                def centre(n):
                    dve.wait_ge(mean_ready, n + 1)
                    if n >= 2:
                        dve.wait_ge(normed, n - 1)
                        dve.wait_ge(squared, n - 1)
                    nc.vector.tensor_tensor(cen[:, n % 2, :], xT[:, n % BATCH, PAD:], ps[:, 0, :], ALU.subtract)\
                        .then_inc(centred, 1)

                def scale(n):
                    dve.wait_ge(rstd_ready, n + 1)
                    if 2 <= n < BATCH:
                        dve.wait_ge(q_ready, n - 1)
                    if n >= BATCH:
                        dve.wait_ge(copied, n - BATCH + 1)
                    nc.vector.tensor_tensor(xn[:, n % 2, :] if n < BATCH else xT[:, n - BATCH, PAD:], cen[:, n % 2, :],
                                            rstd[:, n % 2, :], ALU.mult).then_inc(normed, 1)

                def shift(t):
                    dve.wait_ge(s_ready, t + 1)
                    sv = ps[:, 3 + t % 2, :].rearrange("p (h c) -> p h c", h=HEADS)
                    if t >= 2:
                        dve.wait_ge(d_done, t - 1)
                    nc.vector.tensor_reduce(mx[:, t % 2, :], sv, AX.X, ALU.max).then_inc(m_done, 1)
                    dve.wait_ge(m_done, t + 1)
                    if t >= 2:
                        dve.wait_ge(e_done, t - 1)
                    nc.vector.tensor_tensor(dif[:, t % 2], sv, mx[:, t % 2, :, None].broadcast_to([P, HEADS, CTX]),
                                            ALU.subtract).then_inc(d_done, 1)

                def sums(t):
                    dve.wait_ge(e_done, t + 1)
                    if t >= 2:
                        dve.wait_ge(i_done, t - 1)
                    nc.vector.tensor_reduce(total[:, t % 2, :], ex[:, t % 2], AX.X, ALU.add).then_inc(t_done, 1)
                    dve.wait_ge(t_done, t + 1)
                    if t >= 2:
                        dve.wait_ge(p_done, t - 1)
                    nc.vector.reciprocal(inv[:, t % 2, :], total[:, t % 2, :]).then_inc(i_done, 1)

                dve.wait_ge(kv_ready, 1)
                nc.vector.tensor_copy(kT[:, :, :], ps[:, 3, 0:P].rearrange("p (b c) -> p b c", b=BATCH))\
                    .then_inc(kt_done, 1)
                for s in range(NORM_STEPS):
                    if s < BATCH:
                        centre(s)
                    if 1 <= s <= BATCH:
                        scale(s - 1)
                    if s < BATCH:
                        spread_v(s)
                for t in range(STEPS):
                    _, _, b_add, b_mean, b_var = pieces(t)
                    if t < NT:
                        shift(t)
                    if 0 <= t - 1 < NT:
                        sums(t - 1)
                    if b_add is not None:
                        dve.wait_ge(y_ready, b_add + 1)
                        nc.vector.tensor_tensor(xT[:, b_add, PAD:], xT[:, b_add, PAD:], ps[:, 2, :], ALU.add)\
                            .then_inc(added, 1)
                    if b_mean is not None:
                        centre(BATCH + b_mean)
                    if b_var is not None:
                        scale(BATCH + b_var)


def finish(env, out):
    nc, sem, ps, ident = (env[k] for k in ("nc", "sem", "ps", "ident"))
    xT, x2T = env["xT"], env["x2T"]
    with ExitStack() as st:
        sb = env["sb_in"](st)
        tok = sb("tok", [P, BATCH, TILES, DIM])
        summed, turned, copied = sem("f_summed"), sem("f_turned"), sem("f_copied")
        stored = [sem(f"f_stored{b}") for b in range(BATCH)]

        with nc.Block() as block:
            @block.vector
            def _(dve):
                for b in range(BATCH):
                    nc.vector.tensor_tensor(x2T[:, b, :], x2T[:, b, :], xT[:, b, PAD:], ALU.add).then_inc(summed, 1)

            @block.tensor
            def _(pe):
                for b in range(BATCH):
                    pe.wait_ge(summed, b + 1)
                    for i in range(TILES):
                        m = nc.tensor.transpose(ps[:, b, i * P:(i + 1) * P], x2T[:, b, i * P:(i + 1) * P], ident)
                    m.then_inc(turned, 1)

            @block.scalar
            def _(act):
                for b in range(BATCH):
                    act.wait_ge(turned, b + 1)
                    nc.scalar.activation(tok[:, b], ps[:, b, :].rearrange("p (i d) -> p i d", i=TILES), ACT.Copy)\
                        .then_inc(copied, 1)

            @block.sync
            def _(sp):
                for b in range(BATCH):
                    sp.wait_ge(copied, b + 1)
                    sp.dma_start(out[b].rearrange("(i p) d -> p i d", p=P), tok[:, b]).then_inc(stored[b], 16)
                for b in range(BATCH):
                    sp.wait_ge(stored[b], 16)


def layers(env, kept, wqkv, qk_scales, wo, w1, w2, vecs):
    nc, sem, ps, const, ident, mean_w = (env[k] for k in ("nc", "sem", "ps", "const", "ident", "mean_w"))
    xT, xsT, eps = env["xT"], env["xsT"], env["eps"]
    NT = BATCH * TILES
    with ExitStack() as st:
        sb = env["sb_in"](st)
        wqkv_sb, scales, kb, vb = (kept[k] for k in ("wqkv", "scales", "kb", "vb"))
        wqkv_next = sb("l_wqkv_next", [P, 3 * INNER])
        wo_sb = sb("l_wo", [P, PAIRS, P])
        w1_sb = sb("l_w1", [P, 2 * HIDDEN])
        w2_sb = sb("l_w2", [P, len(HC), P])
        vec = sb("l_vec", [P, N_VEC])
        tab_c = sb("l_tab_c", [P, 2, TILES, DH])
        tab_s = sb("l_tab_s", [P, 2, TILES, DH])
        mask = sb("l_mask", [P, BANK], BF16)
        mask_sel = sb("l_mask_sel", [P, 2, P], BF16)
        sq = sb("l_sq", [P, 2, HEADS, DH])
        norms = sb("l_norms", [P, 2, 2, HEADS])
        qn = sb("l_qn", [P, 2, HEADS, DH])
        rot = sb("l_rot", [P, 2, HEADS, DH])
        rot_s = sb("l_rot_s", [P, 2, HEADS, DH])
        qT = sb("l_qT", [P, PAIRS, P])
        mx = sb("l_mx", [P, 2, HEADS])
        dif = sb("l_dif", [P, HEADS, 2 * WINDOW])
        prob = sb("l_prob", [P, 2, HEADS, 2 * WINDOW])
        total = sb("l_total", [P, 2, HEADS])
        inv = sb("l_inv", [P, 2, HEADS])
        pT = sb("l_pT", [P, PAIRS, P])
        o_tok = sb("l_o_tok", [P, HEADS, DH])
        oT = sb("l_oT", [P, PAIRS, SEQ])
        xf = sb("l_xf", [P, SEQ])
        cen = sb("l_cen", [P, SEQ])
        fsq = sb("l_fsq", [P, SEQ])
        rstd = sb("l_rstd", [P, SEQ])
        xg = sb("l_xg", [P, SEQ])
        gel = sb("l_gel", [P, len(HC), SEQ])
        hid = sb("l_hid", [P, len(HC), SEQ])
        ln256 = sb("l_ln256", [P, 1])

        consts_set = sem("l_consts_set")
        wo_ld, w1_ld, w2_ld, vec_ld = (sem("l_" + n) for n in ("wo_loaded", "w1_loaded", "w2_loaded", "vec_loaded"))
        next_ld, next_scales = sem("l_next_wqkv_loaded"), sem("l_next_scales_loaded")
        wqkv_moved = sem("l_wqkv_moved")
        xs_ready = sem("l_xs_ready")
        cos_ready, sin_ready = sem("l_cosines_ready"), sem("l_sines_ready")
        squared, summed, bounded = sem("l_squared"), sem("l_squares_summed"), sem("l_squares_bounded")
        logged, norm_ready = sem("l_norm_logged"), sem("l_norm_ready")
        sined, cosed, rotated, carried = (sem("l_" + n) for n in ("sined", "cosed", "rotated", "carried"))
        slot_full = [sem(f"l_slot{i}_full") for i in range(4)]
        slot_free = [sem(f"l_slot{i}_free") for i in range(4)]
        maxed, exped, sum_ready, inv_ready = (sem("l_" + n) for n in ("maxed", "exped", "sum_ready", "inv_ready"))
        xf_ready, fsquared, rstd_ready, xn_ready, xg_ready, gelu_ready = (
            sem("l_" + n) for n in ("ffn_x_ready", "ffn_squared", "rstd_ready", "xn_ready", "xg_ready", "gelu_ready"))
        body_sems = range(wo_ld.num, gelu_ready.num + 1)

        HEAD = 6
        STEPS = NT + HEAD

        def batch_at(t, first):
            return (t - first) // TILES if t >= first and (t - first) % TILES == 0 and t - first < NT else None

        def pieces(t):
            return [batch_at(t, first) for first in (6, 7, 8, 9)]

        def plan_turns(steps, tiles):
            turns, taken = {}, [0] * 4

            def plan(key, n):
                turns[key] = n, taken[n]
                taken[n] += 1

            for t in steps:
                b_wo, b_norm, b_hid, b_y = pieces(t)
                if t < tiles:
                    plan(("k", t), 1)
                if 0 <= t - 1 < tiles:
                    plan(("kT", t - 1), 3)
                    plan(("qT", t - 1), 2)
                if t < tiles:
                    plan(("q", t), 0)
                if 0 <= t - 2 < tiles:
                    plan(("pT", t - 2), 2)
                if 0 <= t - 1 < tiles:
                    plan(("s", t - 1), 3)
                if 0 <= t - 2 < tiles:
                    plan(("o", t - 2), 2)
                for key, b in ((("wo", b_wo), b_wo), (("mean", b_norm), b_norm), (("h", b_hid, 0), b_hid)):
                    if b is not None:
                        plan(key, 1)
                if 0 <= t - 1 < tiles:
                    plan(("v", t - 1, 0), 0)
                    plan(("v", t - 1, 1), 3)
                if b_y is not None:
                    plan(("y", b_y), 1)
                if b_hid is not None:
                    plan(("h", b_hid, 1), 1)
                    plan(("h", b_hid, 2), 0)
                if 0 <= t - 2 < tiles:
                    plan(("oT", t - 2), 2)
                if b_norm is not None:
                    plan(("var", b_norm), 0)
            return turns

        with nc.Block() as block:
            @block.gpsimd
            def _(pool):
                pool.memset(ln256[:, :], 8 * LN_2).then_inc(consts_set, 1)

            @block.vector
            def _(dve):
                nc.vector.memset(mask[2 * WINDOW:, :], 0.0).then_inc(consts_set, 1)
                nc.vector.memset(mask_sel[2 * WINDOW:, :, :], 0.0).then_inc(consts_set, 1)
                nc.vector.tensor_copy(mask[0:2 * WINDOW, :], const("wmask")[0:2 * WINDOW, :]).then_inc(consts_set, 1)
                nc.vector.tensor_copy(mask_sel[0:2 * WINDOW, :, :],
                                      const("wsel")[0:2 * WINDOW, :].rearrange("p (a q) -> p a q", a=2))\
                    .then_inc(consts_set, 1)

        def segment(layer, steps, tiles):
            first = steps[0]
            turns = plan_turns(steps, tiles)
            before = {s.num: n for n, group in (
                (2 * first, (squared, summed, bounded, logged, norm_ready, cosed, sined, rotated)),
                (max(first - 1, 0), (carried, maxed, exped)),
                (max(first - 2, 0), (sum_ready, inv_ready)),
                (2 * 32 if first else 0, (xs_ready,))) for s in group}
            more = tiles > NT and first > 0

            def slot(*key):
                n = turns[key][0]
                return ps[:, 2 * n:2 * n + 2, :]

            def filled(key):
                return slot_full[turns[key][0]]

            def read(key):
                return slot_free[turns[key][0]]

            def wait(engine, semaphore, count):
                if count > before[semaphore.num]:
                    engine.wait_ge(semaphore, count - before[semaphore.num])

            def wait_full(engine, *key):
                if key in turns:
                    n, turn = turns[key]
                    engine.wait_ge(slot_full[n], turn + 1)

            def wait_free(engine, *key):
                if key in turns:
                    n, turn = turns[key]
                    engine.wait_ge(slot_free[n], turn + 1)

            def take(pe, *key):
                n, turn = turns[key]
                if turn >= 1:
                    pe.wait_ge(slot_free[n], turn)

            with nc.Block() as block:
                @block.sync
                def _(sp):
                    if first > 0:
                        sp.dma_start(wo_sb[:, :, :], wo[layer].rearrange("(c p) n -> p c n", p=P)).then_inc(wo_ld, 16)
                        sp.dma_start(vec[:, :], vecs[layer]).then_inc(vec_ld, 16)
                        sp.dma_start(w1_sb[:, :], w1[layer]).then_inc(w1_ld, 16)
                        sp.dma_start(w2_sb[:, :, :], w2[layer].rearrange("(c p) n -> p c n", p=P))\
                            .then_inc(w2_ld, 16)
                    if more:
                        sp.dma_start(wqkv_next[:, :], wqkv[layer + 1]).then_inc(next_ld, 16)
                        sp.dma_start(scales[:, :, :], qk_scales[layer + 1][None].broadcast_to([P, 2, DH]))\
                            .then_inc(next_scales, 16)

                    def shift_tokens(dst, batch, semaphore):
                        cols = dst.shape[-1]
                        a = PAD + SEQ - cols
                        sp.dma_start(dst[0:64, :], xT[0:64, batch, a:]).then_inc(semaphore, 16)
                        sp.dma_start(dst[64:P, :], xT[64:P, batch, a - 1:PAD + SEQ - 1]).then_inc(semaphore, 16)

                    def shift_batch(batch):
                        wait_free(sp, "y", batch - BATCH)
                        wait_full(sp, "q", (batch - BATCH) * TILES + TILES - 1)
                        for half in range(2):
                            wait_full(sp, "v", (batch - BATCH) * TILES + TILES - 1, half)
                        wait(sp, xs_ready, 32 * batch)
                        shift_tokens(xsT[:, batch % BATCH, 1:], batch % BATCH, xs_ready)

                    if first == 0:
                        shift_batch(0)
                    for t in steps:
                        b_wo = pieces(t)[0]
                        if b_wo is not None:
                            wait_free(sp, "wo", b_wo)
                            if b_wo >= 1:
                                wait_free(sp, "mean", b_wo - 1)
                                sp.wait_ge(xf_ready, 32 * b_wo)
                            shift_tokens(xf[:, :], b_wo, xf_ready)
                        if t % TILES == TILES - 2 and t + 2 < tiles:
                            shift_batch(t // TILES + 1)

                @block.gpsimd
                def _(pool):
                    def cosine_table():
                        if more:
                            pool.wait_ge(next_scales, 16)
                            wait(pool, cosed, 2 * NT)
                        nc.gpsimd.tensor_tensor(tab_c[:, :, :, :],
                                                const("ropeC").rearrange("p (a i d) -> p a i d", a=2, i=TILES),
                                                scales[:, :, None, :].broadcast_to([P, 2, TILES, DH]), ALU.mult)\
                            .then_inc(cos_ready, 1)
                        pool.wait_ge(cos_ready, 1)

                    def carry(t):
                        wait_free(pool, "kT", t - 1)
                        wait_full(pool, "s", t - 2)
                        nc.gpsimd.tensor_copy(kb[:, t % 2, :, :, 0:WINDOW],
                                              kb[:, (t - 1) % 2, :, :, P:P + WINDOW]).then_inc(carried, 1)

                    def rotate(t, r):
                        n, name, part = 1 - r, ("k", "q")[r], 2 * t + r
                        wait_free(pool, name, t)
                        wait_full(pool, name + "T", t - 1)
                        nc.gpsimd.tensor_tensor(rot[:, n], qn[:, n],
                                                tab_c[:, n, t % TILES, None, :].broadcast_to([P, HEADS, DH]),
                                                ALU.mult).then_inc(cosed, 1)
                        wait(pool, cosed, part + 1)
                        wait(pool, sined, part + 1)
                        nc.gpsimd.tensor_tensor(rot[:, n], rot[:, n], rot_s[:, n], ALU.add).then_inc(rotated, 1)

                    for t in steps:
                        if t < tiles:
                            if t >= 1:
                                carry(t)
                            if t % NT == 0:
                                cosine_table()
                            rotate(t, 0)
                            rotate(t, 1)

                @block.tensor
                def _(pe):
                    def project(name, t):
                        b, i = t // TILES % BATCH, t % TILES
                        if i == 0:
                            wait(pe, xs_ready, 32 * (t // TILES + 1))
                        if t == NT:
                            pe.wait_ge(wqkv_moved, 1)
                        take(pe, name, t)
                        for c in range(2):
                            a = "qk".index(name) * INNER + c * BANK
                            m = nc.tensor.matmul(slot(name, t)[:, c, :], xsT[:, b, PAD + i * P:PAD + (i + 1) * P],
                                                 wqkv_sb[:, a:a + BANK], start=True, stop=True)
                        m.then_inc(filled((name, t)), 1)

                    def turn(name, t):
                        wait(pe, rotated, 2 * t + (1 if name == "k" else 2))
                        take(pe, name + "T", t)
                        dst = slot(name + "T", t)
                        for c in range(PAIRS):
                            m = nc.tensor.transpose(dst[:, c // 4, (c % 4) * P:(c % 4 + 1) * P],
                                                    rot[:, "qk".index(name), 2 * c:2 * c + 2, :], ident)
                        m.then_inc(filled((name + "T", t)), 1)

                    def scores(t):
                        wait_free(pe, "qT", t)
                        wait_free(pe, "kT", t)
                        wait(pe, carried, t)
                        take(pe, "s", t)
                        dst = slot("s", t)
                        opening = int(t % TILES == 0)
                        for n in range(2):
                            nc.tensor.matmul(dst[:, n, :], mask_sel[:, opening, :], mask[:, :], start=True, stop=False,
                                             skip_group_check=True)
                        for c in range(PAIRS):
                            for j in range(P // WINDOW):
                                a = j * WINDOW
                                m = nc.tensor.matmul(dst[a:a + WINDOW, c // 4, (c % 4) * P:(c % 4 + 1) * P],
                                                     qT[:, c, a:a + WINDOW], kb[:, t % 2, c, :, a:a + 2 * WINDOW],
                                                     start=False, stop=True, skip_group_check=True)
                        m.then_inc(filled(("s", t)), 1)

                    def turn_probs(t):
                        wait(pe, exped, t + 1)
                        take(pe, "pT", t)
                        dst = slot("pT", t)
                        for c in range(PAIRS):
                            m = nc.tensor.transpose(dst[:, c // 4, (c % 4) * P:(c % 4 + 1) * P],
                                                    prob[:, t % 2, 2 * c:2 * c + 2, :], ident)
                        m.then_inc(filled(("pT", t)), 1)

                    def values(t):
                        wait_free(pe, "pT", t)
                        wait_free(pe, "v", t, 0)
                        wait_free(pe, "v", t, 1)
                        take(pe, "o", t)
                        dst = slot("o", t)
                        for c in range(PAIRS):
                            for j in range(P // WINDOW):
                                a = j * WINDOW
                                m = nc.tensor.matmul(dst[a:a + WINDOW, c // 4, (c % 4) * P:(c % 4 + 1) * P],
                                                     pT[:, c, a:a + WINDOW], vb[:, j, c, :, :],
                                                     start=True, stop=True, skip_group_check=True)
                        m.then_inc(filled(("o", t)), 1)

                    def turn_out(t):
                        wait_free(pe, "o", t)
                        take(pe, "oT", t)
                        dst = slot("oT", t)
                        for c in range(PAIRS):
                            m = nc.tensor.transpose(dst[:, c // 4, (c % 4) * P:(c % 4 + 1) * P],
                                                    o_tok[:, 2 * c:2 * c + 2, :], ident)
                        m.then_inc(filled(("oT", t)), 1)

                    def project_v(t, half):
                        b, i = t // TILES % BATCH, t % TILES
                        wv = wqkv_sb[:, 2 * INNER:].rearrange("p (c a d) -> p a c d", a=2, d=DH)
                        if t == NT and half == 0:
                            pe.wait_ge(wqkv_moved, 2)
                        take(pe, "v", t, half)
                        dst = slot("v", t, half)
                        for n in range(2):
                            a = i * P + (2 * half + n) * WINDOW
                            for parity in range(2):
                                m = nc.tensor.matmul(dst[64 * parity:64 * parity + 64, n, :],
                                                     xsT[:, b, a:a + 2 * WINDOW], wv[:, parity],
                                                     start=True, stop=True, skip_group_check=True)
                        m.then_inc(filled(("v", t, half)), 1)

                    def project_out(b):
                        if b == 0:
                            pe.wait_ge(wo_ld, 16)
                        wait_free(pe, "oT", (b + 1) * TILES - 1)
                        take(pe, "wo", b)
                        for c in range(PAIRS):
                            m = nc.tensor.matmul(slot("wo", b)[:, 0, :], wo_sb[:, c, :], oT[:, c, :],
                                                 start=(c == 0), stop=(c == PAIRS - 1))
                        m.then_inc(filled(("wo", b)), 1)

                    def moment(name, src, ready, count, b):
                        pe.wait_ge(ready, count)
                        take(pe, name, b)
                        nc.tensor.matmul(slot(name, b)[:, 0, :], mean_w, src[:, :], start=True, stop=True)\
                            .then_inc(filled((name, b)), 1)

                    def hidden(b, c):
                        a, n = HC[c]
                        pe.wait_ge(xg_ready, b + 1)
                        if b == 0 and c == 0:
                            pe.wait_ge(w1_ld, 16)
                        take(pe, "h", b, c)
                        for s in range(2):
                            w = w1_sb[:, s * HIDDEN + a:s * HIDDEN + a + n]
                            m = nc.tensor.matmul(slot("h", b, c)[0:n, s, :], w, xg[:, :], start=True, stop=True)
                        m.then_inc(filled(("h", b, c)), 1)

                    def project_ffn(b):
                        for c in range(len(HC)):
                            wait_free(pe, "h", b, c)
                        if b == 0:
                            pe.wait_ge(w2_ld, 16)
                        take(pe, "y", b)
                        for c, (a, n) in enumerate(HC):
                            m = nc.tensor.matmul(slot("y", b)[:, 0, :], w2_sb[0:n, c, :], hid[0:n, c, :],
                                                 start=(c == 0), stop=(c == len(HC) - 1))
                        m.then_inc(filled(("y", b)), 1)

                    for t in steps:
                        b_wo, b_norm, b_hid, b_y = pieces(t)
                        if t < tiles:
                            project("k", t)
                        if 0 <= t - 1 < tiles:
                            turn("k", t - 1)
                            turn("q", t - 1)
                        if t < tiles:
                            project("q", t)
                        if 0 <= t - 2 < tiles:
                            turn_probs(t - 2)
                        if 0 <= t - 1 < tiles:
                            scores(t - 1)
                        if 0 <= t - 2 < tiles:
                            values(t - 2)
                        if b_wo is not None:
                            project_out(b_wo)
                        if b_norm is not None:
                            moment("mean", xf, xf_ready, 32 * (b_norm + 1), b_norm)
                        if b_hid is not None:
                            hidden(b_hid, 0)
                        if 0 <= t - 1 < tiles:
                            project_v(t - 1, 0)
                            project_v(t - 1, 1)
                        if b_y is not None:
                            project_ffn(b_y)
                        if b_hid is not None:
                            hidden(b_hid, 1)
                            hidden(b_hid, 2)
                        if 0 <= t - 2 < tiles:
                            turn_out(t - 2)
                        if b_norm is not None:
                            moment("var", fsq, fsquared, b_norm + 1, b_norm)

                @block.scalar
                def _(act):
                    if first == 0:
                        nc.scalar.preload_act_table_set(LN_EXP)

                    def copy_slot(key, dst, src=None):
                        wait_full(act, *key)
                        nc.scalar.activation(dst, slot(*key) if src is None else src, ACT.Copy)\
                            .then_inc(read(key), 1)

                    def square(t, r):
                        name, part = ("k", "q")[r], 2 * t + r
                        wait_full(act, name, t)
                        wait(act, summed, part - 1)
                        nc.scalar.activation(sq[:, 1 - r], slot(name, t).rearrange("p n (h d) -> p (n h) d", d=DH),
                                             ACT.Square).then_inc(squared, 1)

                    def inverse_norm(t, r):
                        part = 2 * t + r
                        wait(act, bounded, part + 1)
                        nc.scalar.activation(norms[:, t % 2, 1 - r], norms[:, t % 2, 1 - r], ACT.Ln, scale=65536.0)\
                            .then_inc(logged, 1)
                        wait(act, logged, part + 1)
                        nc.scalar.activation(norms[:, t % 2, 1 - r], norms[:, t % 2, 1 - r], ACT.Exp, scale=-0.5,
                                             bias=ln256[:, 0:1]).then_inc(norm_ready, 1)

                    def copy_q(t):
                        wait_full(act, "s", t - 1)
                        copy_slot(("qT", t), qT[:, :, :].rearrange("p (n c) q -> p n (c q)", n=2))

                    def copy_k(t, parity):
                        wait_full(act, "kT", t)
                        wait_full(act, "s", t - 2)
                        wait(act, carried, t - 1)
                        src = slot("kT", t).rearrange("p n (c q) -> p (n c) q", q=P)
                        rows = slice(64 * parity, 64 * parity + 64)
                        m = nc.scalar.activation(kb[rows, t % 2, :, parity, WINDOW:], src[rows, :, :], ACT.Copy)
                        if parity == 1:
                            m.then_inc(read(("kT", t)), 1)

                    def exps(t):
                        wait_free(act, "s", t)
                        wait_full(act, "pT", t - 2)
                        wait(act, sum_ready, t - 1)
                        nc.scalar.activation(prob[:, t % 2], dif[:, :, :], ACT.Exp, scale=QK_SCALE).then_inc(exped, 1)

                    def copy_probs(t):
                        wait_full(act, "o", t - 1)
                        copy_slot(("pT", t), pT[:, :, :].rearrange("p (n c) q -> p n (c q)", n=2))

                    def copy_v(t, half):
                        wait_full(act, "v", t, half)
                        wait_full(act, "o", t - 1)
                        for parity in range(2):
                            r = slice(64 * parity, 64 * parity + 64)
                            m = nc.scalar.activation(vb[r, 2 * half:2 * half + 2, :, parity, :],
                                                     slot("v", t, half)[r].rearrange("p n (c d) -> p n c d", d=DH),
                                                     ACT.Copy)
                        m.then_inc(read(("v", t, half)), 1)

                    def copy_out(t):
                        i = t % TILES
                        wait_full(act, "oT", t)
                        if i == 0:
                            wait_full(act, "wo", t // TILES - 1)
                        nc.scalar.activation(oT[:, :, i * P:(i + 1) * P],
                                             slot("oT", t).rearrange("p n (c q) -> p (n c) q", q=P), ACT.Copy)\
                            .then_inc(read(("oT", t)), 1)

                    def gelu(b, c):
                        n = HC[c][1]
                        wait_full(act, "h", b, c)
                        if b == 0 and c == 0:
                            act.wait_ge(vec_ld, 16)
                        if b >= 1 and c == 0:
                            for k in range(len(HC)):
                                wait_free(act, "h", b - 1, k)
                        nc.scalar.activation(gel[0:n, c, :], slot("h", b, c)[0:n, 1, :], ACT.Gelu,
                                             bias=vec[0:n, V_B1 + 3 + c:V_B1 + 4 + c]).then_inc(gelu_ready, 1)

                    for t in steps:
                        _, b_norm, b_hid, _ = pieces(t)
                        if t < tiles:
                            square(t, 0)
                        if 0 <= t - 1 < tiles:
                            copy_k(t - 1, 0)
                            copy_q(t - 1)
                        if t < tiles:
                            inverse_norm(t, 0)
                        if 0 <= t - 1 < tiles:
                            copy_k(t - 1, 1)
                        if t < tiles:
                            square(t, 1)
                        if 0 <= t - 2 < tiles:
                            copy_probs(t - 2)
                        if t < tiles:
                            inverse_norm(t, 1)
                        if 0 <= t - 1 < tiles:
                            exps(t - 1)
                        if b_hid is not None:
                            gelu(b_hid, 0)
                        if 0 <= t - 1 < tiles:
                            copy_v(t - 1, 0)
                        if b_norm is not None:
                            wait_free(act, "mean", b_norm)
                            nc.scalar.activation(fsq[:, :], cen[:, :], ACT.Square).then_inc(fsquared, 1)
                        if b_hid is not None:
                            gelu(b_hid, 1)
                        if 0 <= t - 1 < tiles:
                            copy_v(t - 1, 1)
                        if b_hid is not None:
                            gelu(b_hid, 2)
                            nc.scalar.preload_act_table_set(LN_EXP)
                        if 0 <= t - 2 < tiles:
                            copy_out(t - 2)
                        if b_norm is not None:
                            wait_full(act, "var", b_norm)
                            nc.scalar.activation(rstd[:, :], slot("var", b_norm)[:, 0, :], ACT.Ln, bias=eps)\
                                .then_inc(read(("var", b_norm)), 1)
                            wait_free(act, "var", b_norm)
                            nc.scalar.activation(rstd[:, :], rstd[:, :], ACT.Exp, scale=-0.5).then_inc(rstd_ready, 1)

                @block.vector
                def _(dve):
                    def sum_squares(t, r):
                        part, half = 2 * t + r, norms[:, t % 2, 1 - r]
                        wait(dve, squared, part + 1)
                        wait_free(dve, ("k", "q")[r], t - 2)
                        nc.vector.tensor_reduce(half, sq[:, 1 - r], AX.X, ALU.add).then_inc(summed, 1)
                        wait(dve, summed, part + 1)
                        nc.vector.tensor_scalar(half, half, 1e-24, None, ALU.max).then_inc(bounded, 1)

                    def normalise(t, r):
                        name, part = ("k", "q")[r], 2 * t + r
                        wait(dve, norm_ready, part + 1)
                        wait(dve, cosed, part - 1)
                        wait(dve, sined, part - 1)
                        nc.vector.tensor_tensor(qn[:, 1 - r],
                                                slot(name, t).rearrange("p n (h d) -> p (n h) d", d=DH),
                                                norms[:, t % 2, 1 - r, :, None].broadcast_to([P, HEADS, DH]),
                                                ALU.mult).then_inc(read((name, t)), 1)

                    def sine_part(t, r):
                        i, H2, part = t % TILES, DH // 2, 2 * t + r
                        wait_free(dve, ("k", "q")[r], t)
                        wait(dve, rotated, part - 1)
                        if t % NT == 0 and r == 0:
                            dve.wait_ge(sin_ready, 2)
                        for a in (0, H2):
                            m = nc.vector.tensor_tensor(rot_s[:, 1 - r, :, a:a + H2], qn[:, 1 - r, :, H2 - a:DH - a],
                                                        tab_s[:, 1 - r, i, None, a:a + H2]
                                                        .broadcast_to([P, HEADS, H2]), ALU.mult)
                        m.then_inc(sined, 1)

                    def shift_scores(t):
                        s = slot("s", t).rearrange("p n (h k) -> p (n h) k", k=2 * WINDOW)
                        wait_full(dve, "s", t)
                        nc.vector.tensor_reduce(mx[:, t % 2, :], s, AX.X, ALU.max).then_inc(maxed, 1)
                        wait(dve, maxed, t + 1)
                        wait(dve, exped, t)
                        nc.vector.tensor_tensor(dif[:, :, :], s,
                                                mx[:, t % 2, :, None].broadcast_to([P, HEADS, 2 * WINDOW]),
                                                ALU.subtract).then_inc(read(("s", t)), 1)

                    def sums(t):
                        wait(dve, exped, t + 1)
                        nc.vector.tensor_reduce(total[:, t % 2, :], prob[:, t % 2], AX.X, ALU.add)\
                            .then_inc(sum_ready, 1)
                        wait(dve, sum_ready, t + 1)
                        wait_free(dve, "o", t - 2)
                        nc.vector.reciprocal(inv[:, t % 2, :], total[:, t % 2, :]).then_inc(inv_ready, 1)

                    def scale_out(t):
                        wait_full(dve, "o", t)
                        wait(dve, inv_ready, t + 1)
                        wait_full(dve, "oT", t - 1)
                        nc.vector.tensor_tensor(o_tok[:, :, :], slot("o", t).rearrange("p n (h d) -> p (n h) d", d=DH),
                                                inv[:, t % 2, :, None].broadcast_to([P, HEADS, DH]), ALU.mult)\
                            .then_inc(read(("o", t)), 1)

                    def gate(b, c):
                        n = HC[c][1]
                        dve.wait_ge(gelu_ready, len(HC) * b + c + 1)
                        wait_full(dve, "h", b, c)
                        if b >= 1 and c == 0:
                            wait_full(dve, "y", b - 1)
                        nc.vector.scalar_tensor_tensor(out=hid[0:n, c, :], in0=slot("h", b, c)[0:n, 0, :],
                                                       scalar=vec[0:n, V_B1 + c:V_B1 + c + 1],
                                                       in1=gel[0:n, c, :], op0=ALU.add, op1=ALU.mult)\
                            .then_inc(read(("h", b, c)), 1)

                    def sine_table():
                        if more:
                            dve.wait_ge(next_scales, 16)
                            wait(dve, sined, 2 * NT)
                        rope_s = const("ropeS").rearrange("p (a i d) -> p a i d", a=2, i=TILES)
                        for a in (0, DH // 2):
                            o = DH // 2 - a
                            nc.vector.tensor_tensor(tab_s[:, :, :, a:a + DH // 2], rope_s[:, :, :, a:a + DH // 2],
                                                    scales[:, :, None, o:o + DH // 2]
                                                    .broadcast_to([P, 2, TILES, DH // 2]), ALU.mult)\
                                .then_inc(sin_ready, 1)

                    for t in steps:
                        b_wo, b_norm, b_hid, b_y = pieces(t)
                        if 0 <= t - 2 < tiles:
                            sums(t - 2)
                        if t < tiles:
                            sum_squares(t, 0)
                        if b_hid is not None:
                            dve.wait_ge(rstd_ready, b_hid + 1)
                            if b_hid >= 1:
                                wait_full(dve, "h", b_hid - 1, len(HC) - 1)
                            nc.vector.tensor_tensor(xg[:, :], cen[:, :], rstd[:, :], ALU.mult).then_inc(xn_ready, 1)
                            dve.wait_ge(xn_ready, b_hid + 1)
                            if b_hid == 0:
                                dve.wait_ge(vec_ld, 16)
                            nc.vector.tensor_scalar(xg[:, :], xg[:, :], vec[:, V_G:V_G + 1], vec[:, V_B:V_B + 1],
                                                    ALU.mult, ALU.add).then_inc(xg_ready, 1)
                        if t % NT == 0 and t < tiles:
                            sine_table()
                        if t < tiles:
                            normalise(t, 0)
                            sine_part(t, 0)
                            sum_squares(t, 1)
                            normalise(t, 1)
                        if 0 <= t - 1 < tiles:
                            shift_scores(t - 1)
                        if t < tiles:
                            sine_part(t, 1)
                        if 0 <= t - 2 < tiles:
                            scale_out(t - 2)
                        if b_wo is not None:
                            wait_full(dve, "wo", b_wo)
                            nc.vector.tensor_tensor(xT[:, b_wo, PAD:], xT[:, b_wo, PAD:], slot("wo", b_wo)[:, 0, :],
                                                    ALU.add).then_inc(read(("wo", b_wo)), 1)
                        if b_norm is not None:
                            wait_full(dve, "mean", b_norm)
                            if b_norm >= 1:
                                wait_full(dve, "var", b_norm - 1)
                                dve.wait_ge(xn_ready, b_norm)
                            nc.vector.tensor_tensor(cen[:, :], xf[:, :], slot("mean", b_norm)[:, 0, :], ALU.subtract)\
                                .then_inc(read(("mean", b_norm)), 1)
                        if b_hid is not None:
                            for c in range(len(HC)):
                                gate(b_hid, c)
                        if b_y is not None:
                            wait_full(dve, "y", b_y)
                            nc.vector.scalar_tensor_tensor(out=xT[:, b_y, PAD:], in0=slot("y", b_y)[:, 0, :],
                                                           scalar=vec[:, V_B2:V_B2 + 1], in1=xT[:, b_y, PAD:],
                                                           op0=ALU.add, op1=ALU.add).then_inc(read(("y", b_y)), 1)
                        if more and t == NT - 1:
                            dve.wait_ge(next_ld, 16)
                            wait_full(dve, "k", t)
                            wait_full(dve, "q", t)
                            nc.vector.tensor_copy(wqkv_sb[:, 0:2 * INNER], wqkv_next[:, 0:2 * INNER])\
                                .then_inc(wqkv_moved, 1)
                        if more and t == NT:
                            for half in range(2):
                                wait_full(dve, "v", t - 1, half)
                            nc.vector.tensor_copy(wqkv_sb[:, 2 * INNER:], wqkv_next[:, 2 * INNER:])\
                                .then_inc(wqkv_moved, 1)
            nc.all_engine_barrier(sems_to_clear=body_sems)

        segment(0, range(HEAD), STEPS)
        with nc.Fori(0, LAYERS - 1) as layer:
            segment(layer, range(HEAD, STEPS), STEPS)
        segment(LAYERS - 1, range(HEAD, STEPS), NT)


def shape_constants():
    import numpy as np
    c = np.zeros((P, N_CONST), np.float32)

    def put(name, a):
        at, n = CONST[name]
        c[:, at:at + n] = np.asarray(a, np.float32).reshape(P, n)

    f = np.float32
    put("ident", np.eye(P))
    put("mean", np.full((P, P), 1.0 / DIM))
    sums = np.zeros((P, P))
    for j in range(4):
        sums[32 * j + DK, 32 * j:32 * j + 32] = 1.0
    put("sums", sums)
    inv = f(1.0) / np.power(f(10000.0), (np.arange(0, DK, 2, dtype=f) / f(DK)), dtype=f)
    fr = np.arange(SEQ, dtype=f)[:, None] * inv[None, :]
    emb = np.concatenate([fr, fr], -1)
    sign = np.where(np.arange(DK) < DK // 2, -1.0, 1.0)
    put("cosT", np.tile(np.cos(emb).T, (HEADS, 1)))
    put("sinT", np.tile(np.sin(emb).T * sign[:, None], (HEADS, 1)))
    p = np.arange(P)
    put("kmask", (p[:, None] // DK) == np.arange(HEADS)[None, :])
    put("vmask", (4 * np.arange(GROUPS)[None, :, None] + (p // CTX)[:, None, None]) == np.arange(HEADS)[None, None, :])
    half = np.arange(0, DH, 2, dtype=f)
    inv = f(1.0) / np.power(f(10000.0), half / f(DH), dtype=f)
    t = np.arange(SEQ, dtype=f)
    fr = t[:, None] * inv[None, :]
    fr = np.concatenate([fr, fr], -1)
    base = (half + f(0.4 * DH)) / f(1.4 * DH)
    power = (t - SEQ // 2) / f(WINDOW // 2)
    sc = np.power(base[None, :], power[:, None], dtype=f)
    sc = np.concatenate([sc, sc], -1)
    sgn = np.where(np.arange(DH) < DH // 2, -1.0, 1.0).astype(f)
    for name, tab in (("ropeC", np.cos(fr)), ("ropeS", np.sin(fr) * sgn)):
        a = np.stack([tab * sc, tab * (f(1.0) / sc)])
        put(name, a.reshape(2, TILES, P, DH).transpose(2, 0, 1, 3))
    m = np.zeros((P, 8, 2 * WINDOW))
    key = np.arange(2 * WINDOW)
    for r in range(WINDOW):
        bad = (key < r) | (key > r + WINDOW)
        m[r] = np.where(bad, -1e30, 0.0)
        m[WINDOW + r] = np.where(bad | (key < WINDOW), -1e30, 0.0)
    put("wmask", m)
    s = np.zeros((P, 2, P))
    for q in range(P):
        s[q % WINDOW, 0, q] = 1.0
        s[q % WINDOW + (WINDOW if q < WINDOW else 0), 1, q] = 1.0
    put("wsel", s)
    return c


def kernel(x, ctx_512, L0_attn_Wq, L0_attn_Wk, L0_attn_Wv, L0_attn_Wo, L0_xattn_Wq, L0_xattn_Wkv, L0_xattn_Wo,
           L0_ffn_Wqkv, L0_ffn_q_scale, L0_ffn_k_scale, L0_ffn_Wo, L0_ffn_ln_g, L0_ffn_ln_b, L0_ffn_W1, L0_ffn_b1,
           L0_ffn_W2, L0_ffn_b2):
    import numpy as np
    import concourse.bacc as bacc
    from concourse.bass_utils import run_bass_kernel_spmd

    T = lambda a: np.ascontiguousarray(np.asarray(a).T)
    rot = np.arange(DIM).reshape(HEADS, DK)
    rot = np.concatenate([rot[:, 1::2], rot[:, ::2]], -1).reshape(-1)
    wq, wk, wv, wo_a = (T(a) for a in (L0_attn_Wq, L0_attn_Wk, L0_attn_Wv, L0_attn_Wo))
    w_attn = np.zeros((P, 9 * P), wq.dtype)
    for name, a in (("q", wq), ("k", wk), ("qr", wq[:, rot]), ("kr", wk[:, rot]), ("v", wv)):
        w_attn[:, W_ATTN[name]:W_ATTN[name] + P] = a
    for h in range(HEADS):
        at, r = W_ATTN["o0"] + (h // 4) * P, 32 * (h % 4)
        w_attn[r:r + DK, at:at + P] = wo_a[h * DK:(h + 1) * DK]
    vecs = np.zeros((LAYERS, P, N_VEC), np.asarray(x).dtype)
    b1 = np.asarray(L0_ffn_b1)
    for s in range(2):
        for c, (at, n) in enumerate(HC):
            vecs[:, :n, V_B1 + 3 * s + c] = b1[:, s * HIDDEN + at:s * HIDDEN + at + n]
    for col, a in ((V_G, L0_ffn_ln_g), (V_B, L0_ffn_ln_b), (V_B2, L0_ffn_b2)):
        vecs[:, :, col] = np.asarray(a)
    w2 = np.zeros((LAYERS, len(HC) * P, P), vecs.dtype)
    w2[:, :HIDDEN] = np.asarray(L0_ffn_W2)
    arrays = {
        "x": np.asarray(x).reshape(BATCH * SEQ, DIM),
        "ctxT": T(np.asarray(ctx_512).reshape(BATCH * CTX, LATENT)),
        "w_attn": w_attn,
        "w_xq": T(L0_xattn_Wq), "w_xkv": T(L0_xattn_Wkv), "w_xo": T(L0_xattn_Wo),
        "wqkv": np.asarray(L0_ffn_Wqkv),
        "qk_scales": np.stack([np.asarray(L0_ffn_q_scale), np.asarray(L0_ffn_k_scale)], 1),
        "wo": np.asarray(L0_ffn_Wo), "w1": np.asarray(L0_ffn_W1), "w2": w2, "vecs": vecs,
        "consts": shape_constants(),
    }
    nc = bacc.Bacc("TRN2", target_bir_lowering=False, num_devices=1)
    args = [nc.dram_tensor(n, a.shape, mybir.dt.from_np(a.dtype), kind="ExternalInput").ap() for n, a in arrays.items()]
    scratch = nc.dram_tensor("scratch", (BATCH, P, 3, 2, SEQ), BF16, kind="Internal").ap()
    max_scratch = nc.dram_tensor("max_scratch", (BATCH, P, P), BF16, kind="Internal").ap()
    out = nc.dram_tensor("out", (BATCH, SEQ, DIM), F32, kind="ExternalOutput").ap()
    decoder(nc, *args, scratch, max_scratch, out)
    r = run_bass_kernel_spmd(nc, [arrays], core_ids=[0])
    return r.results[0]["out"]
```
